# Optimizing a Trainium2 kernel written in Bass

```python
import numpy as np
import jax
import jax.numpy as jnp

def _softmax(x, axis=-1):
    return jax.nn.softmax(x, axis=axis)

def _gelu(x):
    return jax.nn.gelu(x, approximate=True)

def _silu(x):
    return jax.nn.silu(x)

def _sigmoid(x):
    return jax.nn.sigmoid(x)

def _layernorm(x, axis=-1, eps=1e-05):
    m = jnp.mean(x, axis=axis, keepdims=True)
    v = jnp.var(x, axis=axis, keepdims=True)
    return (x - m) / jnp.sqrt(v + eps)

def _scatter_add(tgt, idx, src, axis=0):
    return tgt.at[idx].add(src)

def _segment_sum(src, seg, n):
    return jax.ops.segment_sum(src, seg, n)
kernel_name = 'mk_prb_d1_jaxref_r2_1b945c'

def setup_inputs(seed: int=0):
    np.random.seed(seed)
    _w = jnp.asarray

    def _L0_attn_setup():
        import jax, jax.numpy as jnp
        import numpy as np
        D_STATE = 16
        DT_RANK = 6
        EPS = 1e-05

        def layer_norm(x, w, b):
            mu = jnp.mean(x, axis=-1, keepdims=True)
            var = jnp.mean((x - mu) ** 2, axis=-1, keepdims=True)
            return (x - mu) * jax.lax.rsqrt(var + EPS) * w + b

        def selective_scan(u, delta, A, Bp, Cp, Dp):
            delta_A = jnp.exp(jnp.einsum('bld,dn->bldn', delta, A))
            delta_B_u = jnp.einsum('bld,bln,bld->bldn', delta, Bp, u)
            Bsz, L, D = u.shape

            def step(x, inp):
                dA_t, dBu_t, C_t = inp
                x = dA_t * x + dBu_t
                y = jnp.einsum('bdn,bn->bd', x, C_t)
                return (x, y)
            x0 = jnp.zeros((Bsz, D, D_STATE), dtype=u.dtype)
            xs = (jnp.swapaxes(delta_A, 0, 1), jnp.swapaxes(delta_B_u, 0, 1), jnp.swapaxes(Cp, 0, 1))
            _, ys = jax.lax.scan(step, x0, xs)
            y = jnp.swapaxes(ys, 0, 1)
            return y + u * Dp

        def ssm(x, x_proj_W, dt_proj_W, dt_proj_b, A_log, D_param):
            A = -jnp.exp(A_log.astype(jnp.float32))
            dbc = x @ x_proj_W.T
            delta_r = dbc[..., :DT_RANK]
            Bp = dbc[..., DT_RANK:DT_RANK + D_STATE]
            Cp = dbc[..., DT_RANK + D_STATE:]
            delta = jax.nn.softplus(delta_r @ dt_proj_W.T + dt_proj_b) * 0.001
            return selective_scan(x, delta, A, Bp, Cp, D_param.astype(jnp.float32))
        key = jax.random.key(seed)
        ks = jax.random.split(key, 10)
        B, L, C, Din = (16, 1024, 1024, 96)
        A = jnp.tile(jnp.arange(1, D_STATE + 1, dtype=jnp.float32)[None, :], (Din, 1))
        return {'feat_patch': jax.random.normal(ks[0], (B, L, C), dtype=jnp.float32), 'ln_w': jnp.ones((C,), jnp.float32), 'ln_b': jnp.zeros((C,), jnp.float32), 'in_proj_W': jax.random.normal(ks[1], (Din, C), jnp.float32) * (1.0 / np.sqrt(C)), 'conv_w': jax.random.normal(ks[2], (Din, 1, 3), jnp.float32) * 0.3, 'conv_b': jnp.zeros((Din,), jnp.float32), 'x_proj_W': jax.random.normal(ks[3], (DT_RANK + 2 * D_STATE, Din), jnp.float32) * (1.0 / np.sqrt(Din)), 'dt_proj_W': jax.random.normal(ks[4], (Din, DT_RANK), jnp.float32) * (1.0 / np.sqrt(DT_RANK)), 'dt_proj_b': jnp.zeros((Din,), jnp.float32), 'A_log': jnp.log(A), 'D_param': jnp.ones((Din,), jnp.float32), 'out_proj_W': jax.random.normal(ks[5], (C, Din), jnp.float32) * (1.0 / np.sqrt(Din))}
    _L0_attn_in = _L0_attn_setup()

    def _L0_ffn_setup():
        import jax, jax.numpy as jnp
        import numpy as np
        B, S, H = (2, 1024, 1024)
        E, G, TKG, K = (32, 8, 4, 8)
        I, SI = (512, 1024)
        ROUTED_SCALE = 2.5

        def _moe_forward(hidden_states, router_w, router_bias, w_gate, w_up, w_down, sw_gate, sw_up, sw_down):
            x = hidden_states.reshape(-1, H)
            T = x.shape[0]
            logits = x.astype(jnp.float32) @ router_w.astype(jnp.float32)
            scores = jax.nn.sigmoid(logits)
            scores_grouped = (scores + router_bias).reshape(T, G, E // G)
            top2, _ = jax.lax.top_k(scores_grouped, 2)
            group_scores = top2.sum(-1)
            _, top_groups = jax.lax.top_k(group_scores, TKG)
            mask = jnp.ones((T, G), bool).at[jnp.arange(T)[:, None], top_groups].set(False)
            masked = jnp.where(mask[:, :, None], 0.0, scores_grouped).reshape(T, E)
            _, top_k_index = jax.lax.top_k(masked, K)
            tkw = jnp.take_along_axis(scores, top_k_index, axis=-1)
            tkw = tkw / tkw.sum(-1, keepdims=True)
            tkw = (tkw * ROUTED_SCALE).astype(hidden_states.dtype)
            flat_idx = top_k_index.reshape(-1)
            sort_idx = jnp.argsort(flat_idx)
            xs = jnp.repeat(x, K, axis=0)[sort_idx]
            group_sizes = jnp.bincount(flat_idx, length=E).astype(jnp.int32)
            gate = jax.lax.ragged_dot(xs, w_gate, group_sizes)
            up = jax.lax.ragged_dot(xs, w_up, group_sizes)
            down = jax.lax.ragged_dot(jax.nn.silu(gate) * up, w_down, group_sizes)
            unsort = jnp.argsort(sort_idx)
            routed = (down[unsort].reshape(T, K, H) * tkw[..., None]).sum(axis=1)
            shared = jax.nn.silu(x @ sw_gate) * (x @ sw_up) @ sw_down
            return (routed + shared).reshape(hidden_states.shape)
        key = jax.random.key(seed)
        ks = jax.random.split(key, 9)

        def w(k, shape, fan_in):
            return jax.random.normal(k, shape, jnp.float32) / np.float32(np.sqrt(fan_in))
        return dict(hidden_states=jax.random.normal(ks[0], (B, S, H), jnp.float32), router_w=w(ks[1], (H, E), H), router_bias=jnp.zeros((E,), jnp.float32), w_gate=w(ks[2], (E, H, I), H), w_up=w(ks[3], (E, H, I), H), w_down=w(ks[4], (E, I, H), I), sw_gate=w(ks[5], (H, SI), H), sw_up=w(ks[6], (H, SI), H), sw_down=w(ks[7], (SI, H), SI))
    _L0_ffn_in = _L0_ffn_setup()
    _d = {'L0_attn_feat_patch': _L0_attn_in['feat_patch'], 'L0_attn_ln_w': _L0_attn_in['ln_w'], 'L0_attn_ln_b': _L0_attn_in['ln_b'], 'L0_attn_in_proj_W': _L0_attn_in['in_proj_W'], 'L0_attn_conv_w': _L0_attn_in['conv_w'], 'L0_attn_conv_b': _L0_attn_in['conv_b'], 'L0_attn_x_proj_W': _L0_attn_in['x_proj_W'], 'L0_attn_dt_proj_W': _L0_attn_in['dt_proj_W'], 'L0_attn_dt_proj_b': _L0_attn_in['dt_proj_b'], 'L0_attn_A_log': _L0_attn_in['A_log'], 'L0_attn_D_param': _L0_attn_in['D_param'], 'L0_attn_out_proj_W': _L0_attn_in['out_proj_W'], 'L0_ffn_router_w': _L0_ffn_in['router_w'], 'L0_ffn_router_bias': _L0_ffn_in['router_bias'], 'L0_ffn_w_gate': _L0_ffn_in['w_gate'], 'L0_ffn_w_up': _L0_ffn_in['w_up'], 'L0_ffn_w_down': _L0_ffn_in['w_down'], 'L0_ffn_sw_gate': _L0_ffn_in['sw_gate'], 'L0_ffn_sw_up': _L0_ffn_in['sw_up'], 'L0_ffn_sw_down': _L0_ffn_in['sw_down']}
    _x0 = _d['L0_attn_feat_patch']
    _d['L0_attn_feat_patch'] = jax.random.normal(jax.random.fold_in(jax.random.key(seed), 1), (2, 4096, 1024), dtype=_x0.dtype)
    del _x0
    return _d

def reference(L0_attn_feat_patch, L0_attn_ln_w, L0_attn_ln_b, L0_attn_in_proj_W, L0_attn_conv_w, L0_attn_conv_b, L0_attn_x_proj_W, L0_attn_dt_proj_W, L0_attn_dt_proj_b, L0_attn_A_log, L0_attn_D_param, L0_attn_out_proj_W, L0_ffn_router_w, L0_ffn_router_bias, L0_ffn_w_gate, L0_ffn_w_up, L0_ffn_w_down, L0_ffn_sw_gate, L0_ffn_sw_up, L0_ffn_sw_down):

    def _L0_attn_ref(feat_patch, ln_w, ln_b, in_proj_W, conv_w, conv_b, x_proj_W, dt_proj_W, dt_proj_b, A_log, D_param, out_proj_W):
        import jax, jax.numpy as jnp
        import numpy as np
        D_STATE = 16
        DT_RANK = 6
        EPS = 1e-05

        def layer_norm(x, w, b):
            mu = jnp.mean(x, axis=-1, keepdims=True)
            var = jnp.mean((x - mu) ** 2, axis=-1, keepdims=True)
            return (x - mu) * jax.lax.rsqrt(var + EPS) * w + b

        def selective_scan(u, delta, A, Bp, Cp, Dp):
            delta_A = jnp.exp(jnp.einsum('bld,dn->bldn', delta, A))
            delta_B_u = jnp.einsum('bld,bln,bld->bldn', delta, Bp, u)
            Bsz, L, D = u.shape

            def step(x, inp):
                dA_t, dBu_t, C_t = inp
                x = dA_t * x + dBu_t
                y = jnp.einsum('bdn,bn->bd', x, C_t)
                return (x, y)
            x0 = jnp.zeros((Bsz, D, D_STATE), dtype=u.dtype)
            xs = (jnp.swapaxes(delta_A, 0, 1), jnp.swapaxes(delta_B_u, 0, 1), jnp.swapaxes(Cp, 0, 1))
            _, ys = jax.lax.scan(step, x0, xs)
            y = jnp.swapaxes(ys, 0, 1)
            return y + u * Dp

        def ssm(x, x_proj_W, dt_proj_W, dt_proj_b, A_log, D_param):
            A = -jnp.exp(A_log.astype(jnp.float32))
            dbc = x @ x_proj_W.T
            delta_r = dbc[..., :DT_RANK]
            Bp = dbc[..., DT_RANK:DT_RANK + D_STATE]
            Cp = dbc[..., DT_RANK + D_STATE:]
            delta = jax.nn.softplus(delta_r @ dt_proj_W.T + dt_proj_b) * 0.001
            return selective_scan(x, delta, A, Bp, Cp, D_param.astype(jnp.float32))
        residual = feat_patch
        x = layer_norm(feat_patch, ln_w, ln_b)
        x = x @ in_proj_W.T
        x_ncl = jnp.swapaxes(x, 1, 2)
        x_ncl = jax.lax.conv_general_dilated(x_ncl, conv_w, window_strides=(1,), padding=((1, 1),), dimension_numbers=('NCH', 'OIH', 'NCH'), feature_group_count=96)
        x_ncl = x_ncl + conv_b[None, :, None]
        x = jnp.swapaxes(x_ncl, 1, 2)
        x = jax.nn.silu(x)
        y = ssm(x, x_proj_W, dt_proj_W, dt_proj_b, A_log, D_param)
        out = y @ out_proj_W.T
        return out + residual

    def _L0_ffn_ref(hidden_states, router_w, router_bias, w_gate, w_up, w_down, sw_gate, sw_up, sw_down):
        import jax, jax.numpy as jnp
        import numpy as np
        B, S, H = (2, 1024, 1024)
        E, G, TKG, K = (32, 8, 4, 8)
        I, SI = (512, 1024)
        ROUTED_SCALE = 2.5

        def _moe_forward(hidden_states, router_w, router_bias, w_gate, w_up, w_down, sw_gate, sw_up, sw_down):
            x = hidden_states.reshape(-1, H)
            T = x.shape[0]
            logits = x.astype(jnp.float32) @ router_w.astype(jnp.float32)
            scores = jax.nn.sigmoid(logits)
            scores_grouped = (scores + router_bias).reshape(T, G, E // G)
            top2, _ = jax.lax.top_k(scores_grouped, 2)
            group_scores = top2.sum(-1)
            _, top_groups = jax.lax.top_k(group_scores, TKG)
            mask = jnp.ones((T, G), bool).at[jnp.arange(T)[:, None], top_groups].set(False)
            masked = jnp.where(mask[:, :, None], 0.0, scores_grouped).reshape(T, E)
            _, top_k_index = jax.lax.top_k(masked, K)
            tkw = jnp.take_along_axis(scores, top_k_index, axis=-1)
            tkw = tkw / tkw.sum(-1, keepdims=True)
            tkw = (tkw * ROUTED_SCALE).astype(hidden_states.dtype)
            flat_idx = top_k_index.reshape(-1)
            sort_idx = jnp.argsort(flat_idx)
            xs = jnp.repeat(x, K, axis=0)[sort_idx]
            group_sizes = jnp.bincount(flat_idx, length=E).astype(jnp.int32)
            gate = jax.lax.ragged_dot(xs, w_gate, group_sizes)
            up = jax.lax.ragged_dot(xs, w_up, group_sizes)
            down = jax.lax.ragged_dot(jax.nn.silu(gate) * up, w_down, group_sizes)
            unsort = jnp.argsort(sort_idx)
            routed = (down[unsort].reshape(T, K, H) * tkw[..., None]).sum(axis=1)
            shared = jax.nn.silu(x @ sw_gate) * (x @ sw_up) @ sw_down
            return (routed + shared).reshape(hidden_states.shape)
        return _moe_forward(hidden_states, router_w, router_bias, w_gate, w_up, w_down, sw_gate, sw_up, sw_down)
    x = L0_attn_feat_patch
    xn = _layernorm(x, axis=-1)
    x = x + _L0_attn_ref(xn, L0_attn_ln_w, L0_attn_ln_b, L0_attn_in_proj_W, L0_attn_conv_w, L0_attn_conv_b, L0_attn_x_proj_W, L0_attn_dt_proj_W, L0_attn_dt_proj_b, L0_attn_A_log, L0_attn_D_param, L0_attn_out_proj_W) + _L0_ffn_ref(xn, L0_ffn_router_w, L0_ffn_router_bias, L0_ffn_w_gate, L0_ffn_w_up, L0_ffn_w_down, L0_ffn_sw_gate, L0_ffn_sw_up, L0_ffn_sw_down)
    return x

_drawn_inputs = setup_inputs


def setup_inputs(seed=0):
    import zlib

    import numpy as np

    out = dict(_drawn_inputs(seed))
    spreads = {'L0_attn_ln_w': (1.0, 0.2),
     'L0_attn_ln_b': (0.0, 0.524),
     'L0_attn_conv_b': (0.0, 0.1),
     'L0_attn_dt_proj_b': (0.0, 2.0),
     'L0_attn_D_param': (1.0, 0.6),
     'L0_ffn_router_bias': (0.0, 0.342)}
    factors = {'L0_attn_x_proj_W': 6.057, 'L0_attn_dt_proj_W': 8.0, 'L0_attn_A_log': 8.0}
    for name, (base, spread) in spreads.items():
        noise = np.random.default_rng([zlib.crc32(name.encode()), seed]).standard_normal(out[name].shape)
        drawn = base * np.exp(spread * noise) if base else spread * noise
        out[name] = jnp.asarray(drawn.astype(out[name].dtype))
    for name, factor in factors.items():
        out[name] = (out[name] * factor).astype(out[name].dtype)
    return out
```

```python
import concourse.bass as bass
from concourse import mybir
from contextlib import ExitStack

F32 = mybir.dt.float32
F32R = mybir.dt.float32r
BF16 = mybir.dt.bfloat16
I32 = mybir.dt.int32
U32 = mybir.dt.uint32
ALU = mybir.AluOpType
ACT = mybir.ActivationFunctionType
AX = mybir.AxisListType

P = 128
H = 1024
KH = H // P
E, G, TKG, K = 32, 8, 4, 8
EG = E // G
I = 512
KI = I // P
SH = 2
D, N, R = 96, 16, 6
PG = P // N
NG = D // PG
C = 512
J = C // P
EPS = 1e-5
ROUTED_SCALE = 2.5
NCH = 6
NST = 3
WC = 2048


def wait_apart(eng, passed, sem, value):
    eng.wait_ge(sem, value)
    eng.sem_inc(passed, 1)


class Steps:

    def __init__(self, eng, sem, base=0, passed=None):
        self.eng, self.sem, self.base, self.passed, self.n = eng, sem, base, passed, 0

    def __call__(self, ins, apart=False):
        self.n += 1
        ins.then_inc(self.sem, 1)
        if apart:
            wait_apart(self.eng, self.passed, self.sem, self.base + self.n)
        else:
            self.eng.wait_ge(self.sem, self.base + self.n)


def bc(ap, axis, shape):
    return ap.unsqueeze(axis).to_broadcast(shape)


def route_stage(nc, t_all, batches, io, slots_all):
    (x, xn_d, base_d, out, table, rw, ipw, lnw, lnb, rbias, zT, cnt_base) = io
    T, B = t_all, batches
    TPB = T // B // P
    NT = T // P
    LP = T // B + 2
    FILL = 512
    SLOTS = slots_all

    with ExitStack() as ctx:
        def sb(name, shape, dt=F32):
            return ctx.enter_context(nc.sbuf_tensor(name, shape, dt))

        def pb(name, shape, dt=F32):
            return ctx.enter_context(nc.psum_tensor(name, shape, dt))

        def sem(name):
            return ctx.enter_context(nc.semaphore(name))

        wcat = sb("wcat", [P, KH, E + D])
        wraw = sb("wraw", [P, KH, D])
        wlnb = sb("wlnb", [P, KH, D])
        lnw_sb = sb("lnw_sb", [P, KH])
        lnb_sb = sb("lnb_sb", [P, KH])
        bias_b = sb("bias_b", [P, E])
        neg_s = sb("neg_s", [P, D])
        c_b = sb("c_b", [P, D])
        ident = sb("ident", [P, P])
        ones_f = sb("ones_f", [P, P])
        ones_b = sb("ones_b", [P, P], BF16)
        tri = sb("tri", [P, P], BF16)
        iota_i = sb("iota_i", [P, E], I32)
        iota_e = sb("iota_e", [P, E])
        cnt_i = sb("cnt_i", [P, E], I32)
        tid_i = sb("tid_i", [P, 1], I32)
        tid = sb("tid", [P, 1])
        fill = sb("fill", [P, FILL, 2], I32)
        shared_fill = sb("shared_fill", [P, T // P, 2], I32)
        zero_row = sb("zero_row", [P, H])
        minus_half = sb("minus_half", [P, 1])

        xt = [sb(f"xt{i}", [P, H]) for i in range(2)]
        xn = [sb(f"xn{i}", [P, H]) for i in range(2)]
        bs = [sb(f"bs{i}", [P, H]) for i in range(2)]
        xnT = [sb(f"xnT{i}", [P, KH, P]) for i in range(2)]
        st = sb("st", [P, 2, 6])
        mv = [sb(f"mv{i}", [P, 2]) for i in range(2)]
        rstd = [sb(f"rstd{i}", [P, 1]) for i in range(2)]
        st2 = sb("st2", [P, 2, 6])
        mv2 = [sb(f"mv2_{i}", [P, 2]) for i in range(2)]
        rs2 = [sb(f"rs2_{i}", [P, 1]) for i in range(2)]
        score = [sb(f"score{i}", [P, E]) for i in range(2)]
        zpre = sb("zpre", [P, D])
        z = [sb(f"z{i}", [P, D]) for i in range(2)]
        biased = sb("biased", [P, E])
        mx = sb("mx", [P, G, 2])
        mn = sb("mn", [P, G, 2])
        top1 = sb("top1", [P, G])
        m2 = sb("m2", [P, G])
        m3 = sb("m3", [P, G])
        gs = sb("gs", [P, G])
        g8 = sb("g8", [P, 8])
        gi = sb("gi", [P, 8], U32)
        gif = sb("gif", [P, 8])
        gcmp = sb("gcmp", [P, G, TKG])
        gmask = sb("gmask", [P, G])
        masked = sb("masked", [P, E])
        v8 = sb("v8", [P, 8])
        i8 = sb("i8", [P, 8], U32)
        i8f = sb("i8f", [P, 8])
        oh = sb("oh", [P, K, E])
        prod = sb("prod", [P, K, E])
        sel = [sb(f"sel{i}", [P, E], BF16) for i in range(2)]
        w8 = sb("w8", [P, K])
        wsum = sb("wsum", [P, 1])
        rinv = sb("rinv", [P, 1])
        slotrow = sb("slotrow", [P, E])
        slotf = sb("slotf", [P, K])
        slot8 = [sb(f"slot8_{i}", [P, K], U32) for i in range(2)]
        payload = [sb(f"payload{i}", [P, K, 2], I32) for i in range(2)]

        tp = [pb(f"tp{i}", [P, 4, P]) for i in range(2)]
        lg = [pb(f"lg{i}", [P, 512]) for i in range(2)]
        rank = pb("rank", [P, 512])
        zp = pb("zp", [P, 512])

        const_loaded = sem("const_loaded")
        dve_passed = sem("dve_passed")
        pool_passed = sem("pool_passed")
        iotas = sem("iotas")
        fills = sem("fills")
        wprep = sem("wprep")
        sums_done = sem("sums_done")
        route_ready = sem("route_ready")
        x_loaded = [sem(f"x_loaded{i}") for i in range(2)]
        xn_ready = sem("xn_ready")
        x_free = sem("x_free")
        var_ready = sem("var_ready")
        rstd_ready = sem("rstd_ready")
        var2_ready = sem("var2_ready")
        rstd2_ready = sem("rstd2_ready")
        base_ready = sem("base_ready")
        xn_stored = [sem(f"xn_stored{i}") for i in range(2)]
        bs_stored = [sem(f"bs_stored{i}") for i in range(2)]
        tp_ready = sem("tp_ready")
        tp_free = sem("tp_free")
        lg_ready = sem("lg_ready")
        score_ready = sem("score_ready")
        lg_free = sem("lg_free")
        z_ready = sem("z_ready")
        zp_ready = sem("zp_ready")
        zp_free = sem("zp_free")
        sel_ready = sem("sel_ready")
        rank_ready = sem("rank_ready")
        rank_free = sem("rank_free")
        payload_ready = sem("payload_ready")
        scattered = [sem(f"scattered{i}") for i in range(2)]
        ln_step = sem("ln_step")
        rt_step = sem("rt_step")
        prep_step = sem("prep_step")

        block = ctx.enter_context(nc.Block())
        FILLS = 16 * (E * T // (P * FILL) + SH + 3)

        @block.sync
        def _(sp):
            sp.dma_start(wcat[:, :, 0:E], rw.rearrange("(k p) e -> p k e", p=P)).then_inc(const_loaded, 16)
            sp.dma_start(wraw[:], ipw.rearrange("(k p) d -> p k d", p=P)).then_inc(const_loaded, 16)
            sp.dma_start(lnw_sb[:], lnw).then_inc(const_loaded, 16)
            sp.dma_start(lnb_sb[:], lnb).then_inc(const_loaded, 16)
            sp.dma_start(bias_b[:], rbias.partition_broadcast(P)).then_inc(const_loaded, 16)
            sp.wait_ge(iotas, 4)
            rows = P * FILL
            for c in range(E * T // rows):
                sp.dma_start(table[c * rows:(c + 1) * rows].rearrange("(p f) w -> p f w", p=P),
                             fill[:]).then_inc(fills, 16)
            sp.dma_start(table[(E + SH) * T:SLOTS], fill[0:1]).then_inc(fills, 16)
            for s in range(SH):
                sp.dma_start(table[(E + s) * T:(E + s + 1) * T].rearrange("(p f) w -> p f w", p=P),
                             shared_fill[:]).then_inc(fills, 16)
            sp.dma_start(xn_d[T:T + P], zero_row[:]).then_inc(fills, 16)
            sp.dma_start(out[T:T + P], zero_row[:]).then_inc(fills, 16)

            def load(t, i, s):
                sp.wait_ge(x_free, s)
                sp.dma_start(xt[i][:], x[bass.ds(t * P, P)]).then_inc(x_loaded[i], 16)

            def store(t, i, s):
                sp.wait_ge(xn_ready, s)
                sp.dma_start(xn_d[bass.ds(t * P, P)], xn[i][:]).then_inc(xn_stored[i], 16)
                sp.wait_ge(base_ready, s)
                sp.dma_start(base_d[bass.ds(t * P, P)], bs[i][:]).then_inc(bs_stored[i], 16)

            sp.dma_start(xt[0][:], x[0:P]).then_inc(x_loaded[0], 16)
            sp.dma_start(xt[1][:], x[P:2 * P]).then_inc(x_loaded[1], 16)
            with sp.Fori(0, NT // 2 - 1) as i:
                for q in range(2):
                    store(i * 2 + q, q, i * 2 + q + 1)
                    load(i * 2 + q + 2, q, i * 2 + q + 1)
            for q in range(2):
                store(T // P - 2 + q, q, T // P - 1 + q)
            for q in range(2):
                sp.wait_ge(xn_stored[q], 16 * (NT // 2))
                sp.wait_ge(bs_stored[q], 16 * (NT // 2))

        @block.gpsimd
        def _(pool):
            pool.memset(ident[:], 0.0).then_inc(iotas, 1)
            pool.memset(ones_b[:], 1.0)
            pool.memset(tri[:], 1.0)
            pool.memset(fill[:], 0)
            pool.memset(zero_row[:], 0.0)
            pool.memset(minus_half[:], -0.5)
            pool.memset(shared_fill[:].bitcast(F32), 1.0).then_inc(iotas, 1)
            pool.wait_ge(iotas, 2)
            pool.iota(fill[:, :, 0].rearrange("p (r j) -> p r j", j=J), pattern=[[1, P], [0, J]], base=T,
                      channel_multiplier=0)
            pool.iota(shared_fill[:, :, 0], pattern=[[1, T // P]], base=0, channel_multiplier=T // P)\
                .then_inc(iotas, 2)
            pool.iota(iota_i[:], pattern=[[1, E]], base=0, channel_multiplier=0)
            pool.iota(cnt_i[:], pattern=[[T, E]], base=0, channel_multiplier=0)
            pool.iota(tid_i[:], pattern=[[0, 1]], base=0, channel_multiplier=1)
            pool.affine_select(out=tri[:], in_=tri[:], compare_op=ALU.is_ge, fill=0.0, base=-1,
                               pattern=[[1, P]], channel_multiplier=-1)
            pool.affine_select(out=ident[:], in_=ident[:], compare_op=ALU.not_equal, fill=1.0, base=0,
                               pattern=[[-1, P]], channel_multiplier=1).then_inc(iotas, 1)
            pool.wait_ge(fills, FILLS)

            def base(t1, i, n):
                pool.wait_ge(xn_ready, t1)
                pool.wait_ge(bs_stored[i], n) if n is not None else None
                pool.tensor_tensor(bs[i][:], xt[i][:], xn[i][:], ALU.add).then_inc(base_ready, 1)
                pool.wait_ge(base_ready, t1)
                pool.sem_inc(x_free, 1)

            def scatter(t1, i):
                wait_apart(pool, pool_passed, payload_ready, t1)
                for j in range(K):
                    pool.indirect_dma_start(
                        out=table, out_offset=bass.IndirectOffsetOnAxis(ap=slot8[i][:, j:j + 1], axis=0),
                        in_=payload[i][:, j, :], in_offset=None).then_inc(scattered[i], 16)

            def inverse_root(t1, var, rstd_, ready, made):
                pool.wait_ge(ready, t1)
                pool.tensor_tensor(rstd_[:], var[:, 1:2], minus_half[:], ALU.pow).then_inc(made, 1)

            inverse_root(1, mv[0], rstd[0], var_ready, rstd_ready)
            base(1, 0, None)
            inverse_root(2, mv[1], rstd[1], var_ready, rstd_ready)
            inverse_root(1, mv2[0], rs2[0], var2_ready, rstd2_ready)
            base(2, 1, None)
            with pool.Fori(0, NT // 2 - 1) as i:
                for q in range(2):
                    inverse_root(i * 2 + q + 3, mv[q], rstd[q], var_ready, rstd_ready)
                    inverse_root(i * 2 + q + 2, mv2[1 - q], rs2[1 - q], var2_ready, rstd2_ready)
                    scatter(i * 2 + q + 1, q)
                    base(i * 2 + q + 3, q, (i + 1) * 16)
            inverse_root(NT, mv2[1], rs2[1], var2_ready, rstd2_ready)
            for q in range(2):
                scatter(NT - 1 + q, q)
            for q in range(2):
                pool.wait_ge(scattered[q], 16 * K * (NT // 2))

        @block.scalar
        def _(act):
            act.sem_inc(tp_free, 2)
            act.sem_inc(zp_free, 1)

            def evacuate(t1, i):
                for h in range(2):
                    act.wait_ge(tp_ready, t1 * 2 - 1 + h)
                    nc.scalar.activation(xnT[i][:, h * 4:h * 4 + 4], tp[h][:], ACT.Copy).then_inc(tp_free, 1)

            def choose(t1, i, b, tb):
                act.wait_ge(lg_ready, t1)
                nc.scalar.activation(score[i][:], lg[i][:, 0:E], ACT.Sigmoid).then_inc(score_ready, 1)
                act.wait_ge(zp_ready, t1)
                nc.scalar.activation(zT[0:D, bass.ds(b * LP + tb * P + 1, P)], zp[0:D, 0:P], ACT.Copy)\
                    .then_inc(zp_free, 1)

            with act.Fori(0, B) as b:
                t0 = b * TPB
                evacuate(t0 + 1, 0)
                with act.Fori(0, TPB // 2 - 1) as i:
                    t = t0 + i * 2
                    evacuate(t + 2, 1)
                    choose(t + 1, 0, b, i * 2)
                    evacuate(t + 3, 0)
                    choose(t + 2, 1, b, i * 2 + 1)
                evacuate(t0 + TPB, 1)
                choose(t0 + TPB - 1, 0, b, TPB - 2)
                choose(t0 + TPB, 1, b, TPB - 1)

        @block.tensor
        def _(pe):
            pe.wait_ge(wprep, 1)
            for k in range(KH):
                nc.tensor.matmul(lg[0][:, 0:D], ones_f[:], wcat[:, k, E:E + D], start=k == 0, stop=k == KH - 1)
            for k in range(KH):
                last = nc.tensor.matmul(lg[1][:, 0:D], ones_f[:], wlnb[:, k], start=k == 0, stop=k == KH - 1)
            last.then_inc(sums_done, 1)
            pe.wait_ge(iotas, 5)
            pe.wait_ge(route_ready, 1)

            def transposes(t1, i):
                pe.wait_ge(xn_ready, t1)
                for h in range(2):
                    pe.wait_ge(tp_free, t1 * 2 - 1 + h)
                    for k in range(4):
                        last = nc.tensor.transpose(tp[h][:, k], xn[i][:, (h * 4 + k) * P:(h * 4 + k + 1) * P],
                                                   ident[:])
                    last.then_inc(tp_ready, 1)

            def project(t1, i):
                pe.wait_ge(tp_free, t1 * 2 + 2)
                pe.wait_ge(lg_free, t1)
                for k in range(KH):
                    last = nc.tensor.matmul(lg[i][:, 0:E + D], xnT[i][:, k], wcat[:, k], start=k == 0,
                                            stop=k == KH - 1)
                last.then_inc(lg_ready, 1)

            def rest(t1, i):
                pe.wait_ge(z_ready, t1)
                pe.wait_ge(zp_free, t1)
                nc.tensor.transpose(zp[0:D, 0:P], z[i][:], ident[:]).then_inc(zp_ready, 1)
                pe.wait_ge(sel_ready, t1)
                pe.wait_ge(rank_free, t1)
                nc.tensor.matmul(rank[:, 0:E], tri[:], sel[i][:], start=True, stop=True)
                nc.tensor.matmul(rank[:, E:2 * E], ones_b[:], sel[i][:], start=True, stop=True)\
                    .then_inc(rank_ready, 1)

            with pe.Fori(0, B) as b:
                t0 = b * TPB
                transposes(t0 + 1, 0)
                project(t0 + 1, 0)
                with pe.Fori(0, TPB // 2 - 1) as i:
                    t = t0 + i * 2
                    transposes(t + 2, 1)
                    project(t + 2, 1)
                    rest(t + 1, 0)
                    transposes(t + 3, 0)
                    project(t + 3, 0)
                    rest(t + 2, 1)
                transposes(t0 + TPB, 1)
                project(t0 + TPB, 1)
                rest(t0 + TPB - 1, 0)
                rest(t0 + TPB, 1)

        @block.vector
        def _(dve):
            v = nc.vector
            dve.sem_inc(rank_free, 1)
            step = Steps(dve, prep_step)
            v.memset(zT[:], 0.0)
            v.memset(ones_f[:], 1.0)
            dve.wait_ge(const_loaded, 16 * 5)
            v.tensor_tensor(wcat[:, :, E:E + D], wraw[:], bc(lnw_sb[:], 2, [P, KH, D]), ALU.mult)
            step(v.tensor_tensor(wlnb[:], wraw[:], bc(lnb_sb[:], 2, [P, KH, D]), ALU.mult))
            dve.sem_inc(wprep, 1)
            dve.wait_ge(iotas, 5)
            v.tensor_copy(iota_e[:], iota_i[:])
            v.tensor_copy(cnt_base[:], cnt_i[:])
            step(v.tensor_copy(tid[:], tid_i[:]))
            dve.wait_ge(sums_done, 1)
            v.tensor_scalar(neg_s[:], lg[0][:, 0:D], -1.0, None, ALU.mult)
            step(v.tensor_copy(c_b[:], lg[1][:, 0:D]))
            dve.sem_inc(route_ready, 1)
            dve.sem_inc(lg_free, 2)

            LN = 4
            RT = 23

            def stats(t, i, n):
                s = Steps(dve, ln_step, t * LN, dve_passed)
                dve.wait_ge(x_loaded[i], n)
                v.bn_stats(st[:, 0], xt[i][:, 0:512])
                s(v.bn_stats(st[:, 1], xt[i][:, 512:1024]), apart=True)
                s(v.bn_aggr(mv[i][:], st[:].rearrange("p a b -> p (a b)")))
                v.tensor_scalar(mv[i][:, 1:2], mv[i][:, 1:2], EPS, None, ALU.add).then_inc(var_ready, 1)

            def norm(t, i, stored):
                s = Steps(dve, ln_step, t * LN + 2, dve_passed)
                dve.wait_ge(rstd_ready, t + 1)
                if stored is not None:
                    dve.wait_ge(xn_stored[i], stored)
                    dve.wait_ge(base_ready, t - 1)
                v.tensor_scalar(xn[i][:], xt[i][:], mv[i][:, 0:1], rstd[i][:], ALU.subtract, ALU.mult)\
                    .then_inc(xn_ready, 1)
                dve.wait_ge(xn_ready, t + 1)
                v.bn_stats(st2[:, 0], xn[i][:, 0:512])
                s(v.bn_stats(st2[:, 1], xn[i][:, 512:1024]), apart=True)
                s(v.bn_aggr(mv2[i][:], st2[:].rearrange("p a b -> p (a b)")))
                v.tensor_scalar(mv2[i][:, 1:2], mv2[i][:, 1:2], EPS, None, ALU.add).then_inc(var2_ready, 1)
                assert s.n == LN - 2

            def route(t, i, done):
                s = Steps(dve, rt_step, t * RT, dve_passed)
                dve.wait_ge(score_ready, t + 1)
                dve.wait_ge(rstd2_ready, t + 1)
                s(v.scalar_tensor_tensor(out=zpre[:], in0=neg_s[:], scalar=mv2[i][:, 0:1], in1=lg[i][:, E:E + D],
                                         op0=ALU.mult, op1=ALU.add))
                dve.sem_inc(lg_free, 1)
                v.scalar_tensor_tensor(out=z[i][:], in0=zpre[:], scalar=rs2[i][:], in1=c_b[:],
                                       op0=ALU.mult, op1=ALU.add).then_inc(z_ready, 1)
                s(v.tensor_tensor(biased[:], score[i][:], bias_b[:], ALU.add))
                b4 = biased[:].rearrange("p (g a b) -> p g a b", g=G, b=2)
                v.tensor_tensor(mx[:], b4[:, :, :, 0], b4[:, :, :, 1], ALU.max)
                s(v.tensor_tensor(mn[:], b4[:, :, :, 0], b4[:, :, :, 1], ALU.min))
                v.tensor_tensor(top1[:], mx[:, :, 0], mx[:, :, 1], ALU.max)
                v.tensor_tensor(m2[:], mx[:, :, 0], mx[:, :, 1], ALU.min)
                s(v.tensor_tensor(m3[:], mn[:, :, 0], mn[:, :, 1], ALU.max))
                s(v.tensor_tensor(m2[:], m2[:], m3[:], ALU.max))
                s(v.tensor_tensor(gs[:], top1[:], m2[:], ALU.add), apart=True)
                s(v.max(g8[:], gs[:]), apart=True)
                s(v.max_index(gi[:], g8[:], gs[:]))
                s(v.tensor_copy(gif[:], gi[:]))
                s(v.tensor_tensor(gcmp[:], bc(iota_e[:, 0:G], 2, [P, G, TKG]),
                                  bc(gif[:, 0:TKG], 1, [P, G, TKG]), ALU.is_equal))
                s(v.tensor_reduce(gmask[:], gcmp[:], AX.X, ALU.add))
                s(v.tensor_tensor(masked[:].rearrange("p (g a) -> p g a", g=G),
                                  biased[:].rearrange("p (g a) -> p g a", g=G),
                                  bc(gmask[:], 2, [P, G, EG]), ALU.mult), apart=True)
                s(v.max(v8[:], masked[:]), apart=True)
                s(v.max_index(i8[:], v8[:], masked[:]))
                s(v.tensor_copy(i8f[:], i8[:]))
                s(v.tensor_tensor(oh[:], bc(iota_e[:], 1, [P, K, E]), bc(i8f[:], 2, [P, K, E]), ALU.is_equal))
                with nc.allow_low_precision(reason="sums of one-hot rows are 0 or 1"):
                    v.tensor_reduce(sel[i][:], oh[:].rearrange("p k e -> p e k"), AX.X, ALU.add)\
                        .then_inc(sel_ready, 1)
                s(v.tensor_tensor(prod[:], oh[:], bc(score[i][:], 1, [P, K, E]), ALU.mult))
                s(v.tensor_reduce(w8[:], prod[:], AX.X, ALU.add))
                s(v.tensor_reduce(wsum[:], w8[:], AX.X, ALU.add))
                s(v.reciprocal(rinv[:], wsum[:]))
                if done is not None:
                    dve.wait_ge(scattered[i], done)
                v.tensor_scalar(payload[i][:, :, 1].bitcast(F32), w8[:], rinv[:], ROUTED_SCALE,
                                ALU.mult, ALU.mult)
                v.tensor_copy(payload[i][:, :, 0], tid[:].to_broadcast([P, K]))
                dve.wait_ge(rank_ready, t + 1)
                s(v.tensor_tensor(slotrow[:], rank[:, 0:E], cnt_base[:], ALU.add))
                v.tensor_tensor(cnt_base[:], rank[:, E:2 * E], cnt_base[:], ALU.add)
                v.tensor_scalar(tid[:], tid[:], float(P), None, ALU.add).then_inc(rank_free, 1)
                s(v.tensor_tensor(prod[:], oh[:], bc(slotrow[:], 1, [P, K, E]), ALU.mult))
                s(v.tensor_reduce(slotf[:], prod[:], AX.X, ALU.add))
                dve.wait_ge(rank_free, t + 2)
                v.tensor_copy(slot8[i][:], slotf[:]).then_inc(payload_ready, 1)
                assert s.n == RT, s.n

            stats(0, 0, 16)
            norm(0, 0, None)
            stats(1, 1, 16)
            norm(1, 1, None)
            for q in range(2):
                stats(2 + q, q, 32)
                route(q, q, None)
                norm(2 + q, q, 16)
            with dve.Fori(1, NT // 2 - 1) as i:
                for q in range(2):
                    stats(i * 2 + 2 + q, q, i * 16 + 32)
                    route(i * 2 + q, q, i * (16 * K))
                    norm(i * 2 + 2 + q, q, i * 16 + 16)
            for q in range(2):
                route(NT - 2 + q, q, 8 * K * (NT - 2))


def scan_stage(nc, t_all, batches, io):
    (base_d, out, zT, convw, convb, xpT, xpB, xpC, dtT, dtb, alog, dpar, opT) = io
    T, B = t_all, batches
    CPB = T // B // C
    LP = T // B + 2
    with ExitStack() as ctx:
        def sb(name, shape, dt=F32):
            return ctx.enter_context(nc.sbuf_tensor(name, shape, dt))

        def pb(name, shape, dt=F32):
            return ctx.enter_context(nc.psum_tensor(name, shape, dt))

        def sem(name):
            return ctx.enter_context(nc.semaphore(name))

        cw = sb("cw", [D, 3])
        cb = sb("cb", [D, 1])
        w_dt = sb("w_dt", [D, R])
        w_B = sb("w_B", [D, P])
        w_C = sb("w_C", [D, P])
        w_dtp = sb("w_dtp", [R, D])
        b_dt = sb("b_dt", [D, 1])
        a_log = sb("a_log", [P, NG])
        a_neg = sb("a_neg", [P, NG])
        dp = sb("dp", [D, 1])
        w_o = sb("w_o", [D, H])
        spread = sb("spread", [D, NG, P])
        gather = sb("gather", [P, NG, D])
        conv = sb("conv", [D, C])
        u = sb("u", [D, C])
        dr = sb("dr", [R, C])
        Bs = sb("Bs", [P, C])
        Cs = sb("Cs", [P, C])
        pre = sb("pre", [D, C])
        ab = sb("ab", [D, C])
        ex = sb("ex", [D, C])
        ln = sb("ln", [D, C])
        ser = sb("ser", [D, C])
        small = sb("small", [D, C])
        delta = sb("delta", [D, C])
        du = sb("du", [D, C])
        dA = [sb(f"dA{i}", [P, C]) for i in range(2)]
        dBu = [sb(f"dBu{i}", [P, C]) for i in range(2)]
        hs = [sb(f"hs{i}", [P, C]) for i in range(2)]
        hc = [sb(f"hc{i}", [P, C]) for i in range(2)]
        state = sb("state", [P, NG])
        yT = sb("yT", [D, C])
        bs = [sb(f"base{i}", [P, H]) for i in range(J)]
        proj = pb("proj", [P, 512])
        rep_d = [pb(f"rep_d{i}", [P, 512]) for i in range(2)]
        rep_u = [pb(f"rep_u{i}", [P, 512]) for i in range(2)]
        yp = pb("yp", [P, 512])
        op = [pb(f"op{i}", [P, 512]) for i in range(2)]

        loaded = sem("loaded")
        dve_passed = sem("dve_passed")
        sp_passed = sem("sp_passed")
        consts = sem("consts")
        a_ready = sem("a_ready")
        conv_ready = sem("conv_ready")
        u_ready = sem("u_ready")
        proj_ready = sem("proj_ready")
        bc_ready = sem("bc_ready")
        pre_ready = sem("pre_ready")
        act_sp = sem("act_sp")
        sp_dve = sem("sp_dve")
        delta_ready = sem("delta_ready")
        rep_ready = sem("rep_ready")
        dA_ready = sem("dA_ready")
        dBu_ready = sem("dBu_ready")
        scan_done = sem("scan_done")
        dA_free = sem("dA_free")
        hc_ready = sem("hc_ready")
        y_acc = sem("y_acc")
        y_ready = sem("y_ready")
        op_ready = sem("op_ready")
        op_free = sem("op_free")
        base_in = [sem(f"base_in{i}") for i in range(J)]
        base_out = sem("base_out")
        dve_step = sem("dve_step")
        state_set = sem("state_set")

        block = ctx.enter_context(nc.Block())
        chunks = B * CPB

        @block.sync
        def _(sp):
            for dst, src in ((cw, convw), (cb, convb), (w_dt, xpT), (w_B, xpB), (w_C, xpC), (w_dtp, dtT),
                             (b_dt, dtb), (a_log, alog), (dp, dpar), (w_o, opT)):
                sp.dma_start(dst[:], src).then_inc(loaded, 16)
            with sp.Fori(0, chunks) as c:
                for j in range(J):
                    sp.dma_start(bs[j][:], base_d[bass.ds(c * C + j * P, P)]).then_inc(base_in[j], 16)
                for j in range(J):
                    sp.wait_ge(op_free, c * (2 * J) + 2 * j + 4)
                    sp.dma_start(out[bass.ds(c * C + j * P, P)], bs[j][:]).then_inc(base_out, 16)
                wait_apart(sp, sp_passed, base_out, c * (16 * J) + 16 * J)

        @block.gpsimd
        def _(pool):
            g = nc.gpsimd
            g.memset(spread[:], 1.0)
            g.memset(gather[:], 1.0).then_inc(consts, 1)
            pool.wait_ge(consts, 1)
            g.affine_select(out=spread[:], in_=spread[:], compare_op=ALU.is_ge, fill=0.0, base=0,
                            pattern=[[P, NG], [1, P]], channel_multiplier=-N)
            g.affine_select(out=gather[:], in_=gather[:], compare_op=ALU.is_ge, fill=0.0, base=0,
                            pattern=[[P, NG], [-N, D]], channel_multiplier=1).then_inc(consts, 1)
            pool.wait_ge(consts, 2)
            g.affine_select(out=spread[:], in_=spread[:], compare_op=ALU.is_ge, fill=0.0, base=N - 1,
                            pattern=[[-P, NG], [-1, P]], channel_multiplier=N)
            g.affine_select(out=gather[:], in_=gather[:], compare_op=ALU.is_ge, fill=0.0, base=N - 1,
                            pattern=[[-P, NG], [N, D]], channel_multiplier=-1).then_inc(consts, 1)
            pool.wait_ge(consts, 3)
            pool.sem_inc(hc_ready, 0 + 2)
            with pool.Fori(0, chunks) as c:
                for q in range(NG):
                    pool.wait_ge(scan_done, c * NG + q + 1)
                    pool.wait_ge(y_acc, c * NG + q + 1)
                    g.tensor_tensor(hc[q % 2][:], hs[q % 2][:], Cs[:], ALU.mult).then_inc(hc_ready, 1)

        @block.scalar
        def _(act):
            a = nc.scalar
            act.wait_ge(loaded, 160)
            a.activation(a_neg[:], a_log[:], ACT.Exp).then_inc(a_ready, 1)
            act.wait_ge(a_ready, 2)
            with act.Fori(0, chunks) as c:
                act.wait_ge(conv_ready, c + 1)
                a.activation(u[:], conv[:], ACT.Silu, bias=cb[:]).then_inc(u_ready, 1)
                act.wait_ge(proj_ready, c * 2 + 1)
                a.activation(dr[:], proj[0:R], ACT.Copy)
                a.activation(Bs[:], op[0][:], ACT.Copy)
                a.activation(Cs[:], op[1][:], ACT.Copy).then_inc(bc_ready, 1)
                act.wait_ge(pre_ready, c + 1)
                a.activation(ab[:], pre[:], ACT.Abs).then_inc(act_sp, 1)
                act.wait_ge(act_sp, c * 3 + 1)
                a.activation(ex[:], ab[:], ACT.Exp, scale=-1.0).then_inc(act_sp, 1)
                act.wait_ge(act_sp, c * 3 + 2)
                a.activation(ln[:], ex[:], ACT.Ln, bias=1.0).then_inc(act_sp, 1)
                for q in range(NG):
                    act.wait_ge(rep_ready, c * NG + q + 1)
                    act.wait_ge(dA_free, c * NG + q + 1)
                    a.activation(dA[q % 2][:], rep_d[q % 2][:], ACT.Exp, scale=a_neg[:, q:q + 1])\
                        .then_inc(dA_ready, 1)

        @block.tensor
        def _(pe):
            m = nc.tensor.matmul
            pe.wait_ge(loaded, 160)
            pe.wait_ge(consts, 3)
            pe.sem_inc(y_acc, 2)
            with pe.Fori(0, chunks) as c:
                pe.wait_ge(u_ready, c + 1)
                pe.wait_ge(op_free, c * (2 * J) + 2)
                m(proj[0:R], w_dt[:], u[:], start=True, stop=True)
                m(op[0][:], w_B[:], u[:], start=True, stop=True)
                m(op[1][:], w_C[:], u[:], start=True, stop=True).then_inc(proj_ready, 1)
                pe.wait_ge(bc_ready, c + 1)
                m(proj[0:D], w_dtp[:], dr[:], start=True, stop=True).then_inc(proj_ready, 1)
                pe.wait_ge(delta_ready, c + 1)

                def spread_to(q):
                    pe.wait_ge(dA_ready, c * NG + q + 1)
                    pe.wait_ge(dBu_ready, c * NG + q + 1)
                    m(rep_d[q % 2][:], spread[:, q], delta[:], start=True, stop=True)
                    m(rep_u[q % 2][:], spread[:, q], du[:], start=True, stop=True).then_inc(rep_ready, 1)

                spread_to(0)
                spread_to(1)
                for q in range(NG):
                    pe.wait_ge(hc_ready, c * NG + q + 3)
                    m(yp[0:D], gather[:, q], hc[q % 2][:], start=q == 0, stop=q == NG - 1).then_inc(y_acc, 1)
                    if q + 2 < NG:
                        spread_to(q + 2)
                pe.wait_ge(y_ready, c + 1)
                for j in range(J):
                    for h in range(2):
                        pe.wait_ge(op_free, c * (2 * J) + 2 * j + h + 1)
                        m(op[h][:], yT[:, j * P:(j + 1) * P], w_o[:, h * 512:(h + 1) * 512], start=True,
                          stop=True).then_inc(op_ready, 1)

        @block.vector
        def _(dve):
            v = nc.vector
            dve.wait_ge(a_ready, 1)
            v.tensor_scalar(a_neg[:], a_neg[:], -1.0, None, ALU.mult).then_inc(a_ready, 1)
            dve.wait_ge(loaded, 160)
            dve.sem_inc(dBu_ready, 2)
            dve.sem_inc(dA_ready, 2)
            dve.sem_inc(op_free, 2)
            dve.sem_inc(dA_free, 2)
            ST = 12
            with dve.Fori(0, B) as b:
                v.memset(state[:], 0.0).then_inc(state_set, 1)
                wait_apart(dve, dve_passed, state_set, b + 1)
                with dve.Fori(0, CPB) as cc:
                    c = b * CPB + cc
                    col = b * LP + cc * C
                    s = Steps(dve, dve_step, c * ST)
                    s(v.tensor_scalar(conv[:], zT[0:D, bass.ds(col, C)], cw[:, 0:1], None, ALU.mult))
                    s(v.scalar_tensor_tensor(out=conv[:], in0=zT[0:D, bass.ds(col + 1, C)], scalar=cw[:, 1:2],
                                             in1=conv[:], op0=ALU.mult, op1=ALU.add))
                    v.scalar_tensor_tensor(out=conv[:], in0=zT[0:D, bass.ds(col + 2, C)], scalar=cw[:, 2:3],
                                           in1=conv[:], op0=ALU.mult, op1=ALU.add).then_inc(conv_ready, 1)
                    dve.wait_ge(proj_ready, c * 2 + 2)
                    v.tensor_scalar(pre[:], proj[0:D], b_dt[:], None, ALU.add).then_inc(pre_ready, 1)
                    dve.wait_ge(act_sp, c * 3 + 2)
                    v.tensor_scalar(small[:], ex[:], 2.0 ** -5, None, ALU.is_lt)
                    s(v.tensor_scalar(ser[:], ex[:], -0.25, 1.0 / 3.0, ALU.mult, ALU.add))
                    s(v.tensor_tensor(ser[:], ser[:], ex[:], ALU.mult))
                    s(v.scalar_tensor_tensor(out=ser[:], in0=ser[:], scalar=-0.5, in1=ex[:], op0=ALU.add,
                                             op1=ALU.mult))
                    s(v.scalar_tensor_tensor(out=ser[:], in0=ser[:], scalar=1.0, in1=ex[:], op0=ALU.add,
                                             op1=ALU.mult))
                    dve.wait_ge(act_sp, c * 3 + 3)
                    s(v.tensor_tensor(ser[:], ser[:], ln[:], ALU.subtract))
                    s(v.tensor_tensor(ser[:], ser[:], small[:], ALU.mult))
                    s(v.tensor_tensor(ser[:], ser[:], ln[:], ALU.add))
                    s(v.scalar_tensor_tensor(out=ser[:], in0=pre[:], scalar=0.0, in1=ser[:], op0=ALU.max,
                                             op1=ALU.add))
                    s(v.tensor_scalar(delta[:], ser[:], 0.001, None, ALU.mult))
                    v.tensor_tensor(du[:], delta[:], u[:], ALU.mult).then_inc(delta_ready, 1)
                    dve.wait_ge(bc_ready, c + 1)
                    for q in range(NG):
                        dve.wait_ge(rep_ready, c * NG + q + 1)
                        v.tensor_tensor(dBu[q % 2][:], rep_u[q % 2][:], Bs[:], ALU.mult).then_inc(dBu_ready, 1)
                        dve.wait_ge(dBu_ready, c * NG + q + 3)
                        dve.wait_ge(dA_ready, c * NG + q + 3)
                        dve.wait_ge(hc_ready, c * NG + q + 1)
                        v.tensor_tensor_scan(hs[q % 2][:], dA[q % 2][:], dBu[q % 2][:], state[:, q:q + 1],
                                             ALU.mult, ALU.add).then_inc(scan_done, 1)
                        dve.wait_ge(scan_done, c * NG + q + 1)
                        v.tensor_copy(state[:, q:q + 1], hs[q % 2][:, C - 1:C]).then_inc(dA_free, 1)
                    dve.wait_ge(dA_free, c * NG + NG + 2)
                    dve.wait_ge(y_acc, c * NG + NG + 2)
                    s(v.scalar_tensor_tensor(out=yT[:], in0=u[:], scalar=dp[:], in1=yp[0:D], op0=ALU.mult,
                                             op1=ALU.add))
                    dve.sem_inc(y_ready, 1)
                    for j in range(J):
                        dve.wait_ge(base_in[j], c * 16 + 16)
                        for h in range(2):
                            dve.wait_ge(op_ready, c * (2 * J) + 2 * j + h + 1)
                            v.tensor_tensor(bs[j][:, h * 512:(h + 1) * 512], op[h][:],
                                            bs[j][:, h * 512:(h + 1) * 512], ALU.add).then_inc(op_free, 1)
                    assert s.n == ST, s.n


def plan_stage(nc, t_all, cnt_base, starts, experts):
    T = t_all
    NSH = SH * T // C
    NR = T * K // C + E - 1
    PAD = (E + SH) * T
    with ExitStack() as ctx:
        def sb(name, shape, dt=F32):
            return ctx.enter_context(nc.sbuf_tensor(name, shape, dt))

        reg_i = sb("reg_i", [1, E], I32)
        blk_i = sb("blk_i", [1, NR], I32)
        reg_f = sb("reg_f", [1, E])
        blk = sb("blk", [1, NR])
        cnt = sb("cnt", [1, E])
        cnt_int = sb("cnt_int", [1, E], I32)
        nblk = sb("nblk", [1, E])
        one = sb("one", [1, E])
        cum = sb("cum", [1, E])
        before = sb("before", [1, NR, E])
        eid = sb("eid", [1, NR])
        first = sb("first", [1, NR])
        start = sb("start", [1, NR])
        idle = sb("idle", [1, NR])
        made = ctx.enter_context(nc.semaphore("made"))
        done = ctx.enter_context(nc.semaphore("done"))
        block = ctx.enter_context(nc.Block())

        @block.gpsimd
        def _(pool):
            g = nc.gpsimd
            g.iota(reg_i[:], pattern=[[T, E]], base=0, channel_multiplier=0)
            g.iota(blk_i[:], pattern=[[1, NR]], base=0, channel_multiplier=0)
            g.iota(starts[:, 0:NSH], pattern=[[C, NSH]], base=E * T, channel_multiplier=0)
            g.iota(starts[:, NSH + NR:NSH + NR + 1], pattern=[[0, 1]], base=PAD, channel_multiplier=0)
            g.iota(experts[:, NSH + NR:NSH + NR + 1], pattern=[[0, 1]], base=E - 1, channel_multiplier=0)
            g.iota(experts[:, 0:NSH].rearrange("p (a b) -> p a b", a=SH), pattern=[[1, SH], [0, T // C]],
                   base=E, channel_multiplier=0).then_inc(made, 1)

        @block.vector
        def _(dve):
            v = nc.vector
            s = Steps(dve, done)
            dve.wait_ge(made, 1)
            v.memset(one[:], 1.0)
            v.tensor_copy(reg_f[:], reg_i[:])
            s(v.tensor_copy(blk[:], blk_i[:]))
            s(v.tensor_tensor(cnt[:], cnt_base[0:1], reg_f[:], ALU.subtract))
            s(v.tensor_scalar(cnt_int[:], cnt[:], float(C - 1), None, ALU.add))
            s(v.tensor_scalar(cnt_int[:], cnt_int[:], C.bit_length() - 1, None, ALU.logical_shift_right))
            s(v.tensor_copy(nblk[:], cnt_int[:]))
            s(v.tensor_tensor_scan(cum[:], one[:], nblk[:], 0.0, ALU.mult, ALU.add))
            s(v.tensor_tensor(before[:], bc(blk[:], 2, [1, NR, E]), bc(cum[:], 1, [1, NR, E]), ALU.is_ge))
            s(v.tensor_reduce(eid[:], before[:], AX.X, ALU.add))
            s(v.tensor_tensor(before[:], before[:], bc(nblk[:], 1, [1, NR, E]), ALU.mult))
            s(v.tensor_reduce(first[:], before[:], AX.X, ALU.add))
            s(v.tensor_tensor(first[:], blk[:], first[:], ALU.subtract))
            v.tensor_scalar(idle[:], eid[:], float(E), None, ALU.is_ge)
            s(v.tensor_scalar(start[:], eid[:], float(T), None, ALU.mult))
            s(v.scalar_tensor_tensor(out=start[:], in0=first[:], scalar=float(C), in1=start[:], op0=ALU.mult,
                                     op1=ALU.add))
            s(v.tensor_scalar(first[:], start[:], -1.0, float(PAD), ALU.mult, ALU.add))
            s(v.tensor_tensor(first[:], first[:], idle[:], ALU.mult))
            s(v.tensor_tensor(starts[:, NSH:NSH + NR], start[:], first[:], ALU.add))
            s(v.tensor_scalar(experts[:, NSH:NSH + NR], eid[:], float(E - 1), None, ALU.min))


def expert_stage(nc, t_all, io):
    (xn_d, out, table, w_all, starts, experts) = io
    T = t_all
    NB = SH * T // C + T * K // C + E - 1
    with ExitStack() as ctx:
        def sb(name, shape, dt=F32):
            return ctx.enter_context(nc.sbuf_tensor(name, shape, dt))

        def pb(name, shape, dt=F32):
            return ctx.enter_context(nc.psum_tensor(name, shape, dt))

        def sem(name):
            return ctx.enter_context(nc.semaphore(name))

        stage = [sb(f"stage{i}", [P, WC]) for i in range(NST)]
        w_hi = [sb(f"w_hi{q}", [P, WC], F32R) for q in range(NCH)]
        w_lo = [sb(f"w_lo{q}", [P, WC], F32R) for q in range(NCH)]
        xraw = sb("xraw", [P, J, H])
        x_hi = sb("x_hi", [P, KH, C], F32R)
        x_lo = sb("x_lo", [P, KH, C], F32R)
        a_hi = sb("a_hi", [P, KI, C], F32R)
        a_lo = sb("a_lo", [P, KI, C], F32R)
        sg = sb("sg", [P, C])
        av = sb("av", [P, C])
        y = sb("y", [P, J, H])
        idx_in = sb("idx_in", [P, J, 2], I32)
        idx_cur = sb("idx_cur", [P, J, 2], I32)
        ident = sb("ident2", [P, P])
        pg = [pb(f"pg{i}", [P, C]) for i in range(2)]
        pu = [pb(f"pu{i}", [P, C]) for i in range(2)]
        tp = [pb(f"tx{i}", [P, J, P]) for i in range(2)]
        pd = [pb(f"pd{i}", [P, 512]) for i in range(2)]

        made = sem("ident_made")
        pool_passed = sem("pool_passed")
        staged = [sem(f"staged{i}") for i in range(NST)]
        split_hi = sem("split_hi")
        split = sem("split")
        idx_loaded = sem("idx_loaded")
        idx_copied = sem("idx_copied")
        gathered = sem("gathered")
        tp_ready = sem("tx_ready")
        xh_ready = sem("xh_ready")
        xT_ready = sem("xT_ready")
        gu_ready = sem("gu_ready")
        gate_read = sem("gate_read")
        up_read = sem("up_read")
        ah_ready = sem("ah_ready")
        a_ready = sem("act_ready")
        a_used = sem("a_used")
        down_ready = sem("down_ready")
        down_read = sem("down_read")
        added = sem("added")
        y_free = sem("y_free")

        block = ctx.enter_context(nc.Block())

        @block.sync
        def _(sp):
            def load(b, q, s):
                e = sp.value_load(experts[0:1, bass.ds(b, 1)], min_val=0, max_val=E + SH - 1) if q in (0, 4) else load.e
                load.e = e
                sp.wait_ge(split, s)
                sp.dma_start(stage[q % NST][:], w_all[bass.ds(e * NCH + q, 1)]
                             .rearrange("a p c -> (a p) c")).then_inc(staged[q % NST], 16)

            for q in range(4):
                load(0, q, q + 1)
            with sp.Fori(0, NB) as b:
                for n, q in enumerate((4, 5)):
                    load(b, q, b * NCH + 4 + n + 1)
                for q in range(4):
                    load(b + 1, q, b * NCH + 6 + q + 1)

        @block.gpsimd
        def _(pool):
            g = nc.gpsimd
            g.memset(ident[:], 0.0).then_inc(made, 1)
            pool.wait_ge(made, 1)
            g.affine_select(out=ident[:], in_=ident[:], compare_op=ALU.not_equal, fill=1.0, base=0,
                            pattern=[[-1, P]], channel_multiplier=1).then_inc(made, 1)
            pool.sem_inc(y_free, J)

            def gather(b, n):
                first = pool.value_load(starts[0:1, bass.ds(b, 1)], min_val=0, max_val=(E + SH) * T)
                g.dma_start(idx_in[:], table[bass.ds(first, C)].rearrange("(p j) w -> p j w", p=P))\
                    .then_inc(idx_loaded, 16)
                wait_apart(pool, pool_passed, idx_loaded, n * 16)
                for j in range(J):
                    g.indirect_dma_start(out=xraw[:, j], out_offset=None, in_=xn_d,
                                         in_offset=bass.IndirectOffsetOnAxis(ap=idx_in[:, j, 0:1], axis=0))\
                        .then_inc(gathered, 16)

            gather(0, 1)
            with pool.Fori(0, NB) as b:
                pool.wait_ge(idx_copied, b + 1)
                pool.wait_ge(tp_ready, b * KH + KH)
                gather(b + 1, b + 2)
                for j in range(J):
                    wait_apart(pool, pool_passed, down_read, b * (2 * J) + 2 * j + 4)
                    g.indirect_dma_start(out=out, out_offset=bass.IndirectOffsetOnAxis(ap=idx_cur[:, j, 0:1], axis=0),
                                         in_=y[:, j], in_offset=None, compute_op=ALU.add).then_inc(added, 16)
                    pool.wait_ge(added, b * (16 * J) + 16 * j + 16)
                    pool.sem_inc(y_free, 1)
            pool.wait_ge(added, 16 * J * NB)
            pool.wait_ge(gathered, 16 * J * (NB + 1))

        @block.scalar
        def _(act):
            a = nc.scalar
            act.sem_inc(gate_read, 2)

            def high(q, n):
                act.wait_ge(staged[q % NST], n)
                a.activation(w_hi[q][:], stage[q % NST][:], ACT.Copy).then_inc(split_hi, 1)

            def x_high(k, n):
                act.wait_ge(tp_ready, n + k + 1)
                a.activation(x_hi[:, k], tp[k % 2][:].rearrange("p j c -> p (j c)"), ACT.Copy)\
                    .then_inc(xh_ready, 1)

            for q in range(4):
                high(q, 16 * (q // NST + 1))
            for k in range(KH):
                x_high(k, 0)
            with act.Fori(0, NB) as b:
                act.wait_ge(down_ready, b * KH + KH)
                for q in (4, 5):
                    high(q, b * 32 + 32)
                for i in range(KI):
                    act.wait_ge(gu_ready, b * KI + i + 1)
                    act.wait_ge(up_read, b * KI + i + 1)
                    a.activation(sg[:], pg[i % 2][:], ACT.Silu).then_inc(gate_read, 1)
                    act.wait_ge(up_read, b * KI + i + 2)
                    a.activation(a_hi[:, i], av[:], ACT.Copy).then_inc(ah_ready, 1)
                    high(i, b * 32 + 32 + 16 * (i // NST + 1))
                for k in range(KH):
                    x_high(k, b * KH + KH)

        @block.vector
        def _(dve):
            v = nc.vector
            dve.sem_inc(up_read, 1)
            dve.sem_inc(split, NST)
            dve.sem_inc(down_read, 2)
            dve.sem_inc(a_ready, 1)

            def low(q, s):
                dve.wait_ge(split_hi, s)
                v.tensor_tensor(w_lo[q][:], stage[q % NST][:], w_hi[q][:], ALU.subtract).then_inc(split, 1)

            def x_low(k, n):
                dve.wait_ge(xh_ready, n + k + 1)
                v.tensor_tensor(x_lo[:, k], tp[k % 2][:].rearrange("p j c -> p (j c)"), x_hi[:, k], ALU.subtract)\
                    .then_inc(xT_ready, 1)

            for q in range(4):
                low(q, q + 1)
            for k in range(KH):
                x_low(k, 0)
            with dve.Fori(0, NB) as b:
                dve.wait_ge(idx_loaded, b * 16 + 16)
                dve.wait_ge(y_free, b * J + J)
                v.tensor_copy(idx_cur[:], idx_in[:]).then_inc(idx_copied, 1)
                dve.wait_ge(idx_copied, b + 1)
                for q in (4, 5):
                    low(q, b * NCH + q + 1)
                for i in range(KI):
                    dve.wait_ge(gate_read, b * KI + i + 3)
                    dve.wait_ge(a_ready, b * KI + i + 1)
                    v.tensor_tensor(av[:], pu[i % 2][:], sg[:], ALU.mult).then_inc(up_read, 1)
                    dve.wait_ge(ah_ready, b * KI + i + 1)
                    v.tensor_tensor(a_lo[:, i], av[:], a_hi[:, i], ALU.subtract).then_inc(a_ready, 1)
                    low(i, b * NCH + NCH + i + 1)
                for k in range(KH):
                    x_low(k, b * KH + KH)
                    j, h = k // 2, k % 2
                    dve.wait_ge(down_ready, b * KH + KH + k + 1)
                    v.tensor_scalar(y[:, j, h * 512:(h + 1) * 512], pd[k % 2][:],
                                    idx_cur[:, j, 1:2].bitcast(F32), None, ALU.mult).then_inc(down_read, 1)

        @block.tensor
        def _(pe):
            m = nc.tensor.matmul
            pe.sem_inc(down_ready, KH)
            pe.wait_ge(made, 2)

            def transposes(k, n):
                pe.wait_ge(xT_ready, n + k - 1) if not (isinstance(n, int) and n + k < 2) else None
                for j in range(J):
                    last = nc.tensor.transpose(tp[k % 2][:, j], xraw[:, j, k * P:(k + 1) * P], ident[:])
                last.then_inc(tp_ready, 1)

            def product(dst, w, cols, x, xs, first, last):
                hi, lo = w
                m(dst, hi[:, cols], x[0][xs], start=first, stop=False)
                m(dst, hi[:, cols], x[1][xs], start=False, stop=False)
                return m(dst, lo[:, cols], x[0][xs], start=False, stop=last)

            pe.wait_ge(gathered, 16 * J)
            for k in range(KH):
                transposes(k, 0)
            with pe.Fori(0, NB) as b:
                pe.wait_ge(xT_ready, b * KH + KH)
                for i in range(KI):
                    pe.wait_ge(split, b * NCH + i + 1 + NST)
                    pe.wait_ge(gate_read, b * KI + i + 1)
                    pe.wait_ge(up_read, b * KI + i) if i >= 1 else pe.wait_ge(gate_read, b * KI + 1)
                    for half, dst in ((0, pg[i % 2]), (1, pu[i % 2])):
                        for k in range(KH):
                            c0 = half * 1024 + k * P
                            last = product(dst[:], (w_hi[i], w_lo[i]), slice(c0, c0 + P), (x_hi, x_lo),
                                           (slice(None), k), k == 0, k == KH - 1)
                    last.then_inc(gu_ready, 1)

                def down(k, ks):
                    j, h = k // 2, k % 2
                    for i in ks:
                        for part, (wa, wb) in enumerate(((a_hi, w_hi), (a_hi, w_lo), (a_lo, w_hi))):
                            last = m(pd[k % 2][:], wa[:, i, j * P:(j + 1) * P], wb[4 + h][:, i * 512:(i + 1) * 512],
                                     start=i == 0 and part == 0, stop=i == KI - 1 and part == 2)
                    return last

                pe.wait_ge(gathered, b * (16 * J) + 32 * J)
                pe.wait_ge(split, b * NCH + NCH + NST)
                for k in range(KH):
                    if k != 1:
                        transposes(k, b * KH + KH)
                    if k == 0:
                        transposes(1, b * KH + KH)
                        pe.wait_ge(down_read, b * KH + 1)
                        pe.wait_ge(a_ready, b * KI + KI)
                        down(0, range(KI - 1))
                        pe.wait_ge(down_read, b * KH + 2)
                        down(1, range(KI - 1))
                        pe.wait_ge(a_ready, b * KI + KI + 1)
                        down(0, (KI - 1,)).then_inc(down_ready, 1)
                    elif k == 1:
                        down(1, (KI - 1,)).then_inc(down_ready, 1)
                    else:
                        pe.wait_ge(down_read, b * KH + k + 1)
                        down(k, range(KI)).then_inc(down_ready, 1)


def build(nc, A, T, B):
    slots = (E + SH) * T + C
    NB = SH * T // C + T * K // C + E - 1
    xn_d = nc.dram_tensor("xn_rows", [T + P, H], F32, kind="Internal").ap()
    base_d = nc.dram_tensor("base_rows", [T, H], F32, kind="Internal").ap()
    table = nc.dram_tensor("slot_table", [slots, 2], I32, kind="Internal").ap()
    with ExitStack() as ctx:
        starts = ctx.enter_context(nc.sbuf_tensor("starts", [1, NB + 1], I32))
        experts = ctx.enter_context(nc.sbuf_tensor("experts", [1, NB + 1], I32))
        with ExitStack() as part:
            cnt_base = part.enter_context(nc.sbuf_tensor("cnt_base", [P, E], F32))
            zT = part.enter_context(nc.sbuf_tensor("zT", [P, B * (T // B + 2)], F32))
            route_stage(nc, T, B, (A["x"], xn_d, base_d, A["out"], table, A["rw"], A["ipw"], A["lnw"], A["lnb"],
                                   A["rbias"], zT, cnt_base), slots)
            scan_stage(nc, T, B, (base_d, A["out"], zT, A["convw"], A["convb"], A["xpT"], A["xpB"], A["xpC"],
                                  A["dtT"], A["dtb"], A["alog"], A["dpar"], A["opT"]))
            plan_stage(nc, T, cnt_base, starts, experts)
        expert_stage(nc, T, (xn_d, A["out"], table, A["w_all"], starts, experts))


def layouts(x, ln_w, ln_b, in_proj_W, conv_w, conv_b, x_proj_W, dt_proj_W, dt_proj_b, A_log, D_param, out_proj_W,
            router_w, router_bias, w_gate, w_up, w_down, sw_gate, sw_up, sw_down):
    import numpy as np

    def halves(w):
        return w.reshape(H, SH, I).transpose(1, 0, 2)

    gate = np.concatenate([w_gate, halves(sw_gate)])
    up = np.concatenate([w_up, halves(sw_up)])
    down = np.concatenate([w_down, sw_down.reshape(SH, I, H)])
    n = E + SH
    gu = np.stack([gate, up]).reshape(2, n, KH, P, KI, P).transpose(1, 4, 3, 0, 2, 5).reshape(n, KI, P, WC)
    dn = down.reshape(n, KI, P, 2, 512).transpose(0, 3, 2, 1, 4).reshape(n, 2, P, WC)
    T = x.shape[0] * x.shape[1]
    return {
        "x": x.reshape(T, H), "rw": router_w, "ipw": in_proj_W.T, "lnw": ln_w.reshape(KH, P).T,
        "lnb": ln_b.reshape(KH, P).T, "rbias": router_bias, "convw": conv_w.reshape(D, 3),
        "convb": conv_b.reshape(D, 1), "xpT": x_proj_W[:R].T, "xpB": np.tile(x_proj_W[R:R + N].T, (1, PG)),
        "xpC": np.tile(x_proj_W[R + N:].T, (1, PG)), "dtT": dt_proj_W.T, "dtb": dt_proj_b.reshape(D, 1),
        "alog": A_log.reshape(NG, P).T, "dpar": D_param.reshape(D, 1), "opT": out_proj_W.T,
        "w_all": np.concatenate([gu, dn], axis=1).reshape(n * NCH, P, WC),
    }


def kernel(**inputs):
    import numpy as np
    import concourse.bacc as bacc
    from concourse import mybir as _mybir
    from concourse.bass_utils import run_bass_kernel_spmd

    names = {k.replace("L0_attn_feat_patch", "x").replace("L0_attn_", "").replace("L0_ffn_", ""): np.asarray(v)
             for k, v in inputs.items()}
    arrays = {k: np.ascontiguousarray(v) for k, v in layouts(**names).items()}
    B, L = names["x"].shape[:2]
    T = B * L
    nc = bacc.Bacc("TRN2", target_bir_lowering=False, num_devices=1)
    A = {k: nc.dram_tensor(f"in_{k}", v.shape, _mybir.dt.from_np(v.dtype), kind="ExternalInput").ap()
         for k, v in arrays.items()}
    A["out"] = nc.dram_tensor("out_rows", [T + P, H], F32, kind="ExternalOutput").ap()
    build(nc, A, T, B)
    r = run_bass_kernel_spmd(nc, [{f"in_{k}": v for k, v in arrays.items()}], core_ids=[0])
    return r.results[0]["out_rows"][:T].reshape(B, L, H)
```

```python
import concourse.bass as bass
from concourse import mybir
from contextlib import ExitStack

F32 = mybir.dt.float32
F32R = mybir.dt.float32r
BF16 = mybir.dt.bfloat16
I32 = mybir.dt.int32
U32 = mybir.dt.uint32
ALU = mybir.AluOpType
ACT = mybir.ActivationFunctionType
AX = mybir.AxisListType

P = 128
H = 1024
KH = H // P
E, G, TKG, K = 32, 8, 4, 8
EG = E // G
I = 512
KI = I // P
SH = 2
D, N, R = 96, 16, 6
PG = P // N
NG = D // PG
C = 512
J = C // P
EPS = 1e-5
ROUTED_SCALE = 2.5
NCH = 6
NST = 3
WC = 2048


def wait_apart(eng, passed, sem, value):
    eng.wait_ge(sem, value)
    eng.sem_inc(passed, 1)


class Steps:

    def __init__(self, eng, sem, base=0, passed=None):
        self.eng, self.sem, self.base, self.passed, self.n = eng, sem, base, passed, 0

    def __call__(self, ins, apart=False):
        self.n += 1
        ins.then_inc(self.sem, 1)
        if apart:
            wait_apart(self.eng, self.passed, self.sem, self.base + self.n)
        else:
            self.eng.wait_ge(self.sem, self.base + self.n)


def bc(ap, axis, shape):
    return ap.unsqueeze(axis).to_broadcast(shape)


def route_stage(nc, T, B, io):
    (x, xn_d, base_d, out, table, rw, ipw, lnw, lnb, rbias, zT, cnt_base, slots, payload) = io
    NC = T // C
    CPB = NC // B
    FILL = 512
    FILLS = 16 * (E * T // (P * FILL) + SH + 3)

    with ExitStack() as ctx:
        def sb(name, shape, dt=F32):
            return ctx.enter_context(nc.sbuf_tensor(name, shape, dt))

        def ring(name, shape, dt=F32):
            return [sb(f"{name}{i}", shape, dt) for i in range(2)]

        def pb(name, shape, dt=F32):
            return ctx.enter_context(nc.psum_tensor(name, shape, dt))

        def sem(name):
            return ctx.enter_context(nc.semaphore(name))

        wcat = sb("wcat", [P, KH, E + D])
        wraw = sb("wraw", [P, KH, D])
        wlnb = sb("wlnb", [P, KH, D])
        lnw_sb = sb("lnw_sb", [P, KH])
        lnb_sb = sb("lnb_sb", [P, KH])
        bias_b = sb("bias_b", [P, E])
        neg_s = sb("neg_s", [P, D])
        c_b = sb("c_b", [P, D])
        ident = sb("ident", [P, P])
        ones_f = sb("ones_f", [P, P])
        ones_b = sb("ones_b", [P, P], BF16)
        tri = sb("tri", [P, P], BF16)
        iota_i = sb("iota_i", [P, E], I32)
        iota_e = sb("iota_e", [P, E])
        cnt_i = sb("cnt_i", [P, E], I32)
        tid_i = sb("tid_i", [P, J], I32)
        tid = sb("tid", [P, J])
        fill = sb("fill", [P, FILL, 2], I32)
        shared_fill = sb("shared_fill", [P, T // P, 2], I32)
        zero_row = sb("zero_row", [P, H])
        minus_half = sb("minus_half", [P, J])

        xt = ring("xt", [P, J, H])
        xn = ring("xn", [P, J, H])
        bs = sb("bs", [P, J, H])
        xnT = ring("xnT", [P, KH, P])
        st = sb("st", [P, J, 2, 6])
        mv = sb("mv", [P, J, 2])
        rstd = sb("rstd", [P, J])
        st2 = sb("st2", [P, J, 2, 6])
        mv2 = ring("mv2_", [P, J, 2])
        rs2 = ring("rs2_", [P, J])
        score = ring("score", [P, J, E])
        zpre = sb("zpre", [P, J, D])
        z = sb("z", [P, J, D])
        biased = sb("biased", [P, J, E])
        mx = sb("mx", [P, J * G, 2])
        mn = sb("mn", [P, J * G, 2])
        top1 = sb("top1", [P, J * G])
        m2 = sb("m2", [P, J * G])
        m3 = sb("m3", [P, J * G])
        gs = sb("gs", [P, J, G])
        g8 = sb("g8", [P, J, 8])
        gi = sb("gi", [P, J, 8], U32)
        gif = sb("gif", [P, J, 8])
        gcmp = sb("gcmp", [P, J, G, TKG])
        gmask = sb("gmask", [P, J, G])
        masked = sb("masked", [P, J, E])
        v8 = sb("v8", [P, J, 8])
        i8 = sb("i8", [P, J, 8], U32)
        i8f = sb("i8f", [P, J, 8])
        oh = sb("oh", [P, J * K, E])
        prod = sb("prod", [P, J * K, E])
        sel = sb("sel", [P, J, E], BF16)
        w8 = sb("w8", [P, J, K])
        wsum = sb("wsum", [P, J])
        rinv = sb("rinv", [P, J])
        slotrow = sb("slotrow", [P, J, E])
        slotf = sb("slotf", [P, J * K])

        tp = [pb(f"tp{i}", [P, 4, P]) for i in range(2)]
        lg = [pb(f"lg{i}", [P, J, E + D]) for i in range(2)]
        rank = pb("rank", [P, 512])
        zp = pb("zp", [P, J * P])

        const_loaded = sem("const_loaded")
        dve_passed = sem("dve_passed")
        iotas = sem("iotas")
        fills = sem("fills")
        wprep = sem("wprep")
        sums_done = sem("sums_done")
        route_ready = sem("route_ready")
        x_loaded = [sem(f"x_loaded{i}") for i in range(2)]
        var_ready = sem("var_ready")
        rstd_ready = sem("rstd_ready")
        var2_ready = sem("var2_ready")
        rstd2_ready = sem("rstd2_ready")
        xn_ready = sem("xn_ready")
        base_ready = sem("base_ready")
        xn_stored = [sem(f"xn_stored{i}") for i in range(2)]
        base_stored = sem("base_stored")
        base_free = sem("base_free")
        tp_ready = sem("tp_ready")
        tp_free = sem("tp_free")
        lg_ready = sem("lg_ready")
        score_ready = sem("score_ready")
        lg_free = sem("lg_free")
        z_ready = sem("z_ready")
        zp_ready = sem("zp_ready")
        zp_free = sem("zp_free")
        sel_ready = sem("sel_ready")
        rank_ready = sem("rank_ready")
        rank_free = sem("rank_free")
        ln_step = sem("ln_step")
        rt_step = sem("rt_step")
        prep_step = sem("prep_step")

        block = ctx.enter_context(nc.Block())

        @block.sync
        def _(sp):
            def rows(dram, c):
                return dram[bass.ds(c * C, C)].rearrange("(j p) h -> p j h", p=P)

            def load(c, i):
                sp.dma_start(xt[i][:], rows(x, c)).then_inc(x_loaded[i], 16)

            def store(c, i, n):
                sp.wait_ge(xn_ready, n * J)
                sp.dma_start(rows(xn_d, c), xn[i][:]).then_inc(xn_stored[i], 16)
                sp.wait_ge(base_ready, n)
                sp.dma_start(rows(base_d, c), bs[:]).then_inc(base_stored, 16)

            load(0, 0)
            sp.dma_start(wcat[:, :, 0:E], rw.rearrange("(k p) e -> p k e", p=P)).then_inc(const_loaded, 16)
            sp.dma_start(wraw[:], ipw.rearrange("(k p) d -> p k d", p=P)).then_inc(const_loaded, 16)
            sp.dma_start(lnw_sb[:], lnw).then_inc(const_loaded, 16)
            sp.dma_start(lnb_sb[:], lnb).then_inc(const_loaded, 16)
            sp.dma_start(bias_b[:], rbias.partition_broadcast(P)).then_inc(const_loaded, 16)
            load(1, 1)
            sp.wait_ge(iotas, 4)
            span = P * FILL
            for c in range(E * T // span):
                sp.dma_start(table[c * span:(c + 1) * span].rearrange("(p f) w -> p f w", p=P),
                             fill[:]).then_inc(fills, 16)
            sp.dma_start(table[(E + SH) * T:(E + SH) * T + C], fill[0:1]).then_inc(fills, 16)
            for s in range(SH):
                sp.dma_start(table[(E + s) * T:(E + s + 1) * T].rearrange("(p f) w -> p f w", p=P),
                             shared_fill[:]).then_inc(fills, 16)
            sp.dma_start(xn_d[T:T + P], zero_row[:]).then_inc(fills, 16)
            sp.dma_start(out[T:T + P], zero_row[:]).then_inc(fills, 16)
            with sp.Fori(0, NC // 2 - 1) as i:
                for q in range(2):
                    store(i * 2 + q, q, i * 2 + q + 1)
                    load(i * 2 + q + 2, q)
            for q in range(2):
                store(NC - 2 + q, q, NC - 1 + q)
            for q in range(2):
                sp.wait_ge(xn_stored[q], 16 * (NC // 2))
            sp.wait_ge(base_stored, 16 * NC)
            sp.wait_ge(fills, FILLS)

        @block.gpsimd
        def _(pool):
            pool.memset(ident[:], 0.0).then_inc(iotas, 1)
            pool.memset(ones_b[:], 1.0)
            pool.memset(tri[:], 1.0)
            pool.memset(fill[:], 0)
            pool.memset(zero_row[:], 0.0)
            pool.memset(minus_half[:], -0.5)
            pool.memset(shared_fill[:].bitcast(F32), 1.0).then_inc(iotas, 1)
            pool.wait_ge(iotas, 2)
            pool.iota(fill[:, :, 0].rearrange("p (h r j) -> p h r j", h=2, j=2),
                      pattern=[[0, 2], [1, P], [0, 2]], base=T, channel_multiplier=0)
            pool.iota(shared_fill[:, :, 0], pattern=[[1, T // P]], base=0, channel_multiplier=T // P)\
                .then_inc(iotas, 2)
            pool.iota(iota_i[:], pattern=[[1, E]], base=0, channel_multiplier=0)
            pool.iota(cnt_i[:], pattern=[[T, E]], base=0, channel_multiplier=0)
            pool.iota(tid_i[:], pattern=[[P, J]], base=0, channel_multiplier=1)
            pool.affine_select(out=tri[:], in_=tri[:], compare_op=ALU.is_ge, fill=0.0, base=-1,
                               pattern=[[1, P]], channel_multiplier=-1)
            pool.affine_select(out=ident[:], in_=ident[:], compare_op=ALU.not_equal, fill=1.0, base=0,
                               pattern=[[-1, P]], channel_multiplier=1).then_inc(iotas, 1)

            def chunk(n, i):
                pool.wait_ge(var_ready, n)
                pool.tensor_tensor(rstd[:], mv[:, :, 1], minus_half[:], ALU.pow).then_inc(rstd_ready, 1)
                for j in range(J):
                    pool.wait_ge(xn_ready, (n - 1) * J + j + 1)
                    if j == 0:
                        pool.wait_ge(base_free, n)
                    last = pool.tensor_tensor(bs[:, j], xt[i][:, j], xn[i][:, j], ALU.add)
                last.then_inc(base_ready, 1)
                pool.wait_ge(var2_ready, n)
                pool.tensor_tensor(rs2[i][:], mv2[i][:, :, 1], minus_half[:], ALU.pow).then_inc(rstd2_ready, 1)
                pool.wait_ge(base_stored, n * 16)
                pool.sem_inc(base_free, 1)

            pool.sem_inc(base_free, 1)
            with pool.Fori(0, NC // 2) as i:
                for q in range(2):
                    chunk(i * 2 + q + 1, q)

        @block.scalar
        def _(act):
            act.sem_inc(tp_free, 2)
            act.sem_inc(zp_free, 1)

            def evacuate(c, n):
                for j in range(J):
                    for h in range(2):
                        act.wait_ge(tp_ready, c * (2 * J) + 2 * j + h + 1)
                        nc.scalar.activation(xnT[j % 2][:, h * 4:h * 4 + 4], tp[h][:], ACT.Copy)\
                            .then_inc(tp_free, 1)

            def choose(c, i):
                act.wait_ge(lg_ready, c * J + J)
                nc.scalar.activation(score[i][:], lg[i][:, :, 0:E], ACT.Sigmoid).then_inc(score_ready, 1)

            def border(c):
                at = (c + 1) * (C + 2)
                act.wait_ge(zp_ready, c + 1)
                nc.scalar.activation(zT[0:D, bass.ds(at + 1, C)], zp[0:D], ACT.Copy)
                nc.scalar.activation(zT[0:D, bass.ds(at - 1, 1)], zp[0:D, 0:1], ACT.Copy)
                nc.scalar.activation(zT[0:D, bass.ds(at + C + 2, 1)], zp[0:D, C - 1:C], ACT.Copy)\
                    .then_inc(zp_free, 1)

            evacuate(0, 1)
            choose(0, 0)
            with act.Fori(0, NC // 2 - 1) as i:
                for q in range(2):
                    evacuate(i * 2 + q + 1, None)
                    choose(i * 2 + q + 1, 1 - q)
                    border(i * 2 + q)
            evacuate(NC - 1, None)
            choose(NC - 1, 1)
            border(NC - 2)
            border(NC - 1)

        @block.tensor
        def _(pe):
            pe.wait_ge(wprep, 1)
            for k in range(KH):
                nc.tensor.matmul(lg[0][:, 0, 0:D], ones_f[:], wcat[:, k, E:E + D], start=k == 0,
                                 stop=k == KH - 1)
            for k in range(KH):
                last = nc.tensor.matmul(lg[1][:, 0, 0:D], ones_f[:], wlnb[:, k], start=k == 0,
                                        stop=k == KH - 1)
            last.then_inc(sums_done, 1)
            pe.wait_ge(iotas, 5)
            pe.wait_ge(route_ready, 1)

            def transposes(c, j, i):
                pe.wait_ge(xn_ready, c * J + j + 1)
                for h in range(2):
                    pe.wait_ge(tp_free, c * (2 * J) + 2 * j + h + 1)
                    for k in range(4):
                        last = nc.tensor.transpose(tp[h][:, k], xn[i][:, j, (h * 4 + k) * P:(h * 4 + k + 1) * P],
                                                   ident[:])
                    last.then_inc(tp_ready, 1)

            def project(c, j, i):
                pe.wait_ge(tp_free, c * (2 * J) + 2 * j + 4)
                if j == 0:
                    pe.wait_ge(lg_free, c + 1)
                for k in range(KH):
                    last = nc.tensor.matmul(lg[i][:, j], xnT[j % 2][:, k], wcat[:, k], start=k == 0,
                                            stop=k == KH - 1)
                last.then_inc(lg_ready, 1)

            def forward(c, i):
                transposes(c, 0, i)
                for j in range(J):
                    project(c, j, i)
                    if j + 1 < J:
                        transposes(c, j + 1, i)

            def rest(c):
                pe.wait_ge(z_ready, c + 1)
                pe.wait_ge(zp_free, c + 1)
                for j in range(J):
                    last = nc.tensor.transpose(zp[0:D, j * P:(j + 1) * P], z[:, j], ident[:])
                last.then_inc(zp_ready, 1)
                pe.wait_ge(sel_ready, c + 1)
                pe.wait_ge(rank_free, c + 1)
                for j in range(J):
                    for jj in range(j):
                        nc.tensor.matmul(rank[:, j * E:(j + 1) * E], ones_b[:], sel[:, jj], start=jj == 0,
                                         stop=False)
                    nc.tensor.matmul(rank[:, j * E:(j + 1) * E], tri[:], sel[:, j], start=j == 0, stop=True)
                for j in range(J):
                    last = nc.tensor.matmul(rank[:, J * E:J * E + E], ones_b[:], sel[:, j], start=j == 0,
                                            stop=j == J - 1)
                last.then_inc(rank_ready, 1)

            forward(0, 0)
            with pe.Fori(0, NC // 2 - 1) as i:
                for q in range(2):
                    forward(i * 2 + q + 1, 1 - q)
                    rest(i * 2 + q)
            forward(NC - 1, 1)
            rest(NC - 2)
            rest(NC - 1)

        @block.vector
        def _(dve):
            v = nc.vector
            dve.sem_inc(rank_free, 1)
            step = Steps(dve, prep_step)
            v.memset(zT[:], 0.0)
            v.memset(ones_f[:], 1.0)
            dve.wait_ge(const_loaded, 16 * 5)
            v.tensor_tensor(wcat[:, :, E:E + D], wraw[:], bc(lnw_sb[:], 2, [P, KH, D]), ALU.mult)
            step(v.tensor_tensor(wlnb[:], wraw[:], bc(lnb_sb[:], 2, [P, KH, D]), ALU.mult))
            dve.sem_inc(wprep, 1)
            dve.wait_ge(iotas, 5)
            v.tensor_copy(iota_e[:], iota_i[:])
            v.tensor_copy(cnt_base[:], cnt_i[:])
            step(v.tensor_copy(tid[:], tid_i[:]))
            dve.wait_ge(sums_done, 1)
            v.tensor_scalar(neg_s[:], lg[0][:, 0, 0:D], -1.0, None, ALU.mult)
            step(v.tensor_copy(c_b[:], lg[1][:, 0, 0:D]))
            dve.sem_inc(route_ready, 1)
            dve.sem_inc(lg_free, 2)

            LN = 4
            RT = 25

            def norms(c, i, loads, stored):
                s = Steps(dve, ln_step, c * LN, dve_passed)
                dve.wait_ge(x_loaded[i], loads)
                for j in range(J):
                    for h in range(2):
                        last = v.bn_stats(st[:, j, h], xt[i][:, j, h * 512:(h + 1) * 512])
                s(last, apart=True)
                for j in range(J):
                    last = v.bn_aggr(mv[:, j], st[:, j].rearrange("p a b -> p (a b)"))
                s(last)
                v.tensor_scalar(mv[:, :, 1], mv[:, :, 1], EPS, None, ALU.add).then_inc(var_ready, 1)
                dve.wait_ge(rstd_ready, c + 1)
                if stored is not None:
                    dve.wait_ge(xn_stored[i], stored)
                    dve.wait_ge(base_ready, c - 1)
                for j in range(J):
                    v.tensor_scalar(xn[i][:, j], xt[i][:, j], mv[:, j, 0:1], rstd[:, j:j + 1], ALU.subtract,
                                    ALU.mult).then_inc(xn_ready, 1)
                dve.wait_ge(xn_ready, c * J + J)
                for j in range(J):
                    for h in range(2):
                        last = v.bn_stats(st2[:, j, h], xn[i][:, j, h * 512:(h + 1) * 512])
                s(last, apart=True)
                for j in range(J):
                    last = v.bn_aggr(mv2[i][:, j], st2[:, j].rearrange("p a b -> p (a b)"))
                s(last)
                v.tensor_scalar(mv2[i][:, :, 1], mv2[i][:, :, 1], EPS, None, ALU.add).then_inc(var2_ready, 1)
                assert s.n == LN

            def route(c, i):
                s = Steps(dve, rt_step, c * RT, dve_passed)
                dve.wait_ge(score_ready, c + 1)
                dve.wait_ge(rstd2_ready, c + 1)
                for j in range(J):
                    last = v.scalar_tensor_tensor(out=zpre[:, j], in0=neg_s[:], scalar=mv2[i][:, j, 0:1],
                                                  in1=lg[i][:, j, E:E + D], op0=ALU.mult, op1=ALU.add)
                s(last)
                dve.sem_inc(lg_free, 1)
                for j in range(J):
                    last = v.scalar_tensor_tensor(out=z[:, j], in0=zpre[:, j], scalar=rs2[i][:, j:j + 1],
                                                  in1=c_b[:], op0=ALU.mult, op1=ALU.add)
                last.then_inc(z_ready, 1)
                s(v.tensor_tensor(biased[:], score[i][:], bc(bias_b[:], 1, [P, J, E]), ALU.add))
                b4 = biased[:].rearrange("p j (g a b) -> p (j g) a b", g=G, b=2)
                v.tensor_tensor(mx[:], b4[:, :, :, 0], b4[:, :, :, 1], ALU.max)
                s(v.tensor_tensor(mn[:], b4[:, :, :, 0], b4[:, :, :, 1], ALU.min))
                v.tensor_tensor(top1[:], mx[:, :, 0], mx[:, :, 1], ALU.max)
                v.tensor_tensor(m2[:], mx[:, :, 0], mx[:, :, 1], ALU.min)
                s(v.tensor_tensor(m3[:], mn[:, :, 0], mn[:, :, 1], ALU.max))
                s(v.tensor_tensor(m2[:], m2[:], m3[:], ALU.max))
                s(v.tensor_tensor(gs[:].rearrange("p j g -> p (j g)"), top1[:], m2[:], ALU.add), apart=True)
                for j in range(J):
                    last = v.max(g8[:, j], gs[:, j])
                s(last, apart=True)
                for j in range(J):
                    last = v.max_index(gi[:, j], g8[:, j], gs[:, j])
                s(last)
                s(v.tensor_copy(gif[:], gi[:]))
                for j in range(J):
                    last = v.tensor_tensor(gcmp[:, j], bc(iota_e[:, 0:G], 2, [P, G, TKG]),
                                           bc(gif[:, j, 0:TKG], 1, [P, G, TKG]), ALU.is_equal)
                s(last)
                s(v.tensor_reduce(gmask[:], gcmp[:], AX.X, ALU.add))
                s(v.tensor_tensor(masked[:].rearrange("p j (g a) -> p (j g) a", g=G),
                                  biased[:].rearrange("p j (g a) -> p (j g) a", g=G),
                                  bc(gmask[:].rearrange("p j g -> p (j g)"), 2, [P, J * G, EG]), ALU.mult),
                  apart=True)
                for j in range(J):
                    last = v.max(v8[:, j], masked[:, j])
                s(last, apart=True)
                for j in range(J):
                    last = v.max_index(i8[:, j], v8[:, j], masked[:, j])
                s(last)
                s(v.tensor_copy(i8f[:], i8[:]))
                s(v.tensor_tensor(oh[:], bc(iota_e[:], 1, [P, J * K, E]),
                                  bc(i8f[:].rearrange("p j k -> p (j k)"), 2, [P, J * K, E]), ALU.is_equal))
                with nc.allow_low_precision(reason="sums of one-hot rows are 0 or 1"):
                    v.tensor_reduce(sel[:], oh[:].rearrange("p (j k) e -> p j e k", j=J), AX.X, ALU.add)\
                        .then_inc(sel_ready, 1)
                for j in range(J):
                    last = v.tensor_tensor(prod[:, j * K:(j + 1) * K], oh[:, j * K:(j + 1) * K],
                                           bc(score[i][:, j], 1, [P, K, E]), ALU.mult)
                s(last)
                s(v.tensor_reduce(w8[:].rearrange("p j k -> p (j k)"), prod[:], AX.X, ALU.add))
                s(v.tensor_reduce(wsum[:], w8[:], AX.X, ALU.add))
                s(v.reciprocal(rinv[:], wsum[:]))
                s(v.tensor_tensor(w8[:], w8[:], bc(rinv[:], 2, [P, J, K]), ALU.mult))
                at = bass.ds(c * (J * K), J * K)
                v.tensor_scalar(payload[:, at, 1].bitcast(F32), w8[:].rearrange("p j k -> p (j k)"), ROUTED_SCALE,
                                None, ALU.mult)
                v.tensor_copy(payload[:, at, 0].rearrange("p (j k) -> p j k", j=J), bc(tid[:], 2, [P, J, K]))
                dve.wait_ge(rank_ready, c + 1)
                s(v.tensor_tensor(slotrow[:], rank[:, 0:J * E].rearrange("p (j e) -> p j e", j=J),
                                  bc(cnt_base[:], 1, [P, J, E]), ALU.add))
                v.tensor_tensor(cnt_base[:], rank[:, J * E:J * E + E], cnt_base[:], ALU.add)
                v.tensor_scalar(tid[:], tid[:], float(C), None, ALU.add).then_inc(rank_free, 1)
                for j in range(J):
                    last = v.tensor_tensor(prod[:, j * K:(j + 1) * K], oh[:, j * K:(j + 1) * K],
                                           bc(slotrow[:, j], 1, [P, K, E]), ALU.mult)
                s(last)
                s(v.tensor_reduce(slotf[:], prod[:], AX.X, ALU.add))
                dve.wait_ge(rank_free, c + 2)
                s(v.tensor_copy(slots[:, at], slotf[:]))
                assert s.n == RT, s.n

            norms(0, 0, 16, None)
            norms(1, 1, 16, None)
            route(0, 0)
            norms(2, 0, 32, 16)
            route(1, 1)
            with dve.Fori(1, NC // 2 - 1) as i:
                norms(i * 2 + 1, 1, i * 16 + 16, i * 16)
                route(i * 2, 0)
                norms(i * 2 + 2, 0, i * 16 + 32, i * 16 + 16)
                route(i * 2 + 1, 1)
            norms(NC - 1, 1, 8 * NC, 8 * NC - 16)
            route(NC - 2, 0)
            route(NC - 1, 1)
            dve.wait_ge(zp_free, NC + 1)
            for b in range(B + 1):
                at = (b * CPB + 1) * (C + 2)
                v.memset(zT[0:D, at - 1:at + 1], 0.0)


def scan_stage(nc, T, B, io):
    (base_d, out, zT, convw, convb, xpT, xpB, xpC, dtT, dtb, alog, dpar, opT) = io
    NC = T // C
    CPB = NC // B
    with ExitStack() as ctx:
        def sb(name, shape, dt=F32):
            return ctx.enter_context(nc.sbuf_tensor(name, shape, dt))

        def ring(name, shape, dt=F32):
            return [sb(f"{name}{i}", shape, dt) for i in range(2)]

        def pb(name, shape, dt=F32):
            return ctx.enter_context(nc.psum_tensor(name, shape, dt))

        def sem(name):
            return ctx.enter_context(nc.semaphore(name))

        cw = sb("cw", [D, 3])
        cb = sb("cb", [D, 1])
        w_dt = sb("w_dt", [D, R])
        w_B = sb("w_B", [D, P])
        w_C = sb("w_C", [D, P])
        w_dtp = sb("w_dtp", [R, D])
        b_dt = sb("b_dt", [D, 1])
        a_log = sb("a_log", [P, NG])
        a_exp = sb("a_exp", [P, NG])
        a_neg = sb("a_neg", [P, NG])
        dp = sb("dp", [D, 1])
        w_o = sb("w_o", [D, H])
        spread_f = sb("spread_f", [D, NG, P])
        spread = sb("spread", [D, NG, P], F32R)
        gather = sb("gather", [P, NG, D])
        conv = sb("conv", [D, C])
        u = ring("u", [D, C])
        dr = sb("dr", [R, C])
        Bs = ring("Bs", [P, C])
        Cs = ring("Cs", [P, C])
        pre = sb("pre", [D, C])
        ab = sb("ab", [D, C])
        ex = sb("ex", [D, C])
        ln = sb("ln", [D, C])
        ser = sb("ser", [D, C])
        small = sb("small", [D, C])
        delta = sb("delta", [D, C])
        du = sb("du", [D, C])
        d_hi = ring("d_hi", [D, C], F32R)
        d_lo = ring("d_lo", [D, C], F32R)
        du_hi = ring("du_hi", [D, C], F32R)
        du_lo = ring("du_lo", [D, C], F32R)
        dA = ring("dA", [P, C])
        dBu = ring("dBu", [P, C])
        hs = ring("hs", [P, C])
        hc = ring("hc", [P, C])
        state = sb("state", [P, NG])
        yT = sb("yT", [D, C])
        bs = [sb(f"base{i}", [P, H]) for i in range(J)]
        proj = pb("proj", [P, 512])
        rep_d = [pb(f"rep_d{i}", [P, 512]) for i in range(2)]
        rep_u = [pb(f"rep_u{i}", [P, 512]) for i in range(2)]
        yp = pb("yp", [P, 512])
        op = [pb(f"op{i}", [P, 512]) for i in range(2)]

        loaded = sem("loaded")
        dve_passed = sem("dve_passed")
        sp_passed = sem("sp_passed")
        consts = sem("consts")
        a_ready = sem("a_ready")
        conv_ready = sem("conv_ready")
        u_ready = sem("u_ready")
        proj_ready = sem("proj_ready")
        bc_ready = sem("bc_ready")
        pre_ready = sem("pre_ready")
        act_sp = sem("act_sp")
        delta_ready = sem("delta_ready")
        hi_ready = sem("hi_ready")
        parts_ready = sem("parts_ready")
        rep_ready = sem("rep_ready")
        dA_ready = sem("dA_ready")
        dBu_ready = sem("dBu_ready")
        scan_done = sem("scan_done")
        dA_free = sem("dA_free")
        hc_ready = sem("hc_ready")
        y_acc = sem("y_acc")
        y_ready = sem("y_ready")
        op_ready = sem("op_ready")
        op_free = sem("op_free")
        base_in = [sem(f"base_in{i}") for i in range(J)]
        base_out = sem("base_out")
        dve_step = sem("dve_step")
        tail_step = sem("tail_step")
        state_set = sem("state_set")

        block = ctx.enter_context(nc.Block())

        @block.sync
        def _(sp):
            for dst, src in ((cw, convw), (cb, convb), (w_dt, xpT), (w_B, xpB), (w_C, xpC), (w_dtp, dtT),
                             (b_dt, dtb), (a_log, alog), (dp, dpar), (w_o, opT)):
                sp.dma_start(dst[:], src).then_inc(loaded, 16)
            with sp.Fori(0, NC) as c:
                for j in range(J):
                    sp.dma_start(bs[j][:], base_d[bass.ds(c * C + j * P, P)]).then_inc(base_in[j], 16)
                for j in range(J):
                    sp.wait_ge(op_free, c * (2 * J) + 2 * j + 4)
                    sp.dma_start(out[bass.ds(c * C + j * P, P)], bs[j][:]).then_inc(base_out, 16)
                wait_apart(sp, sp_passed, base_out, c * (16 * J) + 16 * J)

        @block.gpsimd
        def _(pool):
            g = nc.gpsimd
            g.memset(spread_f[:], 1.0)
            g.memset(gather[:], 1.0).then_inc(consts, 1)
            pool.wait_ge(consts, 1)
            g.affine_select(out=spread_f[:], in_=spread_f[:], compare_op=ALU.is_ge, fill=0.0, base=0,
                            pattern=[[P, NG], [1, P]], channel_multiplier=-N)
            g.affine_select(out=gather[:], in_=gather[:], compare_op=ALU.is_ge, fill=0.0, base=0,
                            pattern=[[P, NG], [-N, D]], channel_multiplier=1).then_inc(consts, 1)
            pool.wait_ge(consts, 2)
            g.affine_select(out=spread_f[:], in_=spread_f[:], compare_op=ALU.is_ge, fill=0.0, base=N - 1,
                            pattern=[[-P, NG], [-1, P]], channel_multiplier=N)
            g.affine_select(out=gather[:], in_=gather[:], compare_op=ALU.is_ge, fill=0.0, base=N - 1,
                            pattern=[[-P, NG], [N, D]], channel_multiplier=-1).then_inc(consts, 1)
            pool.wait_ge(consts, 3)
            pool.sem_inc(hc_ready, 2)
            with pool.Fori(0, NC // 2) as i:
                for r in range(2):
                    for q in range(NG):
                        n = (i * 2 + r) * NG + q
                        pool.wait_ge(scan_done, n + 1)
                        pool.wait_ge(y_acc, n + 1)
                        g.tensor_tensor(hc[q % 2][:], hs[q % 2][:], Cs[r][:], ALU.mult).then_inc(hc_ready, 1)

        @block.scalar
        def _(act):
            a = nc.scalar

            def silu(n, r):
                act.wait_ge(conv_ready, n + 1)
                act.wait_ge(y_ready, n + 1)
                a.activation(u[r][:], conv[:], ACT.Silu, bias=cb[:]).then_inc(u_ready, 1)

            def projected(n, r):
                act.wait_ge(proj_ready, n * 2 + 1)
                a.activation(dr[:], proj[0:R], ACT.Copy)
                a.activation(Bs[r][:], op[0][:], ACT.Copy)
                a.activation(Cs[r][:], op[1][:], ACT.Copy).then_inc(bc_ready, 1)

            def logs(n):
                act.wait_ge(pre_ready, n + 1)
                a.activation(ab[:], pre[:], ACT.Abs).then_inc(act_sp, 1)
                act.wait_ge(act_sp, n * 3 + 1)
                a.activation(ex[:], ab[:], ACT.Exp, scale=-1.0).then_inc(act_sp, 1)
                act.wait_ge(act_sp, n * 3 + 2)
                a.activation(ln[:], ex[:], ACT.Ln, bias=1.0).then_inc(act_sp, 1)

            def highs(n, r):
                act.wait_ge(delta_ready, n + 1)
                a.activation(d_hi[r][:], delta[:], ACT.Copy)
                a.activation(du_hi[r][:], du[:], ACT.Copy).then_inc(hi_ready, 1)

            act.wait_ge(loaded, 160)
            a.activation(a_exp[:], a_log[:], ACT.Exp).then_inc(a_ready, 1)
            act.wait_ge(a_ready, 2)
            silu(0, 0)
            projected(0, 0)
            logs(0)
            highs(0, 0)
            with act.Fori(0, NC // 2) as i:
                for r in range(2):
                    c = i * 2 + r
                    for q in range(NG):
                        act.wait_ge(rep_ready, c * NG + q + 1)
                        act.wait_ge(dA_free, c * NG + q + 1)
                        a.activation(dA[q % 2][:], rep_d[q % 2][:], ACT.Exp, scale=a_neg[:, q:q + 1])\
                            .then_inc(dA_ready, 1)
                        if q == 4:
                            silu(c + 1, 1 - r)
                        if q == 6:
                            projected(c + 1, 1 - r)
                        if q == 9:
                            logs(c + 1)
                    highs(c + 1, 1 - r)

        @block.tensor
        def _(pe):
            m = nc.tensor.matmul
            pe.wait_ge(loaded, 160)
            pe.wait_ge(consts, 4)
            pe.sem_inc(y_acc, 2)

            def project(n, r):
                pe.wait_ge(u_ready, n + 1)
                pe.wait_ge(op_free, (n - 1) * (2 * J) + 2 if not isinstance(n, int) or n > 0 else 2)
                m(proj[0:R], w_dt[:], u[r][:], start=True, stop=True)
                m(op[0][:], w_B[:], u[r][:], start=True, stop=True)
                m(op[1][:], w_C[:], u[r][:], start=True, stop=True).then_inc(proj_ready, 1)

            def time_step(n):
                pe.wait_ge(bc_ready, n + 1)
                m(proj[0:D], w_dtp[:], dr[:], start=True, stop=True).then_inc(proj_ready, 1)

            def spread_to(c, r, q):
                n = c * NG + q
                pe.wait_ge(dA_ready, n + 1)
                pe.wait_ge(dBu_ready, n + 1)
                m(rep_d[q % 2][:], spread[:, q], d_hi[r][:], start=True, stop=False)
                m(rep_d[q % 2][:], spread[:, q], d_lo[r][:], start=False, stop=True)
                m(rep_u[q % 2][:], spread[:, q], du_hi[r][:], start=True, stop=False)
                m(rep_u[q % 2][:], spread[:, q], du_lo[r][:], start=False, stop=True).then_inc(rep_ready, 1)

            def out_tile(c, j):
                if j == 0:
                    pe.wait_ge(y_ready, c + 3)
                for h in range(2):
                    pe.wait_ge(op_free, c * (2 * J) + 2 * j + h + 1)
                    m(op[h][:], yT[:, j * P:(j + 1) * P], w_o[:, h * 512:(h + 1) * 512], start=True,
                      stop=True).then_inc(op_ready, 1)

            def body(c, r, first=False):
                for q in range(NG):
                    pe.wait_ge(hc_ready, c * NG + q + 3)
                    if q == 0 and not first:
                        pe.wait_ge(y_ready, c + 2)
                    m(yp[0:D], gather[:, q], hc[q % 2][:], start=q == 0, stop=q == NG - 1).then_inc(y_acc, 1)
                    if q + 2 < NG:
                        spread_to(c, r, q + 2)
                    if 1 <= q <= J and not first:
                        out_tile(c - 1, q - 1)
                    if q == 5:
                        project(c + 1, 1 - r)
                    if q == 7:
                        time_step(c + 1)
                pe.wait_ge(parts_ready, c + 2)
                spread_to(c + 1, 1 - r, 0)
                spread_to(c + 1, 1 - r, 1)

            project(0, 0)
            time_step(0)
            pe.wait_ge(parts_ready, 1)
            spread_to(0, 0, 0)
            spread_to(0, 0, 1)
            body(0, 0, True)
            body(1, 1)
            with pe.Fori(1, NC // 2) as i:
                for r in range(2):
                    body(i * 2 + r, r)
            for j in range(J):
                out_tile(NC - 1, j)

        @block.vector
        def _(dve):
            v = nc.vector
            dve.wait_ge(consts, 3)
            v.tensor_copy(spread[:], spread_f[:]).then_inc(consts, 1)
            dve.wait_ge(a_ready, 1)
            v.tensor_scalar(a_neg[:], a_exp[:], -1.0, None, ALU.mult).then_inc(a_ready, 1)
            dve.wait_ge(loaded, 160)
            dve.sem_inc(dBu_ready, 2)
            dve.sem_inc(dA_ready, 2)
            dve.sem_inc(op_free, 2)
            dve.sem_inc(dA_free, 2)
            dve.sem_inc(y_ready, 2)
            ST = 11

            def convolve(n, wait=True):
                s = Steps(dve, dve_step, n * ST)
                at = (n + 1) * (C + 2)
                if wait:
                    dve.wait_ge(u_ready, n)
                s(v.tensor_scalar(conv[:], zT[0:D, bass.ds(at, C)], cw[:, 0:1], None, ALU.mult))
                s(v.scalar_tensor_tensor(out=conv[:], in0=zT[0:D, bass.ds(at + 1, C)], scalar=cw[:, 1:2],
                                         in1=conv[:], op0=ALU.mult, op1=ALU.add))
                v.scalar_tensor_tensor(out=conv[:], in0=zT[0:D, bass.ds(at + 2, C)], scalar=cw[:, 2:3],
                                       in1=conv[:], op0=ALU.mult, op1=ALU.add).then_inc(conv_ready, 1)

            def bias_dt(n):
                dve.wait_ge(proj_ready, n * 2 + 2)
                v.tensor_scalar(pre[:], proj[0:D], b_dt[:], None, ALU.add).then_inc(pre_ready, 1)

            def softplus(n, r):
                s = Steps(dve, dve_step, n * ST + 2)
                dve.wait_ge(act_sp, n * 3 + 3)
                v.tensor_scalar(small[:], ex[:], 2.0 ** -5, None, ALU.is_lt)
                s(v.tensor_scalar(ser[:], ex[:], -0.25, 1.0 / 3.0, ALU.mult, ALU.add))
                s(v.tensor_tensor(ser[:], ser[:], ex[:], ALU.mult))
                s(v.scalar_tensor_tensor(out=ser[:], in0=ser[:], scalar=-0.5, in1=ex[:], op0=ALU.add,
                                         op1=ALU.mult))
                s(v.scalar_tensor_tensor(out=ser[:], in0=ser[:], scalar=1.0, in1=ex[:], op0=ALU.add,
                                         op1=ALU.mult))
                s(v.tensor_tensor(ser[:], ser[:], ln[:], ALU.subtract))
                s(v.tensor_tensor(ser[:], ser[:], small[:], ALU.mult))
                s(v.tensor_tensor(ser[:], ser[:], ln[:], ALU.add))
                s(v.scalar_tensor_tensor(out=ser[:], in0=pre[:], scalar=0.0, in1=ser[:], op0=ALU.max,
                                         op1=ALU.add))
                s(v.tensor_scalar(delta[:], ser[:], 0.001, None, ALU.mult))
                v.tensor_tensor(du[:], delta[:], u[r][:], ALU.mult).then_inc(delta_ready, 1)
                assert s.n + 2 == ST, s.n

            def lows(n, r):
                dve.wait_ge(hi_ready, n + 1)
                v.tensor_tensor(d_lo[r][:], delta[:], d_hi[r][:], ALU.subtract)
                v.tensor_tensor(du_lo[r][:], du[:], du_hi[r][:], ALU.subtract).then_inc(parts_ready, 1)

            def tail(c, r):
                dve.wait_ge(y_acc, c * NG + NG + 2)
                v.scalar_tensor_tensor(out=yT[:], in0=u[r][:], scalar=dp[:], in1=yp[0:D], op0=ALU.mult,
                                       op1=ALU.add).then_inc(y_ready, 1)

            def add_tile(c, j):
                dve.wait_ge(base_in[j], c * 16 + 16)
                for h in range(2):
                    dve.wait_ge(op_ready, c * (2 * J) + 2 * j + h + 1)
                    v.tensor_tensor(bs[j][:, h * 512:(h + 1) * 512], op[h][:],
                                    bs[j][:, h * 512:(h + 1) * 512], ALU.add).then_inc(op_free, 1)

            def body(c, r, first=False):
                for q in range(NG):
                    n = c * NG + q
                    dve.wait_ge(rep_ready, n + 1)
                    v.tensor_tensor(dBu[q % 2][:], rep_u[q % 2][:], Bs[r][:], ALU.mult).then_inc(dBu_ready, 1)
                    dve.wait_ge(dBu_ready, n + 3)
                    dve.wait_ge(dA_ready, n + 3)
                    dve.wait_ge(hc_ready, n + 1)
                    v.tensor_tensor_scan(hs[q % 2][:], dA[q % 2][:], dBu[q % 2][:], state[:, q:q + 1],
                                         ALU.mult, ALU.add).then_inc(scan_done, 1)
                    dve.wait_ge(scan_done, n + 1)
                    v.tensor_copy(state[:, q:q + 1], hs[q % 2][:, C - 1:C]).then_inc(dA_free, 1)
                    if q == 0 and not first:
                        tail(c - 1, 1 - r)
                    if 2 <= q <= J + 1 and not first:
                        add_tile(c - 1, q - 2)
                    if q == 3:
                        convolve(c + 1)
                    if q == 8:
                        bias_dt(c + 1)
                    if q == 10:
                        softplus(c + 1, 1 - r)
                lows(c + 1, 1 - r)

            v.memset(state[:], 0.0).then_inc(state_set, 1)
            convolve(0, False)
            bias_dt(0)
            dve.wait_ge(bc_ready, 1)
            softplus(0, 0)
            lows(0, 0)
            dve.wait_ge(state_set, 1)
            body(0, 0, True)
            body(1, 1)
            with dve.Fori(1, CPB // 2) as i:
                for r in range(2):
                    body(i * 2 + r, r)
            with dve.Fori(1, B) as b:
                dve.wait_ge(dA_free, b * (CPB * NG) + 2)
                v.memset(state[:], 0.0).then_inc(state_set, 1)
                wait_apart(dve, dve_passed, state_set, b + 1)
                with dve.Fori(0, CPB // 2) as i:
                    for r in range(2):
                        body(b * CPB + i * 2 + r, r)
            tail(NC - 1, 1)
            for j in range(J):
                add_tile(NC - 1, j)


def plan_stage(nc, T, cnt_base, plan):
    starts, experts, fresh, runs, wide, total = plan
    NSH = SH * T // C
    NR = T * K // C + E - 1
    NB = NSH + NR
    PAD = (E + SH) * T
    with ExitStack() as ctx:
        def sb(name, shape, dt=F32):
            return ctx.enter_context(nc.sbuf_tensor(name, shape, dt))

        reg_i = sb("reg_i", [1, E], I32)
        blk_i = sb("blk_i", [1, NR], I32)
        reg_f = sb("reg_f", [1, E])
        blk = sb("blk", [1, NR])
        cnt = sb("cnt", [1, E])
        cnt_int = sb("cnt_int", [1, E], I32)
        nblk = sb("nblk", [1, E])
        one = sb("one", [1, E])
        cum = sb("cum", [1, E])
        before = sb("before", [1, NR, E])
        eid = sb("eid", [1, NR])
        first = sb("first", [1, NR])
        start = sb("start", [1, NR])
        idle = sb("idle", [1, NR])
        some = sb("some", [1, NR, E])
        steps_ = sb("steps_", [1, E])
        taken = sb("taken", [1, NR])
        wide_f = sb("wide_f", [1, NR])
        exp_f = sb("exp_f", [1, NB + 1])
        fresh_f = sb("fresh_f", [1, NB + 1])
        runs_f = sb("runs_f", [1, NB + 1])
        ones_r = sb("ones_r", [1, NB + 1])
        made = ctx.enter_context(nc.semaphore("made"))
        done = ctx.enter_context(nc.semaphore("done"))
        block = ctx.enter_context(nc.Block())

        @block.gpsimd
        def _(pool):
            g = nc.gpsimd
            g.iota(reg_i[:], pattern=[[T, E]], base=0, channel_multiplier=0)
            g.iota(blk_i[:], pattern=[[1, NR]], base=0, channel_multiplier=0)
            g.iota(starts[:, 0:NSH], pattern=[[C, NSH]], base=E * T, channel_multiplier=0)
            g.iota(starts[:, NSH + NR:NSH + NR + 1], pattern=[[0, 1]], base=PAD, channel_multiplier=0)
            g.iota(experts[:, NSH + NR:NSH + NR + 1], pattern=[[0, 1]], base=E - 1, channel_multiplier=0)
            g.iota(experts[:, 0:NSH].rearrange("p (a b) -> p a b", a=SH), pattern=[[1, SH], [0, T // C]],
                   base=E, channel_multiplier=0).then_inc(made, 1)

        @block.vector
        def _(dve):
            v = nc.vector
            s = Steps(dve, done)
            dve.wait_ge(made, 1)
            v.memset(one[:], 1.0)
            v.tensor_copy(reg_f[:], reg_i[:])
            s(v.tensor_copy(blk[:], blk_i[:]))
            s(v.tensor_tensor(cnt[:], cnt_base[0:1], reg_f[:], ALU.subtract))
            s(v.tensor_scalar(cnt_int[:], cnt[:], float(C - 1), None, ALU.add))
            s(v.tensor_scalar(cnt_int[:], cnt_int[:], C.bit_length() - 1, None, ALU.logical_shift_right))
            s(v.tensor_copy(nblk[:], cnt_int[:]))
            s(v.tensor_tensor_scan(cum[:], one[:], nblk[:], 0.0, ALU.mult, ALU.add))
            s(v.tensor_tensor(before[:], bc(blk[:], 2, [1, NR, E]), bc(cum[:], 1, [1, NR, E]), ALU.is_ge))
            s(v.tensor_reduce(eid[:], before[:], AX.X, ALU.add))
            v.tensor_tensor(steps_[:, 0:E - 1], cnt[:, 1:E], cnt[:, 0:E - 1], ALU.subtract)
            s(v.tensor_scalar(steps_[:, E - 1:E], cnt[:, E - 1:E], -1.0, None, ALU.mult))
            s(v.tensor_tensor(some[:], before[:], bc(steps_[:], 1, [1, NR, E]), ALU.mult))
            s(v.tensor_reduce(taken[:], some[:], AX.X, ALU.add))
            s(v.tensor_scalar(taken[:], taken[:], cnt[:, 0:1], None, ALU.add))
            s(v.tensor_tensor(before[:], before[:], bc(nblk[:], 1, [1, NR, E]), ALU.mult))
            s(v.tensor_reduce(first[:], before[:], AX.X, ALU.add))
            s(v.tensor_tensor(first[:], blk[:], first[:], ALU.subtract))
            s(v.scalar_tensor_tensor(out=taken[:], in0=first[:], scalar=-float(C), in1=taken[:], op0=ALU.mult,
                                     op1=ALU.add))
            v.memset(wide[:, 0:NSH], 1)
            v.memset(wide[:, NB:NB + 1], 0)
            v.tensor_scalar(wide_f[:], taken[:], C / 2 + 0.5, None, ALU.is_ge)
            s(v.tensor_scalar(cnt[:, 0:1], cum[:, E - 1:E], float(NSH), None, ALU.add))
            v.tensor_copy(wide[:, NSH:NB], wide_f[:])
            v.tensor_copy(total[:], cnt[:, 0:1])
            v.tensor_scalar(idle[:], eid[:], float(E), None, ALU.is_ge)
            s(v.tensor_scalar(start[:], eid[:], float(T), None, ALU.mult))
            s(v.scalar_tensor_tensor(out=start[:], in0=first[:], scalar=float(C), in1=start[:], op0=ALU.mult,
                                     op1=ALU.add))
            s(v.tensor_scalar(first[:], start[:], -1.0, float(PAD), ALU.mult, ALU.add))
            s(v.tensor_tensor(first[:], first[:], idle[:], ALU.mult))
            s(v.tensor_tensor(starts[:, NSH:NSH + NR], start[:], first[:], ALU.add))
            s(v.tensor_scalar(experts[:, NSH:NSH + NR], eid[:], float(E - 1), None, ALU.min))
            v.memset(ones_r[:], 1.0)
            v.memset(fresh_f[:, 0:1], 1.0)
            s(v.tensor_copy(exp_f[:], experts[:]))
            s(v.tensor_tensor(fresh_f[:, 1:NB + 1], exp_f[:, 1:NB + 1], exp_f[:, 0:NB], ALU.not_equal))
            s(v.tensor_tensor_scan(runs_f[:], ones_r[:], fresh_f[:], -1.0, ALU.mult, ALU.add))
            v.tensor_copy(fresh[:], fresh_f[:])
            s(v.tensor_copy(runs[:], runs_f[:]))


def expert_stage(nc, T, io, plan):
    (xn_d, out, table, w_all, slots, payload) = io
    starts, experts, fresh, runs, wide, total = plan
    NSH = SH * T // C
    NSC = T // P * K // NSH
    NB = SH * T // C + T * K // C + E - 1
    with ExitStack() as ctx:
        def sb(name, shape, dt=F32):
            return ctx.enter_context(nc.sbuf_tensor(name, shape, dt))

        def pb(name, shape, dt=F32):
            return ctx.enter_context(nc.psum_tensor(name, shape, dt))

        def sem(name):
            return ctx.enter_context(nc.semaphore(name))

        stage = [sb(f"stage{i}", [P, WC]) for i in range(NST)]
        w_hi = [sb(f"w_hi{q}", [P, WC], F32R) for q in range(NCH)]
        w_lo = [sb(f"w_lo{q}", [P, WC], F32R) for q in range(NCH)]
        xraw = sb("xraw", [P, J, H])
        x_hi = sb("x_hi", [P, KH, C], F32R)
        x_lo = sb("x_lo", [P, KH, C], F32R)
        a_hi = sb("a_hi", [P, KI, C], F32R)
        a_lo = sb("a_lo", [P, KI, C], F32R)
        sg = sb("sg", [P, C])
        av = sb("av", [P, C])
        y = sb("y", [P, 2, H])
        slot_cur = sb("slot_cur", [P, NSC], U32)
        payload_cur = sb("payload_cur", [P, NSC, 2], I32)
        idx_in = sb("idx_in", [P, J, 2], I32)
        idx_cur = sb("idx_cur", [P, J, 2], I32)
        ident = sb("ident2", [P, P])
        pg = [pb(f"pg{i}", [P, C]) for i in range(2)]
        pu = [pb(f"pu{i}", [P, C]) for i in range(2)]
        tp = [pb(f"tx{i}", [P, J, P]) for i in range(2)]
        pd = [pb(f"pd{i}", [P, 512]) for i in range(2)]

        made = sem("ident_made")
        pool_passed = sem("pool_passed")
        sp_passed = sem("sp_passed")
        act_passed = sem("act_passed")
        dve_passed = sem("dve_passed")
        pe_passed = sem("pe_passed")
        staged = [sem(f"staged{i}") for i in range(NST)]
        split_hi = sem("split_hi")
        split = sem("split")
        idx_loaded = sem("idx_loaded")
        idx_copied = sem("idx_copied")
        gathered = sem("gathered")
        tp_ready = sem("tx_ready")
        xh_ready = sem("xh_ready")
        xT_ready = sem("xT_ready")
        gu_ready = sem("gu_ready")
        gate_read = sem("gate_read")
        up_read = sem("up_read")
        ah_ready = sem("ah_ready")
        a_ready = sem("act_ready")
        a_used = sem("a_used")
        down_ready = sem("down_ready")
        down_read = sem("down_read")
        added = sem("added")
        y_free = sem("y_free")
        columns_ready = sem("columns_ready")
        scattered = sem("scattered")

        block = ctx.enter_context(nc.Block())

        @block.sync
        def _(sp):
            def load(e, q, s):
                sp.wait_ge(split, s)
                sp.dma_start(stage[q % NST][:], w_all[bass.ds(e * NCH + q, 1)]
                             .rearrange("a p c -> (a p) c")).then_inc(staged[q % NST], 16)

            def value(row, b, top):
                return sp.value_load(row[0:1, bass.ds(b, 1)], min_val=0, max_val=top)

            n_blocks = value(total, 0, NB)
            e = value(experts, 0, E + SH - 1)
            for q in range(4):
                load(e, q, q + 1)
            with sp.Fori(0, NB) as b:
                with sp.If(b < n_blocks):
                    with sp.If(value(fresh, b, 1) > 0):
                        e = value(experts, b, E + SH - 1)
                        for q in (4, 5):
                            load(e, q, b * NCH + q + 1)
                    with sp.Else():
                        sp.sem_inc(sp_passed, 1)
                    with sp.If(value(fresh, b + 1, 1) > 0):
                        e = value(experts, b + 1, E + SH - 1)
                        for q in range(4):
                            load(e, q, b * NCH + NCH + q + 1)
                    with sp.Else():
                        sp.sem_inc(sp_passed, 1)
                    sp.sem_inc(sp_passed, 1)
                with sp.Else():
                    sp.sem_inc(sp_passed, 1)

        @block.gpsimd
        def _(pool):
            g = nc.gpsimd
            g.memset(ident[:], 0.0).then_inc(made, 1)
            pool.wait_ge(made, 1)
            g.affine_select(out=ident[:], in_=ident[:], compare_op=ALU.not_equal, fill=1.0, base=0,
                            pattern=[[-1, P]], channel_multiplier=1).then_inc(made, 1)
            pool.sem_inc(y_free, 2)

            n_blocks = pool.value_load(total[0:1, 0:1], min_val=NSH, max_val=NB)

            def gather(b, n):
                first = pool.value_load(starts[0:1, bass.ds(b, 1)], min_val=0, max_val=(E + SH) * T)
                g.dma_start(idx_in[:].rearrange("p (h j) w -> p h (j w)", h=2),
                            table[bass.ds(first, C)].rearrange("(h p j) w -> p h (j w)", h=2, p=P))\
                    .then_inc(idx_loaded, 16)
                wait_apart(pool, pool_passed, idx_loaded, n * 16)
                for j in range(J):
                    g.indirect_dma_start(out=xraw[:, j], out_offset=None, in_=xn_d,
                                         in_offset=bass.IndirectOffsetOnAxis(ap=idx_in[:, j, 0:1], axis=0))\
                        .then_inc(gathered, 16)

            def next_rows(b):
                pool.wait_ge(idx_copied, b + 1)
                pool.wait_ge(tp_ready, b * KH + KH)
                gather(b + 1, b + 2)

            def scatter(b):
                g.tensor_copy(slot_cur[:], slots[:, bass.ds(b * NSC, NSC)])
                g.tensor_copy(payload_cur[:], payload[:, bass.ds(b * NSC, NSC)]).then_inc(columns_ready, 1)
                wait_apart(pool, pool_passed, columns_ready, b + 1)
                for j in range(NSC):
                    g.indirect_dma_start(
                        out=table, out_offset=bass.IndirectOffsetOnAxis(ap=slot_cur[:, j:j + 1], axis=0),
                        in_=payload_cur[:, j], in_offset=None).then_inc(scattered, 16)

            def adds(b):
                for j in range(J):
                    wait_apart(pool, pool_passed, down_read, b * (2 * J) + 2 * j + 4)
                    g.indirect_dma_start(out=out, out_offset=bass.IndirectOffsetOnAxis(ap=idx_cur[:, j, 0:1], axis=0),
                                         in_=y[:, j % 2], in_offset=None, compute_op=ALU.add).then_inc(added, 16)
                    pool.wait_ge(added, b * (16 * J) + 16 * j + 16)
                    pool.sem_inc(y_free, 1)

            gather(0, 1)
            with pool.Fori(0, NSH - 1) as b:
                next_rows(b)
                scatter(b)
                adds(b)
                pool.wait_ge(scattered, b * (16 * NSC) + 16 * NSC)
                pool.sem_inc(pool_passed, 1)
            scatter(NSH - 1)
            pool.wait_ge(scattered, NSH * (16 * NSC))
            next_rows(NSH - 1)
            adds(NSH - 1)
            with pool.Fori(NSH, NB) as b:
                with pool.If(b < n_blocks):
                    next_rows(b)
                    adds(b)
                with pool.Else():
                    pool.sem_inc(pool_passed, 1)

        @block.scalar
        def _(act):
            a = nc.scalar
            act.sem_inc(gate_read, 2)

            def high(q, n):
                act.wait_ge(staged[q % NST], n)
                a.activation(w_hi[q][:], stage[q % NST][:], ACT.Copy).then_inc(split_hi, 1)

            def x_high(k, n):
                act.wait_ge(tp_ready, n + k + 1)
                a.activation(x_hi[:, k], tp[k % 2][:].rearrange("p j c -> p (j c)"), ACT.Copy)\
                    .then_inc(xh_ready, 1)

            for q in range(4):
                high(q, 16 * (q // NST + 1))
            for k in range(KH):
                x_high(k, 0)
            n_blocks = act.value_load(total[0:1, 0:1], min_val=NSH, max_val=NB)

            def hidden(b, i):
                act.wait_ge(gu_ready, b * KI + i + 1)
                act.wait_ge(up_read, b * KI + i + 1)
                a.activation(sg[:], pg[i % 2][:], ACT.Silu).then_inc(gate_read, 1)
                act.wait_ge(up_read, b * KI + i + 2)
                a.activation(a_hi[:, i], av[:], ACT.Copy).then_inc(ah_ready, 1)

            with act.Fori(0, NB) as b:
                with act.If(b < n_blocks):
                    act.wait_ge(down_ready, b * KH + KH)
                    with act.If(act.value_load(fresh[0:1, bass.ds(b, 1)], min_val=0, max_val=1) > 0):
                        run = act.value_load(runs[0:1, bass.ds(b, 1)], min_val=0, max_val=NB)
                        for q in (4, 5):
                            high(q, run * 32 + 32)
                    with act.Else():
                        act.sem_inc(split_hi, 2)
                    with act.If(act.value_load(fresh[0:1, bass.ds(b + 1, 1)], min_val=0, max_val=1) > 0):
                        run = act.value_load(runs[0:1, bass.ds(b + 1, 1)], min_val=1, max_val=NB)
                        for i in range(KI):
                            hidden(b, i)
                            high(i, run * 32 + 16 * (i // NST) + 16)
                    with act.Else():
                        for i in range(KI):
                            hidden(b, i)
                        act.sem_inc(split_hi, KI)
                    for k in range(KH):
                        x_high(k, b * KH + KH)
                with act.Else():
                    act.sem_inc(act_passed, 1)

        @block.vector
        def _(dve):
            v = nc.vector
            dve.sem_inc(up_read, 1)
            dve.sem_inc(split, NST)
            dve.sem_inc(down_read, 2)
            dve.sem_inc(a_ready, 1)

            def low(q, s):
                dve.wait_ge(split_hi, s)
                v.tensor_tensor(w_lo[q][:], stage[q % NST][:], w_hi[q][:], ALU.subtract).then_inc(split, 1)

            def x_low(k, n):
                dve.wait_ge(xh_ready, n + k + 1)
                v.tensor_tensor(x_lo[:, k], tp[k % 2][:].rearrange("p j c -> p (j c)"), x_hi[:, k], ALU.subtract)\
                    .then_inc(xT_ready, 1)

            for q in range(4):
                low(q, q + 1)
            for k in range(KH):
                x_low(k, 0)
            n_blocks = dve.value_load(total[0:1, 0:1], min_val=NSH, max_val=NB)

            def hidden(b, i):
                dve.wait_ge(gate_read, b * KI + i + 3)
                dve.wait_ge(a_ready, b * KI + i + 1)
                v.tensor_tensor(av[:], pu[i % 2][:], sg[:], ALU.mult).then_inc(up_read, 1)
                dve.wait_ge(ah_ready, b * KI + i + 1)
                v.tensor_tensor(a_lo[:, i], av[:], a_hi[:, i], ALU.subtract).then_inc(a_ready, 1)

            with dve.Fori(0, NB) as b:
                with dve.If(b < n_blocks):
                    dve.wait_ge(idx_loaded, b * 16 + 16)
                    dve.wait_ge(y_free, b * J + 2)
                    v.tensor_copy(idx_cur[:], idx_in[:]).then_inc(idx_copied, 1)
                    wait_apart(dve, dve_passed, idx_copied, b + 1)
                    with dve.If(dve.value_load(fresh[0:1, bass.ds(b, 1)], min_val=0, max_val=1) > 0):
                        for q in (4, 5):
                            low(q, b * NCH + q + 1)
                    with dve.Else():
                        dve.sem_inc(split, 2)
                    with dve.If(dve.value_load(fresh[0:1, bass.ds(b + 1, 1)], min_val=0, max_val=1) > 0):
                        for i in range(KI):
                            hidden(b, i)
                            low(i, b * NCH + NCH + i + 1)
                    with dve.Else():
                        for i in range(KI):
                            hidden(b, i)
                        dve.sem_inc(split, KI)
                    for k in range(KH):
                        x_low(k, b * KH + KH)
                        j, h = k // 2, k % 2
                        dve.wait_ge(down_ready, b * KH + KH + k + 1)
                        if h == 0:
                            dve.wait_ge(y_free, b * J + j + 1)
                        v.tensor_scalar(y[:, j % 2, h * 512:(h + 1) * 512], pd[k % 2][:],
                                        idx_cur[:, j, 1:2].bitcast(F32), None, ALU.mult).then_inc(down_read, 1)
                with dve.Else():
                    dve.sem_inc(dve_passed, 1)

        @block.tensor
        def _(pe):
            m = nc.tensor.matmul
            pe.sem_inc(down_ready, KH)
            pe.wait_ge(made, 2)

            def transposes(k, n):
                pe.wait_ge(xT_ready, n + k - 1) if not (isinstance(n, int) and n + k < 2) else None
                for j in range(J):
                    last = nc.tensor.transpose(tp[k % 2][:, j], xraw[:, j, k * P:(k + 1) * P], ident[:])
                last.then_inc(tp_ready, 1)

            def product(dst, w, cols, x, xs, first, last):
                hi, lo = w
                m(dst, hi[:, cols], x[0][xs], start=first, stop=False)
                m(dst, hi[:, cols], x[1][xs], start=False, stop=False)
                return m(dst, lo[:, cols], x[0][xs], start=False, stop=last)

            pe.wait_ge(gathered, 16 * J)
            for k in range(KH):
                transposes(k, 0)
            n_blocks = pe.value_load(total[0:1, 0:1], min_val=NSH, max_val=NB)

            def block_of(b, cols, groups):
                pe.wait_ge(xT_ready, b * KH + KH)
                for i in range(KI):
                    pe.wait_ge(split, b * NCH + i + 1 + NST)
                    pe.wait_ge(gate_read, b * KI + i + 1)
                    if i:
                        pe.wait_ge(up_read, b * KI + i)
                    for half, dst in ((0, pg[i % 2]), (1, pu[i % 2])):
                        for k in range(KH):
                            c0 = half * 1024 + k * P
                            last = product(dst[:, 0:cols], (w_hi[i], w_lo[i]), slice(c0, c0 + P), (x_hi, x_lo),
                                           (slice(None), k, slice(0, cols)), k == 0, k == KH - 1)
                    last.then_inc(gu_ready, 1)

                def down(k, ks):
                    j, h = k // 2, k % 2
                    for i in ks:
                        for part, (wa, wb) in enumerate(((a_hi, w_hi), (a_hi, w_lo), (a_lo, w_hi))):
                            last = m(pd[k % 2][:], wa[:, i, j * P:(j + 1) * P], wb[4 + h][:, i * 512:(i + 1) * 512],
                                     start=i == 0 and part == 0, stop=i == KI - 1 and part == 2)
                    return last

                pe.wait_ge(gathered, b * (16 * J) + 32 * J)
                pe.wait_ge(split, b * NCH + NCH + NST)
                transposes(0, b * KH + KH)
                transposes(1, b * KH + KH)
                pe.wait_ge(down_read, b * KH + 1)
                pe.wait_ge(a_ready, b * KI + KI)
                down(0, range(KI - 1))
                pe.wait_ge(down_read, b * KH + 2)
                down(1, range(KI - 1))
                pe.wait_ge(a_ready, b * KI + KI + 1)
                down(0, (KI - 1,)).then_inc(down_ready, 1)
                down(1, (KI - 1,)).then_inc(down_ready, 1)
                for k in range(2, KH):
                    transposes(k, b * KH + KH)
                    if k < groups:
                        pe.wait_ge(down_read, b * KH + k + 1)
                        down(k, range(KI)).then_inc(down_ready, 1)
                    else:
                        if k == groups:
                            pe.wait_ge(down_ready, b * KH + KH + k)
                        pe.sem_inc(down_ready, 1)

            with pe.Fori(0, NB) as b:
                with pe.If(b < n_blocks):
                    with pe.If(pe.value_load(wide[0:1, bass.ds(b, 1)], min_val=0, max_val=1) > 0):
                        block_of(b, C, KH)
                    with pe.Else():
                        block_of(b, C // 2, KH // 2)
                    pe.sem_inc(pe_passed, 1)
                with pe.Else():
                    pe.sem_inc(pe_passed, 1)


def build(nc, A, T, B):
    rows = (E + SH) * T + C
    NB = SH * T // C + T * K // C + E - 1
    xn_d = nc.dram_tensor("xn_rows", [T + P, H], F32, kind="Internal").ap()
    base_d = nc.dram_tensor("base_rows", [T, H], F32, kind="Internal").ap()
    table = nc.dram_tensor("slot_table", [rows, 2], I32, kind="Internal").ap()
    with ExitStack() as ctx:
        def sb(name, shape, dt):
            return ctx.enter_context(nc.sbuf_tensor(name, shape, dt))

        slots = sb("slots", [P, T // P * K], U32)
        payload = sb("payload", [P, T // P * K, 2], I32)
        plan = [sb(name, [1, NB + 1], I32) for name in ("starts", "experts", "fresh", "runs", "wide")]
        plan.append(sb("total", [1, 1], I32))
        with ExitStack() as part:
            cnt_base = part.enter_context(nc.sbuf_tensor("cnt_base", [P, E], F32))
            zT = part.enter_context(nc.sbuf_tensor("zT", [P, (T // C + 2) * (C + 2)], F32))
            route_stage(nc, T, B, (A["x"], xn_d, base_d, A["out"], table, A["rw"], A["ipw"], A["lnw"], A["lnb"],
                                   A["rbias"], zT, cnt_base, slots, payload))
            scan_stage(nc, T, B, (base_d, A["out"], zT, A["convw"], A["convb"], A["xpT"], A["xpB"], A["xpC"],
                                  A["dtT"], A["dtb"], A["alog"], A["dpar"], A["opT"]))
            plan_stage(nc, T, cnt_base, plan)
        expert_stage(nc, T, (xn_d, A["out"], table, A["w_all"], slots, payload), plan)


def layouts(x, ln_w, ln_b, in_proj_W, conv_w, conv_b, x_proj_W, dt_proj_W, dt_proj_b, A_log, D_param, out_proj_W,
            router_w, router_bias, w_gate, w_up, w_down, sw_gate, sw_up, sw_down):
    import numpy as np

    def halves(w):
        return w.reshape(H, SH, I).transpose(1, 0, 2)

    gate = np.concatenate([w_gate, halves(sw_gate)])
    up = np.concatenate([w_up, halves(sw_up)])
    down = np.concatenate([w_down, sw_down.reshape(SH, I, H)])
    n = E + SH
    gu = np.stack([gate, up]).reshape(2, n, KH, P, KI, P).transpose(1, 4, 3, 0, 2, 5).reshape(n, KI, P, WC)
    dn = down.reshape(n, KI, P, 2, 512).transpose(0, 3, 2, 1, 4).reshape(n, 2, P, WC)
    T = x.shape[0] * x.shape[1]
    return {
        "x": x.reshape(T, H), "rw": router_w, "ipw": in_proj_W.T, "lnw": ln_w.reshape(KH, P).T,
        "lnb": ln_b.reshape(KH, P).T, "rbias": router_bias, "convw": conv_w.reshape(D, 3),
        "convb": conv_b.reshape(D, 1), "xpT": x_proj_W[:R].T, "xpB": np.tile(x_proj_W[R:R + N].T, (1, PG)),
        "xpC": np.tile(x_proj_W[R + N:].T, (1, PG)), "dtT": dt_proj_W.T, "dtb": dt_proj_b.reshape(D, 1),
        "alog": A_log.reshape(NG, P).T, "dpar": D_param.reshape(D, 1), "opT": out_proj_W.T,
        "w_all": np.concatenate([gu, dn], axis=1).reshape(n * NCH, P, WC),
    }


def kernel(**inputs):
    import numpy as np
    import concourse.bacc as bacc
    from concourse import mybir as _mybir
    from concourse.bass_utils import run_bass_kernel_spmd

    names = {k.replace("L0_attn_feat_patch", "x").replace("L0_attn_", "").replace("L0_ffn_", ""): np.asarray(v)
             for k, v in inputs.items()}
    arrays = {k: np.ascontiguousarray(v) for k, v in layouts(**names).items()}
    B, L = names["x"].shape[:2]
    T = B * L
    nc = bacc.Bacc("TRN2", target_bir_lowering=False, num_devices=1)
    A = {k: nc.dram_tensor(f"in_{k}", v.shape, _mybir.dt.from_np(v.dtype), kind="ExternalInput").ap()
         for k, v in arrays.items()}
    A["out"] = nc.dram_tensor("out_rows", [T + P, H], F32, kind="ExternalOutput").ap()
    build(nc, A, T, B)
    r = run_bass_kernel_spmd(nc, [{f"in_{k}": v for k, v in arrays.items()}], core_ids=[0])
    return r.results[0]["out_rows"][:T].reshape(B, L, H)
```

```python
import concourse.bass as bass
from concourse import mybir
from contextlib import ExitStack

F32 = mybir.dt.float32
F32R = mybir.dt.float32r
BF16 = mybir.dt.bfloat16
I32 = mybir.dt.int32
U32 = mybir.dt.uint32
ALU = mybir.AluOpType
ACT = mybir.ActivationFunctionType
AX = mybir.AxisListType

P = 128
H = 1024
KH = H // P
E, G, TKG, K = 32, 8, 4, 8
EG = E // G
I = 512
KI = I // P
SH = 2
D, N, R = 96, 16, 6
PG = P // N
NG = D // PG
C = 512
J = C // P
EPS = 1e-5
ROUTED_SCALE = 2.5
NCH = 6
NST = 3
WC = 2048


def wait_apart(eng, passed, sem, value):
    eng.wait_ge(sem, value)
    eng.sem_inc(passed, 1)


class Steps:

    def __init__(self, eng, sem, base=0, passed=None):
        self.eng, self.sem, self.base, self.passed, self.n = eng, sem, base, passed, 0

    def __call__(self, ins, apart=False):
        self.n += 1
        ins.then_inc(self.sem, 1)
        if apart:
            wait_apart(self.eng, self.passed, self.sem, self.base + self.n)
        else:
            self.eng.wait_ge(self.sem, self.base + self.n)


def bc(ap, axis, shape):
    return ap.unsqueeze(axis).to_broadcast(shape)


def route_stage(nc, T, B, io):
    (x, xn_d, base_d, out, table, rw, ipw, lnw, lnb, rbias, zT, cnt_base, slots, payload) = io
    NC = T // C
    CPB = NC // B
    FILL = 512
    FILLS = 16 * (E * T // (P * FILL) + SH + 3)

    with ExitStack() as ctx:
        def sb(name, shape, dt=F32):
            return ctx.enter_context(nc.sbuf_tensor(name, shape, dt))

        def ring(name, shape, dt=F32):
            return [sb(f"{name}{i}", shape, dt) for i in range(2)]

        def pb(name, shape, dt=F32):
            return ctx.enter_context(nc.psum_tensor(name, shape, dt))

        def sem(name):
            return ctx.enter_context(nc.semaphore(name))

        wcat = sb("wcat", [P, KH, E + D])
        wraw = sb("wraw", [P, KH, D])
        wlnb = sb("wlnb", [P, KH, D])
        lnw_sb = sb("lnw_sb", [P, KH])
        lnb_sb = sb("lnb_sb", [P, KH])
        bias_b = sb("bias_b", [P, E])
        neg_s = sb("neg_s", [P, D])
        c_b = sb("c_b", [P, D])
        ident = sb("ident", [P, P])
        ones_f = sb("ones_f", [P, P])
        ones_b = sb("ones_b", [P, P], BF16)
        tri = sb("tri", [P, P], BF16)
        iota_i = sb("iota_i", [P, E], I32)
        iota_e = sb("iota_e", [P, E])
        cnt_i = sb("cnt_i", [P, E], I32)
        tid_i = sb("tid_i", [P, J], I32)
        tid = sb("tid", [P, J])
        fill = sb("fill", [P, FILL, 2], I32)
        shared_fill = sb("shared_fill", [P, T // P, 2], I32)
        zero_row = sb("zero_row", [P, H])
        minus_half = sb("minus_half", [P, J])

        xt = ring("xt", [P, J, H])
        xn = ring("xn", [P, J, H])
        bs = sb("bs", [P, J, H])
        xnT = ring("xnT", [P, KH, P])
        st = sb("st", [P, J, 2, 6])
        mv = sb("mv", [P, J, 2])
        rstd = sb("rstd", [P, J])
        st2 = sb("st2", [P, J, 2, 6])
        mv2 = ring("mv2_", [P, J, 2])
        rs2 = ring("rs2_", [P, J])
        score = ring("score", [P, J, E])
        zpre = sb("zpre", [P, J, D])
        z = sb("z", [P, J, D])
        biased = sb("biased", [P, J, E])
        mx = sb("mx", [P, J * G, 2])
        mn = sb("mn", [P, J * G, 2])
        top1 = sb("top1", [P, J * G])
        m2 = sb("m2", [P, J * G])
        m3 = sb("m3", [P, J * G])
        gs = sb("gs", [P, J, G])
        g8 = sb("g8", [P, J, 8])
        gi = sb("gi", [P, J, 8], U32)
        gif = sb("gif", [P, J, 8])
        gcmp = sb("gcmp", [P, J, G, TKG])
        gmask = sb("gmask", [P, J, G])
        masked = sb("masked", [P, J, E])
        v8 = sb("v8", [P, J, 8])
        i8 = sb("i8", [P, J, 8], U32)
        i8f = sb("i8f", [P, J, 8])
        oh = sb("oh", [P, J * K, E])
        prod = sb("prod", [P, J * K, E])
        sel = sb("sel", [P, J, E], BF16)
        w8 = sb("w8", [P, J, K])
        wsum = sb("wsum", [P, J])
        rinv = sb("rinv", [P, J])
        slotrow = sb("slotrow", [P, J, E])
        slotf = sb("slotf", [P, J * K])

        tp = [pb(f"tp{i}", [P, 4, P]) for i in range(2)]
        lg = [pb(f"lg{i}", [P, J, E + D]) for i in range(2)]
        rank = pb("rank", [P, 512])
        zp = pb("zp", [P, J * P])

        const_loaded = sem("const_loaded")
        dve_passed = sem("dve_passed")
        iotas = sem("iotas")
        fills = sem("fills")
        wprep = sem("wprep")
        sums_done = sem("sums_done")
        route_ready = sem("route_ready")
        x_loaded = [sem(f"x_loaded{i}") for i in range(2)]
        var_ready = sem("var_ready")
        rstd_ready = sem("rstd_ready")
        var2_ready = sem("var2_ready")
        rstd2_ready = sem("rstd2_ready")
        xn_ready = sem("xn_ready")
        base_ready = sem("base_ready")
        xn_stored = [sem(f"xn_stored{i}") for i in range(2)]
        base_stored = sem("base_stored")
        base_free = sem("base_free")
        tp_ready = sem("tp_ready")
        tp_free = sem("tp_free")
        lg_ready = sem("lg_ready")
        score_ready = sem("score_ready")
        lg_free = sem("lg_free")
        z_ready = sem("z_ready")
        zp_ready = sem("zp_ready")
        zp_free = sem("zp_free")
        sel_ready = sem("sel_ready")
        rank_ready = sem("rank_ready")
        rank_free = sem("rank_free")
        ln_step = sem("ln_step")
        rt_step = sem("rt_step")
        prep_step = sem("prep_step")

        block = ctx.enter_context(nc.Block())

        @block.sync
        def _(sp):
            def rows(dram, c):
                return dram[bass.ds(c * C, C)].rearrange("(j p) h -> p j h", p=P)

            def load(c, i):
                sp.dma_start(xt[i][:], rows(x, c)).then_inc(x_loaded[i], 16)

            def store(c, i, n):
                sp.wait_ge(xn_ready, n * J)
                sp.dma_start(rows(xn_d, c), xn[i][:]).then_inc(xn_stored[i], 16)
                sp.wait_ge(base_ready, n)
                sp.dma_start(rows(base_d, c), bs[:]).then_inc(base_stored, 16)

            load(0, 0)
            sp.dma_start(wcat[:, :, 0:E], rw.rearrange("(k p) e -> p k e", p=P)).then_inc(const_loaded, 16)
            sp.dma_start(wraw[:], ipw.rearrange("(k p) d -> p k d", p=P)).then_inc(const_loaded, 16)
            sp.dma_start(lnw_sb[:], lnw).then_inc(const_loaded, 16)
            sp.dma_start(lnb_sb[:], lnb).then_inc(const_loaded, 16)
            sp.dma_start(bias_b[:], rbias.partition_broadcast(P)).then_inc(const_loaded, 16)
            load(1, 1)
            sp.wait_ge(iotas, 4)
            span = P * FILL
            for c in range(E * T // span):
                sp.dma_start(table[c * span:(c + 1) * span].rearrange("(p f) w -> p f w", p=P),
                             fill[:]).then_inc(fills, 16)
            sp.dma_start(table[(E + SH) * T:(E + SH) * T + C], fill[0:1]).then_inc(fills, 16)
            for s in range(SH):
                sp.dma_start(table[(E + s) * T:(E + s + 1) * T].rearrange("(p f) w -> p f w", p=P),
                             shared_fill[:]).then_inc(fills, 16)
            sp.dma_start(xn_d[T:T + P], zero_row[:]).then_inc(fills, 16)
            sp.dma_start(out[T:T + P], zero_row[:]).then_inc(fills, 16)
            with sp.Fori(0, NC // 2 - 1) as i:
                for q in range(2):
                    store(i * 2 + q, q, i * 2 + q + 1)
                    load(i * 2 + q + 2, q)
            for q in range(2):
                store(NC - 2 + q, q, NC - 1 + q)
            for q in range(2):
                sp.wait_ge(xn_stored[q], 16 * (NC // 2))
            sp.wait_ge(base_stored, 16 * NC)
            sp.wait_ge(fills, FILLS)

        @block.gpsimd
        def _(pool):
            pool.memset(ident[:], 0.0).then_inc(iotas, 1)
            pool.memset(ones_b[:], 1.0)
            pool.memset(tri[:], 1.0)
            pool.memset(fill[:], 0)
            pool.memset(zero_row[:], 0.0)
            pool.memset(minus_half[:], -0.5)
            pool.memset(shared_fill[:].bitcast(F32), 1.0).then_inc(iotas, 1)
            pool.wait_ge(iotas, 2)
            pool.iota(fill[:, :, 0].rearrange("p (j r) -> p j r", r=P), pattern=[[0, J], [1, P]], base=T,
                      channel_multiplier=0)
            pool.iota(shared_fill[:, :, 0], pattern=[[1, T // P]], base=0, channel_multiplier=T // P)\
                .then_inc(iotas, 2)
            pool.iota(iota_i[:], pattern=[[1, E]], base=0, channel_multiplier=0)
            pool.iota(cnt_i[:], pattern=[[T, E]], base=0, channel_multiplier=0)
            pool.iota(tid_i[:], pattern=[[P, J]], base=0, channel_multiplier=1)
            pool.affine_select(out=tri[:], in_=tri[:], compare_op=ALU.is_ge, fill=0.0, base=-1,
                               pattern=[[1, P]], channel_multiplier=-1)
            pool.affine_select(out=ident[:], in_=ident[:], compare_op=ALU.not_equal, fill=1.0, base=0,
                               pattern=[[-1, P]], channel_multiplier=1).then_inc(iotas, 1)

            def chunk(n, i):
                pool.wait_ge(var_ready, n)
                pool.tensor_tensor(rstd[:], mv[:, :, 1], minus_half[:], ALU.pow).then_inc(rstd_ready, 1)
                for j in range(J):
                    pool.wait_ge(xn_ready, (n - 1) * J + j + 1)
                    if j == 0:
                        pool.wait_ge(base_free, n)
                    last = pool.tensor_tensor(bs[:, j], xt[i][:, j], xn[i][:, j], ALU.add)
                last.then_inc(base_ready, 1)
                pool.wait_ge(var2_ready, n)
                pool.tensor_tensor(rs2[i][:], mv2[i][:, :, 1], minus_half[:], ALU.pow).then_inc(rstd2_ready, 1)
                pool.wait_ge(base_stored, n * 16)
                pool.sem_inc(base_free, 1)

            pool.sem_inc(base_free, 1)
            with pool.Fori(0, NC // 2) as i:
                for q in range(2):
                    chunk(i * 2 + q + 1, q)

        @block.scalar
        def _(act):
            act.sem_inc(tp_free, 2)
            act.sem_inc(zp_free, 1)

            def evacuate(c, n):
                for j in range(J):
                    for h in range(2):
                        act.wait_ge(tp_ready, c * (2 * J) + 2 * j + h + 1)
                        nc.scalar.activation(xnT[j % 2][:, h * 4:h * 4 + 4], tp[h][:], ACT.Copy)\
                            .then_inc(tp_free, 1)

            def choose(c, i):
                act.wait_ge(lg_ready, c * J + J)
                nc.scalar.activation(score[i][:], lg[i][:, :, 0:E], ACT.Sigmoid).then_inc(score_ready, 1)

            def border(c):
                at = (c + 1) * (C + 2)
                act.wait_ge(zp_ready, c + 1)
                nc.scalar.activation(zT[0:D, bass.ds(at + 1, C)], zp[0:D], ACT.Copy)
                nc.scalar.activation(zT[0:D, bass.ds(at - 1, 1)], zp[0:D, 0:1], ACT.Copy)
                nc.scalar.activation(zT[0:D, bass.ds(at + C + 2, 1)], zp[0:D, C - 1:C], ACT.Copy)\
                    .then_inc(zp_free, 1)

            evacuate(0, 1)
            choose(0, 0)
            with act.Fori(0, NC // 2 - 1) as i:
                for q in range(2):
                    evacuate(i * 2 + q + 1, None)
                    choose(i * 2 + q + 1, 1 - q)
                    border(i * 2 + q)
            evacuate(NC - 1, None)
            choose(NC - 1, 1)
            border(NC - 2)
            border(NC - 1)

        @block.tensor
        def _(pe):
            pe.wait_ge(wprep, 1)
            for k in range(KH):
                nc.tensor.matmul(lg[0][:, 0, 0:D], ones_f[:], wcat[:, k, E:E + D], start=k == 0,
                                 stop=k == KH - 1)
            for k in range(KH):
                last = nc.tensor.matmul(lg[1][:, 0, 0:D], ones_f[:], wlnb[:, k], start=k == 0,
                                        stop=k == KH - 1)
            last.then_inc(sums_done, 1)
            pe.wait_ge(iotas, 5)
            pe.wait_ge(route_ready, 1)

            def transposes(c, j, i):
                pe.wait_ge(xn_ready, c * J + j + 1)
                for h in range(2):
                    pe.wait_ge(tp_free, c * (2 * J) + 2 * j + h + 1)
                    for k in range(4):
                        last = nc.tensor.transpose(tp[h][:, k], xn[i][:, j, (h * 4 + k) * P:(h * 4 + k + 1) * P],
                                                   ident[:])
                    last.then_inc(tp_ready, 1)

            def project(c, j, i):
                pe.wait_ge(tp_free, c * (2 * J) + 2 * j + 4)
                if j == 0:
                    pe.wait_ge(lg_free, c + 1)
                for k in range(KH):
                    last = nc.tensor.matmul(lg[i][:, j], xnT[j % 2][:, k], wcat[:, k], start=k == 0,
                                            stop=k == KH - 1)
                last.then_inc(lg_ready, 1)

            def forward(c, i):
                transposes(c, 0, i)
                for j in range(J):
                    project(c, j, i)
                    if j + 1 < J:
                        transposes(c, j + 1, i)

            def rest(c):
                pe.wait_ge(z_ready, c + 1)
                pe.wait_ge(zp_free, c + 1)
                for j in range(J):
                    last = nc.tensor.transpose(zp[0:D, j * P:(j + 1) * P], z[:, j], ident[:])
                last.then_inc(zp_ready, 1)
                pe.wait_ge(sel_ready, c + 1)
                pe.wait_ge(rank_free, c + 1)
                for j in range(J):
                    for jj in range(j):
                        nc.tensor.matmul(rank[:, j * E:(j + 1) * E], ones_b[:], sel[:, jj], start=jj == 0,
                                         stop=False)
                    nc.tensor.matmul(rank[:, j * E:(j + 1) * E], tri[:], sel[:, j], start=j == 0, stop=True)
                for j in range(J):
                    last = nc.tensor.matmul(rank[:, J * E:J * E + E], ones_b[:], sel[:, j], start=j == 0,
                                            stop=j == J - 1)
                last.then_inc(rank_ready, 1)

            forward(0, 0)
            with pe.Fori(0, NC // 2 - 1) as i:
                for q in range(2):
                    forward(i * 2 + q + 1, 1 - q)
                    rest(i * 2 + q)
            forward(NC - 1, 1)
            rest(NC - 2)
            rest(NC - 1)

        @block.vector
        def _(dve):
            v = nc.vector
            dve.sem_inc(rank_free, 1)
            step = Steps(dve, prep_step)
            v.memset(zT[:], 0.0)
            v.memset(ones_f[:], 1.0)
            dve.wait_ge(const_loaded, 16 * 5)
            v.tensor_tensor(wcat[:, :, E:E + D], wraw[:], bc(lnw_sb[:], 2, [P, KH, D]), ALU.mult)
            step(v.tensor_tensor(wlnb[:], wraw[:], bc(lnb_sb[:], 2, [P, KH, D]), ALU.mult))
            dve.sem_inc(wprep, 1)
            dve.wait_ge(iotas, 5)
            v.tensor_copy(iota_e[:], iota_i[:])
            v.tensor_copy(cnt_base[:], cnt_i[:])
            step(v.tensor_copy(tid[:], tid_i[:]))
            dve.wait_ge(sums_done, 1)
            v.tensor_scalar(neg_s[:], lg[0][:, 0, 0:D], -1.0, None, ALU.mult)
            step(v.tensor_copy(c_b[:], lg[1][:, 0, 0:D]))
            dve.sem_inc(route_ready, 1)
            dve.sem_inc(lg_free, 2)

            LN = 4
            RT = 25

            def norms(c, i, loads, stored):
                s = Steps(dve, ln_step, c * LN, dve_passed)
                dve.wait_ge(x_loaded[i], loads)
                for j in range(J):
                    for h in range(2):
                        last = v.bn_stats(st[:, j, h], xt[i][:, j, h * 512:(h + 1) * 512])
                s(last, apart=True)
                for j in range(J):
                    last = v.bn_aggr(mv[:, j], st[:, j].rearrange("p a b -> p (a b)"))
                s(last)
                v.tensor_scalar(mv[:, :, 1], mv[:, :, 1], EPS, None, ALU.add).then_inc(var_ready, 1)
                dve.wait_ge(rstd_ready, c + 1)
                if stored is not None:
                    dve.wait_ge(xn_stored[i], stored)
                    dve.wait_ge(base_ready, c - 1)
                for j in range(J):
                    v.tensor_scalar(xn[i][:, j], xt[i][:, j], mv[:, j, 0:1], rstd[:, j:j + 1], ALU.subtract,
                                    ALU.mult).then_inc(xn_ready, 1)
                dve.wait_ge(xn_ready, c * J + J)
                for j in range(J):
                    for h in range(2):
                        last = v.bn_stats(st2[:, j, h], xn[i][:, j, h * 512:(h + 1) * 512])
                s(last, apart=True)
                for j in range(J):
                    last = v.bn_aggr(mv2[i][:, j], st2[:, j].rearrange("p a b -> p (a b)"))
                s(last)
                v.tensor_scalar(mv2[i][:, :, 1], mv2[i][:, :, 1], EPS, None, ALU.add).then_inc(var2_ready, 1)
                assert s.n == LN

            def route(c, i):
                s = Steps(dve, rt_step, c * RT, dve_passed)
                dve.wait_ge(score_ready, c + 1)
                dve.wait_ge(rstd2_ready, c + 1)
                for j in range(J):
                    last = v.scalar_tensor_tensor(out=zpre[:, j], in0=neg_s[:], scalar=mv2[i][:, j, 0:1],
                                                  in1=lg[i][:, j, E:E + D], op0=ALU.mult, op1=ALU.add)
                s(last)
                dve.sem_inc(lg_free, 1)
                for j in range(J):
                    last = v.scalar_tensor_tensor(out=z[:, j], in0=zpre[:, j], scalar=rs2[i][:, j:j + 1],
                                                  in1=c_b[:], op0=ALU.mult, op1=ALU.add)
                last.then_inc(z_ready, 1)
                s(v.tensor_tensor(biased[:], score[i][:], bc(bias_b[:], 1, [P, J, E]), ALU.add))
                b4 = biased[:].rearrange("p j (g a b) -> p (j g) a b", g=G, b=2)
                v.tensor_tensor(mx[:], b4[:, :, :, 0], b4[:, :, :, 1], ALU.max)
                s(v.tensor_tensor(mn[:], b4[:, :, :, 0], b4[:, :, :, 1], ALU.min))
                v.tensor_tensor(top1[:], mx[:, :, 0], mx[:, :, 1], ALU.max)
                v.tensor_tensor(m2[:], mx[:, :, 0], mx[:, :, 1], ALU.min)
                s(v.tensor_tensor(m3[:], mn[:, :, 0], mn[:, :, 1], ALU.max))
                s(v.tensor_tensor(m2[:], m2[:], m3[:], ALU.max))
                s(v.tensor_tensor(gs[:].rearrange("p j g -> p (j g)"), top1[:], m2[:], ALU.add), apart=True)
                for j in range(J):
                    last = v.max(g8[:, j], gs[:, j])
                s(last, apart=True)
                for j in range(J):
                    last = v.max_index(gi[:, j], g8[:, j], gs[:, j])
                s(last)
                s(v.tensor_copy(gif[:], gi[:]))
                for j in range(J):
                    last = v.tensor_tensor(gcmp[:, j], bc(iota_e[:, 0:G], 2, [P, G, TKG]),
                                           bc(gif[:, j, 0:TKG], 1, [P, G, TKG]), ALU.is_equal)
                s(last)
                s(v.tensor_reduce(gmask[:], gcmp[:], AX.X, ALU.add))
                s(v.tensor_tensor(masked[:].rearrange("p j (g a) -> p (j g) a", g=G),
                                  biased[:].rearrange("p j (g a) -> p (j g) a", g=G),
                                  bc(gmask[:].rearrange("p j g -> p (j g)"), 2, [P, J * G, EG]), ALU.mult),
                  apart=True)
                for j in range(J):
                    last = v.max(v8[:, j], masked[:, j])
                s(last, apart=True)
                for j in range(J):
                    last = v.max_index(i8[:, j], v8[:, j], masked[:, j])
                s(last)
                s(v.tensor_copy(i8f[:], i8[:]))
                s(v.tensor_tensor(oh[:], bc(iota_e[:], 1, [P, J * K, E]),
                                  bc(i8f[:].rearrange("p j k -> p (j k)"), 2, [P, J * K, E]), ALU.is_equal))
                with nc.allow_low_precision(reason="sums of one-hot rows are 0 or 1"):
                    v.tensor_reduce(sel[:], oh[:].rearrange("p (j k) e -> p j e k", j=J), AX.X, ALU.add)\
                        .then_inc(sel_ready, 1)
                for j in range(J):
                    last = v.tensor_tensor(prod[:, j * K:(j + 1) * K], oh[:, j * K:(j + 1) * K],
                                           bc(score[i][:, j], 1, [P, K, E]), ALU.mult)
                s(last)
                s(v.tensor_reduce(w8[:].rearrange("p j k -> p (j k)"), prod[:], AX.X, ALU.add))
                s(v.tensor_reduce(wsum[:], w8[:], AX.X, ALU.add))
                s(v.reciprocal(rinv[:], wsum[:]))
                s(v.tensor_tensor(w8[:], w8[:], bc(rinv[:], 2, [P, J, K]), ALU.mult))
                at = bass.ds(c * (J * K), J * K)
                v.tensor_scalar(payload[:, at, 1].bitcast(F32), w8[:].rearrange("p j k -> p (j k)"), ROUTED_SCALE,
                                None, ALU.mult)
                v.tensor_copy(payload[:, at, 0].rearrange("p (j k) -> p j k", j=J), bc(tid[:], 2, [P, J, K]))
                dve.wait_ge(rank_ready, c + 1)
                s(v.tensor_tensor(slotrow[:], rank[:, 0:J * E].rearrange("p (j e) -> p j e", j=J),
                                  bc(cnt_base[:], 1, [P, J, E]), ALU.add))
                v.tensor_tensor(cnt_base[:], rank[:, J * E:J * E + E], cnt_base[:], ALU.add)
                v.tensor_scalar(tid[:], tid[:], float(C), None, ALU.add).then_inc(rank_free, 1)
                for j in range(J):
                    last = v.tensor_tensor(prod[:, j * K:(j + 1) * K], oh[:, j * K:(j + 1) * K],
                                           bc(slotrow[:, j], 1, [P, K, E]), ALU.mult)
                s(last)
                s(v.tensor_reduce(slotf[:], prod[:], AX.X, ALU.add))
                dve.wait_ge(rank_free, c + 2)
                s(v.tensor_copy(slots[:, at], slotf[:]))
                assert s.n == RT, s.n

            norms(0, 0, 16, None)
            norms(1, 1, 16, None)
            route(0, 0)
            norms(2, 0, 32, 16)
            route(1, 1)
            with dve.Fori(1, NC // 2 - 1) as i:
                norms(i * 2 + 1, 1, i * 16 + 16, i * 16)
                route(i * 2, 0)
                norms(i * 2 + 2, 0, i * 16 + 32, i * 16 + 16)
                route(i * 2 + 1, 1)
            norms(NC - 1, 1, 8 * NC, 8 * NC - 16)
            route(NC - 2, 0)
            route(NC - 1, 1)
            dve.wait_ge(zp_free, NC + 1)
            for b in range(B + 1):
                at = (b * CPB + 1) * (C + 2)
                v.memset(zT[0:D, at - 1:at + 1], 0.0)


def scan_stage(nc, T, B, io):
    (base_d, out, zT, convw, convb, xpT, xpB, xpC, dtT, dtb, alog, dpar, opT) = io
    NC = T // C
    CPB = NC // B
    with ExitStack() as ctx:
        def sb(name, shape, dt=F32):
            return ctx.enter_context(nc.sbuf_tensor(name, shape, dt))

        def ring(name, shape, dt=F32):
            return [sb(f"{name}{i}", shape, dt) for i in range(2)]

        def pb(name, shape, dt=F32):
            return ctx.enter_context(nc.psum_tensor(name, shape, dt))

        def sem(name):
            return ctx.enter_context(nc.semaphore(name))

        cw = sb("cw", [D, 3])
        cb = sb("cb", [D, 1])
        w_dt = sb("w_dt", [D, R])
        w_B = sb("w_B", [D, P])
        w_C = sb("w_C", [D, P])
        w_dtp = sb("w_dtp", [R, D])
        b_dt = sb("b_dt", [D, 1])
        a_log = sb("a_log", [P, NG])
        a_exp = sb("a_exp", [P, NG])
        a_neg = sb("a_neg", [P, NG])
        dp = sb("dp", [D, 1])
        w_o = sb("w_o", [D, H])
        spread_f = sb("spread_f", [D, NG, P])
        spread = sb("spread", [D, NG, P], F32R)
        gather = sb("gather", [P, NG, D])
        conv = sb("conv", [D, C])
        u = ring("u", [D, C])
        dr = sb("dr", [R, C])
        Bs = ring("Bs", [P, C])
        Cs = ring("Cs", [P, C])
        pre = sb("pre", [D, C])
        ab = sb("ab", [D, C])
        ex = sb("ex", [D, C])
        ln = sb("ln", [D, C])
        ser = sb("ser", [D, C])
        small = sb("small", [D, C])
        delta = sb("delta", [D, C])
        du = sb("du", [D, C])
        d_hi = ring("d_hi", [D, C], F32R)
        d_lo = ring("d_lo", [D, C], F32R)
        du_hi = ring("du_hi", [D, C], F32R)
        du_lo = ring("du_lo", [D, C], F32R)
        dA = ring("dA", [P, C])
        dBu = ring("dBu", [P, C])
        hs = ring("hs", [P, C])
        hc = ring("hc", [P, C])
        state = sb("state", [P, NG])
        yT = sb("yT", [D, C])
        bs = [sb(f"base{i}", [P, H]) for i in range(J)]
        proj = pb("proj", [P, 512])
        rep_d = [pb(f"rep_d{i}", [P, 512]) for i in range(2)]
        rep_u = [pb(f"rep_u{i}", [P, 512]) for i in range(2)]
        yp = pb("yp", [P, 512])
        op = [pb(f"op{i}", [P, 512]) for i in range(2)]

        loaded = sem("loaded")
        dve_passed = sem("dve_passed")
        sp_passed = sem("sp_passed")
        consts = sem("consts")
        a_ready = sem("a_ready")
        conv_ready = sem("conv_ready")
        u_ready = sem("u_ready")
        proj_ready = sem("proj_ready")
        bc_ready = sem("bc_ready")
        pre_ready = sem("pre_ready")
        act_sp = sem("act_sp")
        delta_ready = sem("delta_ready")
        hi_ready = sem("hi_ready")
        parts_ready = sem("parts_ready")
        rep_ready = sem("rep_ready")
        dA_ready = sem("dA_ready")
        dBu_ready = sem("dBu_ready")
        scan_done = sem("scan_done")
        dA_free = sem("dA_free")
        hc_ready = sem("hc_ready")
        y_acc = sem("y_acc")
        y_ready = sem("y_ready")
        op_ready = sem("op_ready")
        op_free = sem("op_free")
        base_in = [sem(f"base_in{i}") for i in range(J)]
        base_out = sem("base_out")
        dve_step = sem("dve_step")
        state_set = sem("state_set")

        block = ctx.enter_context(nc.Block())

        @block.sync
        def _(sp):
            for dst, src in ((cw, convw), (cb, convb), (w_dt, xpT), (w_B, xpB), (w_C, xpC), (w_dtp, dtT),
                             (b_dt, dtb), (a_log, alog), (dp, dpar), (w_o, opT)):
                sp.dma_start(dst[:], src).then_inc(loaded, 16)
            with sp.Fori(0, NC) as c:
                for j in range(J):
                    sp.dma_start(bs[j][:], base_d[bass.ds(c * C + j * P, P)]).then_inc(base_in[j], 16)
                for j in range(J):
                    sp.wait_ge(op_free, c * (2 * J) + 2 * j + 4)
                    sp.dma_start(out[bass.ds(c * C + j * P, P)], bs[j][:]).then_inc(base_out, 16)
                wait_apart(sp, sp_passed, base_out, c * (16 * J) + 16 * J)

        @block.gpsimd
        def _(pool):
            g = nc.gpsimd
            g.memset(spread_f[:], 1.0)
            g.memset(gather[:], 1.0).then_inc(consts, 1)
            pool.wait_ge(consts, 1)
            g.affine_select(out=spread_f[:], in_=spread_f[:], compare_op=ALU.is_ge, fill=0.0, base=0,
                            pattern=[[P, NG], [1, P]], channel_multiplier=-N)
            g.affine_select(out=gather[:], in_=gather[:], compare_op=ALU.is_ge, fill=0.0, base=0,
                            pattern=[[P, NG], [-N, D]], channel_multiplier=1).then_inc(consts, 1)
            pool.wait_ge(consts, 2)
            g.affine_select(out=spread_f[:], in_=spread_f[:], compare_op=ALU.is_ge, fill=0.0, base=N - 1,
                            pattern=[[-P, NG], [-1, P]], channel_multiplier=N)
            g.affine_select(out=gather[:], in_=gather[:], compare_op=ALU.is_ge, fill=0.0, base=N - 1,
                            pattern=[[-P, NG], [N, D]], channel_multiplier=-1).then_inc(consts, 1)
            pool.wait_ge(consts, 3)
            pool.sem_inc(hc_ready, 2)
            with pool.Fori(0, NC // 2) as i:
                for r in range(2):
                    for q in range(NG):
                        n = (i * 2 + r) * NG + q
                        pool.wait_ge(scan_done, n + 1)
                        pool.wait_ge(y_acc, n + 1)
                        g.tensor_tensor(hc[q % 2][:], hs[q % 2][:], Cs[r][:], ALU.mult).then_inc(hc_ready, 1)

        @block.scalar
        def _(act):
            a = nc.scalar

            def silu(n, r):
                act.wait_ge(conv_ready, n + 1)
                act.wait_ge(y_ready, n + 1)
                a.activation(u[r][:], conv[:], ACT.Silu, bias=cb[:]).then_inc(u_ready, 1)

            def projected(n, r):
                act.wait_ge(proj_ready, n * 2 + 1)
                a.activation(dr[:], proj[0:R], ACT.Copy)
                a.activation(Bs[r][:], op[0][:], ACT.Copy)
                a.activation(Cs[r][:], op[1][:], ACT.Copy).then_inc(bc_ready, 1)

            def logs(n):
                act.wait_ge(pre_ready, n + 1)
                a.activation(ab[:], pre[:], ACT.Abs).then_inc(act_sp, 1)
                act.wait_ge(act_sp, n * 3 + 1)
                a.activation(ex[:], ab[:], ACT.Exp, scale=-1.0).then_inc(act_sp, 1)
                act.wait_ge(act_sp, n * 3 + 2)
                a.activation(ln[:], ex[:], ACT.Ln, bias=1.0).then_inc(act_sp, 1)

            def highs(n, r):
                act.wait_ge(delta_ready, n + 1)
                a.activation(d_hi[r][:], delta[:], ACT.Copy)
                a.activation(du_hi[r][:], du[:], ACT.Copy).then_inc(hi_ready, 1)

            act.wait_ge(loaded, 160)
            a.activation(a_exp[:], a_log[:], ACT.Exp).then_inc(a_ready, 1)
            act.wait_ge(a_ready, 2)
            silu(0, 0)
            projected(0, 0)
            logs(0)
            highs(0, 0)
            with act.Fori(0, NC // 2) as i:
                for r in range(2):
                    c = i * 2 + r
                    for q in range(NG):
                        act.wait_ge(rep_ready, c * NG + q + 1)
                        act.wait_ge(dA_free, c * NG + q + 1)
                        a.activation(dA[q % 2][:], rep_d[q % 2][:], ACT.Exp, scale=a_neg[:, q:q + 1])\
                            .then_inc(dA_ready, 1)
                        if q == 1:
                            silu(c + 1, 1 - r)
                        if q == 2:
                            projected(c + 1, 1 - r)
                        if q == 4:
                            logs(c + 1)
                        if q == 9:
                            highs(c + 1, 1 - r)

        @block.tensor
        def _(pe):
            m = nc.tensor.matmul
            pe.wait_ge(loaded, 160)
            pe.wait_ge(consts, 4)
            pe.sem_inc(y_acc, 2)

            def project(n, r):
                pe.wait_ge(u_ready, n + 1)
                pe.wait_ge(op_free, (n - 2) * (2 * J) + 2 if not isinstance(n, int) or n > 1 else 2)
                m(proj[0:R], w_dt[:], u[r][:], start=True, stop=True)
                m(op[0][:], w_B[:], u[r][:], start=True, stop=True)
                m(op[1][:], w_C[:], u[r][:], start=True, stop=True).then_inc(proj_ready, 1)

            def time_step(n):
                pe.wait_ge(bc_ready, n + 1)
                m(proj[0:D], w_dtp[:], dr[:], start=True, stop=True).then_inc(proj_ready, 1)

            def spread_to(c, r, q):
                n = c * NG + q
                pe.wait_ge(dA_ready, n + 1)
                pe.wait_ge(dBu_ready, n + 1)
                m(rep_d[q % 2][:], spread[:, q], d_hi[r][:], start=True, stop=False)
                m(rep_d[q % 2][:], spread[:, q], d_lo[r][:], start=False, stop=True)
                m(rep_u[q % 2][:], spread[:, q], du_hi[r][:], start=True, stop=False)
                m(rep_u[q % 2][:], spread[:, q], du_lo[r][:], start=False, stop=True).then_inc(rep_ready, 1)

            def out_half(c, n):
                j, h = n // 2, n % 2
                if n == 0:
                    pe.wait_ge(y_ready, c + 3)
                pe.wait_ge(op_free, c * (2 * J) + n + 1)
                m(op[h][:], yT[:, j * P:(j + 1) * P], w_o[:, h * 512:(h + 1) * 512], start=True,
                  stop=True).then_inc(op_ready, 1)

            def body(c, r, first=False):
                for q in range(NG):
                    if q + 2 < NG:
                        spread_to(c, r, q + 2)
                    else:
                        if q + 2 == NG:
                            pe.wait_ge(parts_ready, c + 2)
                        spread_to(c + 1, 1 - r, q + 2 - NG)
                    pe.wait_ge(hc_ready, c * NG + q + 3)
                    if q == 0 and not first:
                        pe.wait_ge(y_ready, c + 2)
                    m(yp[0:D], gather[:, q], hc[q % 2][:], start=q == 0, stop=q == NG - 1).then_inc(y_acc, 1)
                    if q == 1:
                        project(c + 1, 1 - r)
                    if q == 3:
                        time_step(c + 1)
                    if 3 <= q < 3 + 2 * J and not first:
                        out_half(c - 1, q - 3)

            project(0, 0)
            time_step(0)
            pe.wait_ge(parts_ready, 1)
            spread_to(0, 0, 0)
            spread_to(0, 0, 1)
            body(0, 0, True)
            body(1, 1)
            with pe.Fori(1, NC // 2) as i:
                for r in range(2):
                    body(i * 2 + r, r)
            for n in range(2 * J):
                out_half(NC - 1, n)

        @block.vector
        def _(dve):
            v = nc.vector
            dve.wait_ge(consts, 3)
            v.tensor_copy(spread[:], spread_f[:]).then_inc(consts, 1)
            dve.wait_ge(a_ready, 1)
            v.tensor_scalar(a_neg[:], a_exp[:], -1.0, None, ALU.mult).then_inc(a_ready, 1)
            dve.wait_ge(loaded, 160)
            dve.sem_inc(dBu_ready, 2)
            dve.sem_inc(dA_ready, 2)
            dve.sem_inc(op_free, 2)
            dve.sem_inc(dA_free, 2)
            dve.sem_inc(y_ready, 2)
            ST = 11

            def convolve(n, wait=True):
                s = Steps(dve, dve_step, n * ST)
                at = (n + 1) * (C + 2)
                if wait:
                    dve.wait_ge(u_ready, n)
                s(v.tensor_scalar(conv[:], zT[0:D, bass.ds(at, C)], cw[:, 0:1], None, ALU.mult))
                s(v.scalar_tensor_tensor(out=conv[:], in0=zT[0:D, bass.ds(at + 1, C)], scalar=cw[:, 1:2],
                                         in1=conv[:], op0=ALU.mult, op1=ALU.add))
                v.scalar_tensor_tensor(out=conv[:], in0=zT[0:D, bass.ds(at + 2, C)], scalar=cw[:, 2:3],
                                       in1=conv[:], op0=ALU.mult, op1=ALU.add).then_inc(conv_ready, 1)

            def bias_dt(n):
                dve.wait_ge(proj_ready, n * 2 + 2)
                v.tensor_scalar(pre[:], proj[0:D], b_dt[:], None, ALU.add).then_inc(pre_ready, 1)

            def softplus(n, r, part):
                s = Steps(dve, dve_step, n * ST + 2 + (0, 2, 4, 7)[part])
                if part == 0:
                    dve.wait_ge(act_sp, n * 3 + 3)
                    v.tensor_scalar(small[:], ex[:], 2.0 ** -5, None, ALU.is_lt)
                    s(v.tensor_scalar(ser[:], ex[:], -0.25, 1.0 / 3.0, ALU.mult, ALU.add))
                    s(v.tensor_tensor(ser[:], ser[:], ex[:], ALU.mult))
                if part == 1:
                    s(v.scalar_tensor_tensor(out=ser[:], in0=ser[:], scalar=-0.5, in1=ex[:], op0=ALU.add,
                                             op1=ALU.mult))
                    s(v.scalar_tensor_tensor(out=ser[:], in0=ser[:], scalar=1.0, in1=ex[:], op0=ALU.add,
                                             op1=ALU.mult))
                if part == 2:
                    s(v.tensor_tensor(ser[:], ser[:], ln[:], ALU.subtract))
                    s(v.tensor_tensor(ser[:], ser[:], small[:], ALU.mult))
                    s(v.tensor_tensor(ser[:], ser[:], ln[:], ALU.add))
                if part == 3:
                    s(v.scalar_tensor_tensor(out=ser[:], in0=pre[:], scalar=0.0, in1=ser[:], op0=ALU.max,
                                             op1=ALU.add))
                    s(v.tensor_scalar(delta[:], ser[:], 0.001, None, ALU.mult))
                    v.tensor_tensor(du[:], delta[:], u[r][:], ALU.mult).then_inc(delta_ready, 1)

            def lows(n, r):
                dve.wait_ge(hi_ready, n + 1)
                v.tensor_tensor(d_lo[r][:], delta[:], d_hi[r][:], ALU.subtract)
                v.tensor_tensor(du_lo[r][:], du[:], du_hi[r][:], ALU.subtract).then_inc(parts_ready, 1)

            def tail(c, r):
                dve.wait_ge(y_acc, c * NG + NG + 2)
                v.scalar_tensor_tensor(out=yT[:], in0=u[r][:], scalar=dp[:], in1=yp[0:D], op0=ALU.mult,
                                       op1=ALU.add).then_inc(y_ready, 1)

            def add_half(c, n):
                j, h = n // 2, n % 2
                if h == 0:
                    dve.wait_ge(base_in[j], c * 16 + 16)
                dve.wait_ge(op_ready, c * (2 * J) + n + 1)
                v.tensor_tensor(bs[j][:, h * 512:(h + 1) * 512], op[h][:],
                                bs[j][:, h * 512:(h + 1) * 512], ALU.add).then_inc(op_free, 1)

            def body(c, r, first=False):
                for q in range(NG):
                    n = c * NG + q
                    if q == 10:
                        lows(c + 1, 1 - r)
                    dve.wait_ge(rep_ready, n + 1)
                    v.tensor_tensor(dBu[q % 2][:], rep_u[q % 2][:], Bs[r][:], ALU.mult).then_inc(dBu_ready, 1)
                    dve.wait_ge(dBu_ready, n + 3)
                    dve.wait_ge(dA_ready, n + 3)
                    dve.wait_ge(hc_ready, n + 1)
                    v.tensor_tensor_scan(hs[q % 2][:], dA[q % 2][:], dBu[q % 2][:], state[:, q:q + 1],
                                         ALU.mult, ALU.add).then_inc(scan_done, 1)
                    dve.wait_ge(scan_done, n + 1)
                    v.tensor_copy(state[:, q:q + 1], hs[q % 2][:, C - 1:C]).then_inc(dA_free, 1)
                    if q == 0 and not first:
                        tail(c - 1, 1 - r)
                    if 4 <= q < 4 + 2 * J and not first:
                        add_half(c - 1, q - 4)
                    if q == 4:
                        bias_dt(c + 1)
                    if 5 <= q < 9:
                        softplus(c + 1, 1 - r, q - 5)
                    if q == 9:
                        convolve(c + 2)

            v.memset(state[:], 0.0).then_inc(state_set, 1)
            convolve(0, False)
            bias_dt(0)
            dve.wait_ge(bc_ready, 1)
            for part in range(4):
                softplus(0, 0, part)
            lows(0, 0)
            convolve(1)
            dve.wait_ge(state_set, 1)
            body(0, 0, True)
            body(1, 1)
            with dve.Fori(1, CPB // 2) as i:
                for r in range(2):
                    body(i * 2 + r, r)
            with dve.Fori(1, B) as b:
                dve.wait_ge(dA_free, b * (CPB * NG) + 2)
                v.memset(state[:], 0.0).then_inc(state_set, 1)
                wait_apart(dve, dve_passed, state_set, b + 1)
                with dve.Fori(0, CPB // 2) as i:
                    for r in range(2):
                        body(b * CPB + i * 2 + r, r)
            tail(NC - 1, 1)
            for n in range(2 * J):
                add_half(NC - 1, n)


def plan_stage(nc, T, cnt_base, plan, ahead, xn_d, table, w_all):
    starts, experts, fresh, runs, tiles, before_t = plan
    NSH = SH * T // C
    NR = T * K // C + E - 1
    NB = NSH + NR
    PAD = (E + SH) * T
    with ExitStack() as ctx:
        def sb(name, shape, dt=F32):
            return ctx.enter_context(nc.sbuf_tensor(name, shape, dt))

        reg_i = sb("reg_i", [1, E], I32)
        blk_i = sb("blk_i", [1, NR], I32)
        reg_f = sb("reg_f", [1, E])
        blk = sb("blk", [1, NR])
        cnt = sb("cnt", [1, E])
        cnt_int = sb("cnt_int", [1, E], I32)
        nblk = sb("nblk", [1, E])
        one = sb("one", [1, E])
        cum = sb("cum", [1, E])
        before = sb("before", [1, NR, E])
        eid = sb("eid", [1, NR])
        first = sb("first", [1, NR])
        start = sb("start", [1, NR])
        idle = sb("idle", [1, NR])
        some = sb("some", [1, NR, E])
        steps_ = sb("steps_", [1, E])
        taken = sb("taken", [1, NR])
        taken_i = sb("taken_i", [1, NR], I32)
        tiles_f = sb("tiles_f", [1, NB + 1])
        through_f = sb("through_f", [1, NB + 1])
        exp_f = sb("exp_f", [1, NB + 1])
        fresh_f = sb("fresh_f", [1, NB + 1])
        runs_f = sb("runs_f", [1, NB + 1])
        ones_r = sb("ones_r", [1, NB + 1])
        made = ctx.enter_context(nc.semaphore("made"))
        done = ctx.enter_context(nc.semaphore("done"))
        block = ctx.enter_context(nc.Block())

        @block.sync
        def _(sp):
            for q in range(NST):
                sp.dma_start(ahead["stage"][q][:], w_all[E * NCH + q]).then_inc(ahead["staged"][q], 16)

        @block.gpsimd
        def _(pool):
            g = nc.gpsimd

            def slots_of(b):
                first = E * T + b * C
                g.dma_start(ahead["idx_in"][:], table[first:first + C].rearrange("(j p) w -> p j w", p=P))\
                    .then_inc(ahead["idx_loaded"], 16)

            slots_of(0)
            g.iota(reg_i[:], pattern=[[T, E]], base=0, channel_multiplier=0)
            g.iota(blk_i[:], pattern=[[1, NR]], base=0, channel_multiplier=0)
            g.iota(starts[:, 0:NSH], pattern=[[C, NSH]], base=E * T, channel_multiplier=0)
            g.iota(starts[:, NSH + NR:NSH + NR + 2], pattern=[[0, 2]], base=PAD, channel_multiplier=0)
            g.iota(experts[:, NSH + NR:NSH + NR + 1], pattern=[[0, 1]], base=E - 1, channel_multiplier=0)
            g.iota(experts[:, 0:NSH].rearrange("p (a b) -> p a b", a=SH), pattern=[[1, SH], [0, T // C]],
                   base=E, channel_multiplier=0).then_inc(made, 1)
            pool.wait_ge(ahead["idx_loaded"], 16)
            g.tensor_copy(ahead["idx_next"][:], ahead["idx_in"][:]).then_inc(ahead["idx_moved"], 1)
            pool.wait_ge(ahead["idx_moved"], 1)
            slots_of(1)
            for j in range(J):
                g.indirect_dma_start(out=ahead["xraw"][:, j], out_offset=None, in_=xn_d,
                                     in_offset=bass.IndirectOffsetOnAxis(ap=ahead["idx_next"][:, j, 0:1], axis=0))\
                    .then_inc(ahead["gathered"], 16)

        @block.vector
        def _(dve):
            v = nc.vector
            s = Steps(dve, done)
            dve.wait_ge(made, 1)
            v.memset(one[:], 1.0)
            v.tensor_copy(reg_f[:], reg_i[:])
            s(v.tensor_copy(blk[:], blk_i[:]))
            s(v.tensor_tensor(cnt[:], cnt_base[0:1], reg_f[:], ALU.subtract))
            s(v.tensor_scalar(cnt_int[:], cnt[:], float(C - 1), None, ALU.add))
            s(v.tensor_scalar(cnt_int[:], cnt_int[:], C.bit_length() - 1, None, ALU.logical_shift_right))
            s(v.tensor_copy(nblk[:], cnt_int[:]))
            s(v.tensor_tensor_scan(cum[:], one[:], nblk[:], 0.0, ALU.mult, ALU.add))
            s(v.tensor_tensor(before[:], bc(blk[:], 2, [1, NR, E]), bc(cum[:], 1, [1, NR, E]), ALU.is_ge))
            s(v.tensor_reduce(eid[:], before[:], AX.X, ALU.add))
            v.tensor_tensor(steps_[:, 0:E - 1], cnt[:, 1:E], cnt[:, 0:E - 1], ALU.subtract)
            s(v.tensor_scalar(steps_[:, E - 1:E], cnt[:, E - 1:E], -1.0, None, ALU.mult))
            s(v.tensor_tensor(some[:], before[:], bc(steps_[:], 1, [1, NR, E]), ALU.mult))
            s(v.tensor_reduce(taken[:], some[:], AX.X, ALU.add))
            s(v.tensor_scalar(taken[:], taken[:], cnt[:, 0:1], None, ALU.add))
            s(v.tensor_tensor(before[:], before[:], bc(nblk[:], 1, [1, NR, E]), ALU.mult))
            s(v.tensor_reduce(first[:], before[:], AX.X, ALU.add))
            s(v.tensor_tensor(first[:], blk[:], first[:], ALU.subtract))
            s(v.scalar_tensor_tensor(out=taken[:], in0=first[:], scalar=-float(C), in1=taken[:], op0=ALU.mult,
                                     op1=ALU.add))
            v.memset(tiles[:, 0:NSH], J)
            v.memset(tiles[:, NB:NB + 1], 0)
            s(v.tensor_scalar(taken[:], taken[:], 0.0, float(C), ALU.max, ALU.min))
            s(v.tensor_scalar(taken_i[:], taken[:], float(P - 1), None, ALU.add))
            s(v.tensor_scalar(tiles[:, NSH:NB], taken_i[:], P.bit_length() - 1, None, ALU.logical_shift_right))
            v.memset(ones_r[:], 1.0)
            s(v.tensor_copy(tiles_f[:], tiles[:]))
            s(v.tensor_tensor_scan(through_f[:], ones_r[:], tiles_f[:], 0.0, ALU.mult, ALU.add))
            v.memset(before_t[:, 0:1], 0)
            v.tensor_copy(before_t[:, 1:NB + 2], through_f[:])
            v.tensor_scalar(idle[:], eid[:], float(E), None, ALU.is_ge)
            s(v.tensor_scalar(start[:], eid[:], float(T), None, ALU.mult))
            s(v.scalar_tensor_tensor(out=start[:], in0=first[:], scalar=float(C), in1=start[:], op0=ALU.mult,
                                     op1=ALU.add))
            s(v.tensor_scalar(first[:], start[:], -1.0, float(PAD), ALU.mult, ALU.add))
            s(v.tensor_tensor(first[:], first[:], idle[:], ALU.mult))
            s(v.tensor_tensor(starts[:, NSH:NSH + NR], start[:], first[:], ALU.add))
            s(v.tensor_scalar(experts[:, NSH:NSH + NR], eid[:], float(E - 1), None, ALU.min))
            v.memset(fresh_f[:, 0:1], 1.0)
            s(v.tensor_copy(exp_f[:], experts[:]))
            s(v.tensor_tensor(fresh_f[:, 1:NB + 1], exp_f[:, 1:NB + 1], exp_f[:, 0:NB], ALU.not_equal))
            s(v.tensor_tensor_scan(runs_f[:], ones_r[:], fresh_f[:], -1.0, ALU.mult, ALU.add))
            v.tensor_copy(fresh[:], fresh_f[:])
            s(v.tensor_copy(runs[:], runs_f[:]))


def value_of(eng, row, b, top):
    return eng.value_load(row[0:1, bass.ds(b, 1)], min_val=0, max_val=top)


def by_tiles(eng, passed, count, work, idle=None):
    with eng.If(count > J - 1):
        work(J)
    with eng.Else():
        with eng.If(count > 0):
            with eng.If(count > 1):
                with eng.If(count > 2):
                    work(3)
                with eng.Else():
                    work(2)
                eng.sem_inc(passed, 1)
            with eng.Else():
                work(1)
            eng.sem_inc(passed, 1)
        with eng.Else():
            if idle:
                idle()
            eng.sem_inc(passed, 1)
        eng.sem_inc(passed, 1)


def expert_stage(nc, T, io, plan, ahead):
    (xn_d, out, table, w_all, slots, payload) = io
    starts, experts, fresh, runs, tiles, before_t = plan
    NSH = SH * T // C
    NSC = T // P * K // NSH
    NB = SH * T // C + T * K // C + E - 1
    with ExitStack() as ctx:
        def sb(name, shape, dt=F32):
            return ctx.enter_context(nc.sbuf_tensor(name, shape, dt))

        def pb(name, shape, dt=F32):
            return ctx.enter_context(nc.psum_tensor(name, shape, dt))

        def sem(name):
            return ctx.enter_context(nc.semaphore(name))

        stage, staged, xraw, gathered = (ahead[name] for name in ("stage", "staged", "xraw", "gathered"))
        idx_in = ahead["idx_in"]
        idx_next = ahead["idx_next"]
        idx_loaded, idx_moved = ahead["idx_loaded"], ahead["idx_moved"]
        w_hi = [sb(f"w_hi{q}", [P, WC], F32R) for q in range(NCH)]
        w_lo = [sb(f"w_lo{q}", [P, WC], F32R) for q in range(NCH)]
        x_hi = sb("x_hi", [P, KH, C], F32R)
        x_lo = sb("x_lo", [P, KH, C], F32R)
        a_hi = sb("a_hi", [P, KI, C], F32R)
        a_lo = sb("a_lo", [P, KI, C], F32R)
        sg = sb("sg", [P, C])
        av = sb("av", [P, C])
        y = sb("y", [P, 2, H])
        slot_cur = sb("slot_cur", [P, NSC], U32)
        payload_cur = sb("payload_cur", [P, NSC, 2], I32)
        idx_cur = sb("idx_cur", [P, J, 2], I32)
        ident = sb("ident2", [P, P])
        pg = [pb(f"pg{i}", [P, C]) for i in range(2)]
        pu = [pb(f"pu{i}", [P, C]) for i in range(2)]
        tp = [pb(f"tx{i}", [P, J, P]) for i in range(2)]
        pd = [pb(f"pd{i}", [P, 512]) for i in range(2)]

        made = sem("ident_made")
        pool_passed = sem("pool_passed")
        sp_passed = sem("sp_passed")
        act_passed = sem("act_passed")
        dve_passed = sem("dve_passed")
        pe_passed = sem("pe_passed")
        split_hi = sem("split_hi")
        split = sem("split")
        idx_copied = sem("idx_copied")
        tp_ready = sem("tx_ready")
        xh_ready = sem("xh_ready")
        xT_ready = sem("xT_ready")
        gu_ready = sem("gu_ready")
        gate_read = sem("gate_read")
        up_read = sem("up_read")
        ah_ready = sem("ah_ready")
        a_ready = sem("act_ready")
        down_ready = sem("down_ready")
        down_read = sem("down_read")
        added = sem("added")
        y_free = sem("y_free")
        columns_ready = sem("columns_ready")
        scattered = sem("scattered")

        block = ctx.enter_context(nc.Block())

        @block.sync
        def _(sp):
            def load(e, q, s):
                sp.wait_ge(split, s)
                sp.dma_start(stage[q % NST][:], w_all[bass.ds(e * NCH + q, 1)]
                             .rearrange("a p c -> (a p) c")).then_inc(staged[q % NST], 16)

            def value(row, b, top):
                return sp.value_load(row[0:1, bass.ds(b, 1)], min_val=0, max_val=top)

            e = value(experts, 0, E + SH - 1)
            load(e, NST, NST + 1)
            with sp.Fori(0, NB) as b:
                with sp.If(value(tiles, b, J) > 0):
                    with sp.If(value(fresh, b, 1) > 0):
                        e = value(experts, b, E + SH - 1)
                        for q in (4, 5):
                            load(e, q, b * NCH + q + 1)
                    with sp.Else():
                        sp.sem_inc(sp_passed, 1)
                    with sp.If(value(fresh, b + 1, 1) > 0):
                        e = value(experts, b + 1, E + SH - 1)
                        for q in range(4):
                            load(e, q, b * NCH + NCH + q + 1)
                    with sp.Else():
                        sp.sem_inc(sp_passed, 1)
                    sp.sem_inc(sp_passed, 1)
                with sp.Else():
                    sp.sem_inc(sp_passed, 1)

        @block.gpsimd
        def _(pool):
            g = nc.gpsimd
            g.memset(ident[:], 0.0).then_inc(made, 1)
            pool.wait_ge(made, 1)
            g.affine_select(out=ident[:], in_=ident[:], compare_op=ALU.not_equal, fill=1.0, base=0,
                            pattern=[[-1, P]], channel_multiplier=1).then_inc(made, 1)
            pool.sem_inc(y_free, 2)

            def load_slots(b):
                first = pool.value_load(starts[0:1, bass.ds(b, 1)], min_val=0, max_val=(E + SH) * T)
                g.dma_start(idx_in[:], table[bass.ds(first, C)].rearrange("(j p) w -> p j w", p=P))\
                    .then_inc(idx_loaded, 16)

            def gather(b, n, more=True):
                wait_apart(pool, pool_passed, idx_loaded, n * 16)
                g.tensor_copy(idx_next[:], idx_in[:]).then_inc(idx_moved, 1)
                wait_apart(pool, pool_passed, idx_moved, n)
                if more:
                    load_slots(b + 1)

                def rows_of(count):
                    for j in range(count):
                        g.indirect_dma_start(out=xraw[:, j], out_offset=None, in_=xn_d,
                                             in_offset=bass.IndirectOffsetOnAxis(ap=idx_next[:, j, 0:1], axis=0))\
                            .then_inc(gathered, 16)
                by_tiles(pool, pool_passed, value_of(pool, tiles, b, J), rows_of)

            def next_rows(b, more=True):
                pool.wait_ge(idx_copied, b + 1)
                pool.wait_ge(tp_ready, b * KH + KH)
                gather(b + 1, b + 2, more)

            def scatter(b):
                g.tensor_copy(slot_cur[:], slots[:, bass.ds(b * NSC, NSC)])
                g.tensor_copy(payload_cur[:], payload[:, bass.ds(b * NSC, NSC)]).then_inc(columns_ready, 1)
                wait_apart(pool, pool_passed, columns_ready, b + 1)
                for j in range(NSC):
                    g.indirect_dma_start(
                        out=table, out_offset=bass.IndirectOffsetOnAxis(ap=slot_cur[:, j:j + 1], axis=0),
                        in_=payload_cur[:, j], in_offset=None).then_inc(scattered, 16)

            def adds_of(b, start, count):
                for j in range(count):
                    wait_apart(pool, pool_passed, down_read, b * (2 * J) + 2 * j + 4)
                    g.indirect_dma_start(out=out, out_offset=bass.IndirectOffsetOnAxis(ap=idx_cur[:, j, 0:1], axis=0),
                                         in_=y[:, j % 2], in_offset=None, compute_op=ALU.add).then_inc(added, 16)
                    pool.wait_ge(added, start * 16 + 16 * j + 16)
                    pool.sem_inc(y_free, 1)
                if count < J:
                    pool.sem_inc(y_free, J - count)

            def adds(b):
                start = value_of(pool, before_t, b, NB * J)
                by_tiles(pool, pool_passed, value_of(pool, tiles, b, J), lambda count: adds_of(b, start, count))

            def shared(b, more=True):
                next_rows(b, more)
                scatter(b)
                adds(b)
                pool.wait_ge(scattered, b * (16 * NSC) + 16 * NSC)
                pool.sem_inc(pool_passed, 1)

            with pool.Fori(0, NSH - 2) as b:
                shared(b)
            shared(NSH - 2, False)
            scatter(NSH - 1)
            pool.wait_ge(scattered, NSH * (16 * NSC))
            load_slots(NSH)
            next_rows(NSH - 1)
            adds(NSH - 1)
            with pool.Fori(NSH, NB) as b:
                with pool.If(value_of(pool, tiles, b, J) > 0):
                    next_rows(b)
                    adds(b)
                with pool.Else():
                    pool.sem_inc(pool_passed, 1)

        @block.scalar
        def _(act):
            a = nc.scalar
            act.sem_inc(gate_read, 2)

            def high(q, n):
                act.wait_ge(staged[q % NST], n)
                a.activation(w_hi[q][:], stage[q % NST][:], ACT.Copy).then_inc(split_hi, 1)

            def x_high(k, n):
                act.wait_ge(tp_ready, n + k + 1)
                a.activation(x_hi[:, k], tp[k % 2][:].rearrange("p j c -> p (j c)"), ACT.Copy)\
                    .then_inc(xh_ready, 1)

            for q in range(4):
                high(q, 16 * (q // NST + 1))
            for k in range(KH):
                x_high(k, 0)

            def hidden(b, i, cols):
                act.wait_ge(gu_ready, b * KI + i + 1)
                act.wait_ge(up_read, b * KI + i + 1)
                a.activation(sg[:, 0:cols], pg[i % 2][:, 0:cols], ACT.Silu).then_inc(gate_read, 1)
                act.wait_ge(up_read, b * KI + i + 2)
                a.activation(a_hi[:, i, 0:cols], av[:, 0:cols], ACT.Copy).then_inc(ah_ready, 1)

            def columns(b, cols):
                with act.If(value_of(act, fresh, b + 1, 1) > 0):
                    run = value_of(act, runs, b + 1, NB)
                    for i in range(KI):
                        hidden(b, i, cols)
                        if i < KI - 1:
                            high(i, run * 32 + 16 * (i // NST) + 16)
                    for k in range(2):
                        x_high(k, b * KH + KH)
                    high(KI - 1, run * 32 + 16 * ((KI - 1) // NST) + 16)
                with act.Else():
                    for i in range(KI):
                        hidden(b, i, cols)
                    act.sem_inc(split_hi, KI)
                    for k in range(2):
                        x_high(k, b * KH + KH)
                act.sem_inc(act_passed, 1)

            with act.Fori(0, NB) as b:
                with act.If(value_of(act, tiles, b, J) > 0):
                    act.wait_ge(down_ready, b * KH + KH)
                    with act.If(value_of(act, fresh, b, 1) > 0):
                        run = value_of(act, runs, b, NB)
                        for q in (4, 5):
                            high(q, run * 32 + 32)
                    with act.Else():
                        act.sem_inc(split_hi, 2)
                    with act.If(value_of(act, tiles, b, J) > 2):
                        columns(b, C)
                    with act.Else():
                        columns(b, C // 2)
                    for k in range(2, KH):
                        x_high(k, b * KH + KH)
                with act.Else():
                    act.sem_inc(act_passed, 1)

        @block.vector
        def _(dve):
            v = nc.vector
            dve.sem_inc(up_read, 1)
            dve.sem_inc(split, NST)
            dve.sem_inc(down_read, 2)
            dve.sem_inc(a_ready, 1)

            def low(q, s):
                dve.wait_ge(split_hi, s)
                v.tensor_tensor(w_lo[q][:], stage[q % NST][:], w_hi[q][:], ALU.subtract).then_inc(split, 1)

            def x_low(k, n):
                dve.wait_ge(xh_ready, n + k + 1)
                v.tensor_tensor(x_lo[:, k], tp[k % 2][:].rearrange("p j c -> p (j c)"), x_hi[:, k], ALU.subtract)\
                    .then_inc(xT_ready, 1)

            for q in range(4):
                low(q, q + 1)
            for k in range(KH):
                x_low(k, 0)

            def hidden(b, i, cols):
                dve.wait_ge(gate_read, b * KI + i + 3)
                dve.wait_ge(a_ready, b * KI + i + 1)
                v.tensor_tensor(av[:, 0:cols], pu[i % 2][:, 0:cols], sg[:, 0:cols], ALU.mult).then_inc(up_read, 1)
                dve.wait_ge(ah_ready, b * KI + i + 1)
                v.tensor_tensor(a_lo[:, i, 0:cols], av[:, 0:cols], a_hi[:, i, 0:cols], ALU.subtract)\
                    .then_inc(a_ready, 1)

            def columns(b, cols):
                with dve.If(value_of(dve, fresh, b + 1, 1) > 0):
                    for i in range(KI):
                        hidden(b, i, cols)
                        if i:
                            low(i - 1, b * NCH + NCH + i)
                    for k in range(2):
                        x_low(k, b * KH + KH)
                    low(KI - 1, b * NCH + NCH + KI)
                with dve.Else():
                    for i in range(KI):
                        hidden(b, i, cols)
                    dve.sem_inc(split, KI)
                    for k in range(2):
                        x_low(k, b * KH + KH)
                dve.sem_inc(dve_passed, 1)

            def scaled(b, count):
                done = 2
                for k in range(2 * count):
                    j, h = k // 2, k % 2
                    for _ in range(2 if count == 2 and k > 1 else 1):
                        if done < KH:
                            x_low(done, b * KH + KH)
                            done += 1
                    dve.wait_ge(down_ready, b * KH + KH + k + 1)
                    if h == 0:
                        dve.wait_ge(y_free, b * J + j + 1)
                    v.tensor_scalar(y[:, j % 2, h * 512:(h + 1) * 512], pd[k % 2][:],
                                    idx_cur[:, j, 1:2].bitcast(F32), None, ALU.mult).then_inc(down_read, 1)
                for k in range(done, KH):
                    x_low(k, b * KH + KH)
                if count < J:
                    dve.wait_ge(down_read, b * KH + 2 * count + 2)
                    wait_apart(dve, dve_passed, down_ready, b * KH + 2 * KH)
                    dve.sem_inc(down_read, KH - 2 * count)

            with dve.Fori(0, NB) as b:
                with dve.If(value_of(dve, tiles, b, J) > 0):
                    dve.wait_ge(idx_moved, b + 1)
                    dve.wait_ge(y_free, b * J + 2)
                    v.tensor_copy(idx_cur[:], idx_next[:]).then_inc(idx_copied, 1)
                    wait_apart(dve, dve_passed, idx_copied, b + 1)
                    with dve.If(value_of(dve, fresh, b, 1) > 0):
                        for q in (4, 5):
                            low(q, b * NCH + q + 1)
                    with dve.Else():
                        dve.sem_inc(split, 2)
                    with dve.If(value_of(dve, tiles, b, J) > 2):
                        columns(b, C)
                    with dve.Else():
                        columns(b, C // 2)
                    by_tiles(dve, dve_passed, value_of(dve, tiles, b, J), lambda count: scaled(b, count))
                with dve.Else():
                    dve.sem_inc(dve_passed, 1)

        @block.tensor
        def _(pe):
            m = nc.tensor.matmul
            pe.sem_inc(down_ready, KH)
            pe.wait_ge(made, 2)

            def transposes(k, n):
                pe.wait_ge(xT_ready, n + k - 1) if not (isinstance(n, int) and n + k < 2) else None
                for j in range(J):
                    last = nc.tensor.transpose(tp[k % 2][:, j], xraw[:, j, k * P:(k + 1) * P], ident[:])
                last.then_inc(tp_ready, 1)

            def product(dst, w, cols, x, xs, first, last):
                hi, lo = w
                m(dst, hi[:, cols], x[0][xs], start=first, stop=False)
                m(dst, hi[:, cols], x[1][xs], start=False, stop=False)
                return m(dst, lo[:, cols], x[0][xs], start=False, stop=last)

            pe.wait_ge(gathered, 16 * J)
            for k in range(KH):
                transposes(k, 0)
            def block_of(b, count):
                cols = max(count, 2) * P
                groups = 2 * count
                pe.wait_ge(xT_ready, b * KH + KH)
                for i in range(KI):
                    pe.wait_ge(split, b * NCH + i + 1 + NST)
                    pe.wait_ge(gate_read, b * KI + i + 1)
                    if i:
                        pe.wait_ge(up_read, b * KI + i)
                    for half, dst in ((0, pg[i % 2]), (1, pu[i % 2])):
                        for k in range(KH):
                            c0 = half * 1024 + k * P
                            last = product(dst[:, 0:cols], (w_hi[i], w_lo[i]), slice(c0, c0 + P), (x_hi, x_lo),
                                           (slice(None), k, slice(0, cols)), k == 0, k == KH - 1)
                    last.then_inc(gu_ready, 1)

                def down(k, ks):
                    j, h = k // 2, k % 2
                    for i in ks:
                        for part, (wa, wb) in enumerate(((a_hi, w_hi), (a_hi, w_lo), (a_lo, w_hi))):
                            last = m(pd[k % 2][:], wa[:, i, j * P:(j + 1) * P], wb[4 + h][:, i * 512:(i + 1) * 512],
                                     start=i == 0 and part == 0, stop=i == KI - 1 and part == 2)
                    return last

                pe.wait_ge(gathered, value_of(pe, before_t, b + 2, NB * J) * 16)
                pe.wait_ge(split, b * NCH + NCH + NST)
                transposes(0, b * KH + KH)
                transposes(1, b * KH + KH)
                pe.wait_ge(down_read, b * KH + 1)
                pe.wait_ge(a_ready, b * KI + KI)
                down(0, range(KI - 1))
                pe.wait_ge(down_read, b * KH + 2)
                down(1, range(KI - 1))
                pe.wait_ge(a_ready, b * KI + KI + 1)
                transposes(2, b * KH + KH)
                down(0, (KI - 1,)).then_inc(down_ready, 1)
                transposes(3, b * KH + KH)
                down(1, (KI - 1,)).then_inc(down_ready, 1)
                made = 4
                for k in range(2, groups):
                    pe.wait_ge(down_read, b * KH + k + 1)
                    for part in ((range(2), range(2, KI)) if count == 2 else (range(KI),)):
                        if made < KH:
                            transposes(made, b * KH + KH)
                            made += 1
                        last = down(k, part)
                    last.then_inc(down_ready, 1)
                for k in range(made, KH):
                    transposes(k, b * KH + KH)
                if count < J:
                    pe.wait_ge(down_ready, b * KH + KH + groups)
                    pe.sem_inc(down_ready, KH - groups)

            with pe.Fori(0, NB) as b:
                by_tiles(pe, pe_passed, value_of(pe, tiles, b, J), lambda count: block_of(b, count),
                         lambda: pe.sem_inc(pe_passed, 1))


def build(nc, A, T, B):
    rows = (E + SH) * T + C
    NB = SH * T // C + T * K // C + E - 1
    xn_d = nc.dram_tensor("xn_rows", [T + P, H], F32, kind="Internal").ap()
    base_d = nc.dram_tensor("base_rows", [T, H], F32, kind="Internal").ap()
    table = nc.dram_tensor("slot_table", [rows, 2], I32, kind="Internal").ap()
    with ExitStack() as ctx:
        def sb(name, shape, dt):
            return ctx.enter_context(nc.sbuf_tensor(name, shape, dt))

        slots = sb("slots", [P, T // P * K], U32)
        payload = sb("payload", [P, T // P * K, 2], I32)
        plan = [sb("starts", [1, NB + 2], I32)]
        plan += [sb(name, [1, NB + 1], I32) for name in ("experts", "fresh", "runs", "tiles")]
        plan.append(sb("before_t", [1, NB + 2], I32))
        cnt_base = sb("cnt_base", [P, E], F32)
        with ExitStack() as part:
            zT = part.enter_context(nc.sbuf_tensor("zT", [P, (T // C + 3) * (C + 2)], F32))
            route_stage(nc, T, B, (A["x"], xn_d, base_d, A["out"], table, A["rw"], A["ipw"], A["lnw"], A["lnb"],
                                   A["rbias"], zT, cnt_base, slots, payload))
            scan_stage(nc, T, B, (base_d, A["out"], zT, A["convw"], A["convb"], A["xpT"], A["xpB"], A["xpC"],
                                  A["dtT"], A["dtb"], A["alog"], A["dpar"], A["opT"]))
        ahead = {"stage": [sb(f"stage{i}", [P, WC], F32) for i in range(NST)], "xraw": sb("xraw", [P, J, H], F32),
                 "idx_in": sb("idx_in", [P, J, 2], I32), "idx_next": sb("idx_next", [P, J, 2], I32),
                 "staged": [ctx.enter_context(nc.semaphore(f"staged{i}")) for i in range(NST)]}
        for name in ("idx_loaded", "idx_moved", "gathered"):
            ahead[name] = ctx.enter_context(nc.semaphore(name))
        plan_stage(nc, T, cnt_base, plan, ahead, xn_d, table, A["w_all"])
        expert_stage(nc, T, (xn_d, A["out"], table, A["w_all"], slots, payload), plan, ahead)


def layouts(x, ln_w, ln_b, in_proj_W, conv_w, conv_b, x_proj_W, dt_proj_W, dt_proj_b, A_log, D_param, out_proj_W,
            router_w, router_bias, w_gate, w_up, w_down, sw_gate, sw_up, sw_down):
    import numpy as np

    def halves(w):
        return w.reshape(H, SH, I).transpose(1, 0, 2)

    gate = np.concatenate([w_gate, halves(sw_gate)])
    up = np.concatenate([w_up, halves(sw_up)])
    down = np.concatenate([w_down, sw_down.reshape(SH, I, H)])
    n = E + SH
    gu = np.stack([gate, up]).reshape(2, n, KH, P, KI, P).transpose(1, 4, 3, 0, 2, 5).reshape(n, KI, P, WC)
    dn = down.reshape(n, KI, P, 2, 512).transpose(0, 3, 2, 1, 4).reshape(n, 2, P, WC)
    T = x.shape[0] * x.shape[1]
    return {
        "x": x.reshape(T, H), "rw": router_w, "ipw": in_proj_W.T, "lnw": ln_w.reshape(KH, P).T,
        "lnb": ln_b.reshape(KH, P).T, "rbias": router_bias, "convw": conv_w.reshape(D, 3),
        "convb": conv_b.reshape(D, 1), "xpT": x_proj_W[:R].T, "xpB": np.tile(x_proj_W[R:R + N].T, (1, PG)),
        "xpC": np.tile(x_proj_W[R + N:].T, (1, PG)), "dtT": dt_proj_W.T, "dtb": dt_proj_b.reshape(D, 1),
        "alog": A_log.reshape(NG, P).T, "dpar": D_param.reshape(D, 1), "opT": out_proj_W.T,
        "w_all": np.concatenate([gu, dn], axis=1).reshape(n * NCH, P, WC),
    }


def kernel(**inputs):
    import numpy as np
    import concourse.bacc as bacc
    from concourse import mybir as _mybir
    from concourse.bass_utils import run_bass_kernel_spmd

    names = {k.replace("L0_attn_feat_patch", "x").replace("L0_attn_", "").replace("L0_ffn_", ""): np.asarray(v)
             for k, v in inputs.items()}
    arrays = {k: np.ascontiguousarray(v) for k, v in layouts(**names).items()}
    B, L = names["x"].shape[:2]
    T = B * L
    nc = bacc.Bacc("TRN2", target_bir_lowering=False, num_devices=1)
    A = {k: nc.dram_tensor(f"in_{k}", v.shape, _mybir.dt.from_np(v.dtype), kind="ExternalInput").ap()
         for k, v in arrays.items()}
    A["out"] = nc.dram_tensor("out_rows", [T + P, H], F32, kind="ExternalOutput").ap()
    build(nc, A, T, B)
    r = run_bass_kernel_spmd(nc, [{f"in_{k}": v for k, v in arrays.items()}], core_ids=[0])
    return r.results[0]["out_rows"][:T].reshape(B, L, H)
```
